# Optimizing a Trainium2 kernel written in Bass

```python
import numpy as np
import jax
import jax.numpy as jnp

def _softmax(x, axis=-1):
    return jax.nn.softmax(x, axis=axis)

def _gelu(x):
    return jax.nn.gelu(x, approximate=True)

def _silu(x):
    return jax.nn.silu(x)

def _sigmoid(x):
    return jax.nn.sigmoid(x)

def _layernorm(x, axis=-1, eps=1e-05):
    m = jnp.mean(x, axis=axis, keepdims=True)
    v = jnp.var(x, axis=axis, keepdims=True)
    return (x - m) / jnp.sqrt(v + eps)

def _scatter_add(tgt, idx, src, axis=0):
    return tgt.at[idx].add(src)

def _segment_sum(src, seg, n):
    return jax.ops.segment_sum(src, seg, n)
kernel_name = 'mk_adj_ffn_d1_adj_r2_0c1cb7'

def setup_inputs(seed: int=0):
    np.random.seed(seed)
    _w = jnp.asarray

    def _rec_inputs():
        import jax
        import jax.numpy as jnp
        _gk = jax.random.key(seed)
        x = -0.0005207 + 1.001 * jax.random.normal(jax.random.fold_in(_gk, 1), (8192, 128), jnp.float32)
        _w = (1.0 + jnp.arange(8192, dtype=jnp.float32)) ** (-0.5)
        _w = _w / _w.mean()
        _pij = jnp.clip(0.000976562 * _w[:, None] * _w[None, :], 0.0, 1.0)
        _a = jax.random.uniform(jax.random.fold_in(_gk, 2), (8192, 8192)) < _pij
        _a = jnp.logical_or(_a, jnp.eye(8192, dtype=bool))
        _af = _a.astype(jnp.float32)
        _af = _af * jax.random.uniform(jax.random.fold_in(_gk, 3), (8192, 8192), jnp.float32, 0.05, 1)
        adj = _af
        return (x, adj)
    x, adj = _rec_inputs()

    def _L0_gnn_setup():
        import jax, jax.numpy as jnp
        import numpy as np
        N = 4096
        D_IN = 128
        D_OUT = 128
        key = jax.random.key(seed)
        k1, k2, k3 = jax.random.split(key, 3)
        x = jax.random.normal(k1, (N, D_IN), dtype=jnp.float32)
        adj = jax.random.uniform(k2, (N, N), dtype=jnp.float32)
        W = jax.random.normal(k3, (D_OUT, D_IN), dtype=jnp.float32) * (1.0 / np.sqrt(D_IN))
        return {'x': x, 'adj': adj, 'W': W}
    _L0_gnn_all = _L0_gnn_setup()
    _L0_gnn_in = {k: v for k, v in _L0_gnn_all.items() if k in ('W',)}
    del _L0_gnn_all

    def _L0_ffn_setup():
        import jax, jax.numpy as jnp
        import numpy as np
        H, P, G, NS, K = (8, 64, 64, 64, 3)
        D_INNER = H * P
        CONV_DIM = D_INNER + 2 * NS
        D_IN_PROJ = 2 * D_INNER + 2 * NS + 2 * H

        def _hydra(u, in_w, conv_w, conv_b, dt_bias, A_log, Dp, fcD_w, norm_w, out_w):
            Bt, L, _ = u.shape
            zxbcdt = u @ in_w.T
            z = zxbcdt[..., :D_INNER]
            xBC = zxbcdt[..., D_INNER:D_INNER + CONV_DIM]
            dt = zxbcdt[..., -2 * H:]
            dt = jnp.concatenate([dt[..., :H], jnp.flip(dt[..., H:], axis=1)], axis=0)
            dt = jax.nn.softplus(dt + dt_bias)
            xp = jnp.pad(xBC, ((0, 0), (K - 1, 0), (0, 0)))
            xBC = sum((xp[:, k:k + L, :] * conv_w[:, k] for k in range(K))) + conv_b
            xBC = jax.nn.silu(xBC)
            x = xBC[..., :D_INNER]
            Bm = xBC[..., D_INNER:D_INNER + NS]
            Cm = xBC[..., D_INNER + NS:]
            x_og = x
            x2 = jnp.concatenate([x, jnp.flip(x, 1)], 0).reshape(2 * Bt, L, H, P)
            B2 = jnp.concatenate([Bm, jnp.flip(Bm, 1)], 0)
            C2 = jnp.concatenate([Cm, jnp.flip(Cm, 1)], 0)
            dA = jnp.exp(dt * -jnp.exp(A_log))
            dBx = jnp.einsum('blh,bln,blhp->blhpn', dt, B2, x2)

            def step(h, inp):
                dA_t, dBx_t, C_t = inp
                h = h * dA_t[:, :, None, None] + dBx_t
                return (h, jnp.einsum('bhpn,bn->bhp', h, C_t))
            h0 = jnp.zeros((2 * Bt, H, P, NS), u.dtype)
            _, ys = jax.lax.scan(step, h0, (dA.transpose(1, 0, 2), dBx.transpose(1, 0, 2, 3, 4), C2.transpose(1, 0, 2)))
            y = ys.transpose(1, 0, 2, 3).reshape(2 * Bt, L, D_INNER)
            y_fw, y_bw = (y[:Bt], jnp.flip(y[Bt:], 1))
            y = jnp.pad(y_fw[:, :-1], ((0, 0), (1, 0), (0, 0))) + jnp.pad(y_bw[:, 1:], ((0, 0), (0, 1), (0, 0)))
            y = y + x_og * jnp.repeat(x_og @ fcD_w.T + Dp, P, axis=-1)
            yg = y * jax.nn.silu(z)
            yg = yg * jax.lax.rsqrt(jnp.mean(jnp.square(yg), -1, keepdims=True) + 1e-05) * norm_w
            return yg @ out_w.T
        key = jax.random.key(seed)
        ks = jax.random.split(key, 10)
        dim, Bsz, N = (128, 4, 4096)
        s = 0.02
        return {'x': jax.random.normal(ks[0], (Bsz, N, dim), jnp.float32), 'W_fx': jax.random.normal(ks[1], (D_INNER, dim), jnp.float32) * s, 'b_fx': jnp.zeros((D_INNER,), jnp.float32), 'W_x': jax.random.normal(ks[2], (D_INNER, dim), jnp.float32) * s, 'b_x': jnp.zeros((D_INNER,), jnp.float32), 'W_slice': jax.random.normal(ks[3], (G, P), jnp.float32) * s, 'b_slice': jnp.zeros((G,), jnp.float32), 'temperature': jnp.full((1, H, 1, 1), 0.5, jnp.float32), 'hy_in_w': jax.random.normal(ks[4], (D_IN_PROJ, D_INNER), jnp.float32) * s, 'hy_conv_w': jax.random.normal(ks[5], (CONV_DIM, K), jnp.float32) * s, 'hy_conv_b': jnp.zeros((CONV_DIM,), jnp.float32), 'hy_dt_bias': jnp.log(jnp.expm1(jnp.full((H,), 0.01, jnp.float32))), 'hy_A_log': jnp.log(jnp.linspace(1.0, 16.0, H)).astype(jnp.float32), 'hy_D': jnp.ones((H,), jnp.float32), 'hy_fcD_w': jax.random.normal(ks[6], (H, D_INNER), jnp.float32) * s, 'hy_norm_w': jnp.ones((D_INNER,), jnp.float32), 'hy_out_w': jax.random.normal(ks[7], (D_INNER, D_INNER), jnp.float32) * s, 'out_w': jax.random.normal(ks[8], (dim, D_INNER), jnp.float32) * s, 'out_b': jnp.zeros((dim,), jnp.float32)}
    _L0_ffn_all = _L0_ffn_setup()
    _L0_ffn_in = {k: v for k, v in _L0_ffn_all.items() if k in ('W_fx', 'b_fx', 'W_x', 'b_x', 'W_slice', 'b_slice', 'temperature', 'hy_in_w', 'hy_conv_w', 'hy_conv_b', 'hy_dt_bias', 'hy_A_log', 'hy_D', 'hy_fcD_w', 'hy_norm_w', 'hy_out_w', 'out_w', 'out_b')}
    del _L0_ffn_all
    return {'x': x, 'adj': adj, 'L0_gnn_W': _L0_gnn_in['W'], 'L0_ffn_W_fx': _L0_ffn_in['W_fx'], 'L0_ffn_b_fx': _L0_ffn_in['b_fx'], 'L0_ffn_W_x': _L0_ffn_in['W_x'], 'L0_ffn_b_x': _L0_ffn_in['b_x'], 'L0_ffn_W_slice': _L0_ffn_in['W_slice'], 'L0_ffn_b_slice': _L0_ffn_in['b_slice'], 'L0_ffn_temperature': _L0_ffn_in['temperature'], 'L0_ffn_hy_in_w': _L0_ffn_in['hy_in_w'], 'L0_ffn_hy_conv_w': _L0_ffn_in['hy_conv_w'], 'L0_ffn_hy_conv_b': _L0_ffn_in['hy_conv_b'], 'L0_ffn_hy_dt_bias': _L0_ffn_in['hy_dt_bias'], 'L0_ffn_hy_A_log': _L0_ffn_in['hy_A_log'], 'L0_ffn_hy_D': _L0_ffn_in['hy_D'], 'L0_ffn_hy_fcD_w': _L0_ffn_in['hy_fcD_w'], 'L0_ffn_hy_norm_w': _L0_ffn_in['hy_norm_w'], 'L0_ffn_hy_out_w': _L0_ffn_in['hy_out_w'], 'L0_ffn_out_w': _L0_ffn_in['out_w'], 'L0_ffn_out_b': _L0_ffn_in['out_b']}

def reference(x, adj, L0_gnn_W, L0_ffn_W_fx, L0_ffn_b_fx, L0_ffn_W_x, L0_ffn_b_x, L0_ffn_W_slice, L0_ffn_b_slice, L0_ffn_temperature, L0_ffn_hy_in_w, L0_ffn_hy_conv_w, L0_ffn_hy_conv_b, L0_ffn_hy_dt_bias, L0_ffn_hy_A_log, L0_ffn_hy_D, L0_ffn_hy_fcD_w, L0_ffn_hy_norm_w, L0_ffn_hy_out_w, L0_ffn_out_w, L0_ffn_out_b):
    import jax
    import jax.numpy as jnp

    def _L0_gnn_ref(x, adj, W):
        import jax, jax.numpy as jnp
        import numpy as np
        N = 4096
        D_IN = 128
        D_OUT = 128
        A_hat = adj + jnp.eye(adj.shape[0], dtype=adj.dtype)
        d_inv_sqrt = jnp.sum(A_hat, axis=1) ** (-0.5)
        A_norm = d_inv_sqrt[:, None] * A_hat * d_inv_sqrt[None, :]
        support = x @ W.T
        out = A_norm @ support
        return jax.nn.relu(out)

    def _L0_ffn_ref(x, W_fx, b_fx, W_x, b_x, W_slice, b_slice, temperature, hy_in_w, hy_conv_w, hy_conv_b, hy_dt_bias, hy_A_log, hy_D, hy_fcD_w, hy_norm_w, hy_out_w, out_w, out_b):
        import jax, jax.numpy as jnp
        import numpy as np
        H, P, G, NS, K = (8, 64, 64, 64, 3)
        D_INNER = H * P
        CONV_DIM = D_INNER + 2 * NS
        D_IN_PROJ = 2 * D_INNER + 2 * NS + 2 * H

        def _hydra(u, in_w, conv_w, conv_b, dt_bias, A_log, Dp, fcD_w, norm_w, out_w):
            Bt, L, _ = u.shape
            zxbcdt = u @ in_w.T
            z = zxbcdt[..., :D_INNER]
            xBC = zxbcdt[..., D_INNER:D_INNER + CONV_DIM]
            dt = zxbcdt[..., -2 * H:]
            dt = jnp.concatenate([dt[..., :H], jnp.flip(dt[..., H:], axis=1)], axis=0)
            dt = jax.nn.softplus(dt + dt_bias)
            xp = jnp.pad(xBC, ((0, 0), (K - 1, 0), (0, 0)))
            xBC = sum((xp[:, k:k + L, :] * conv_w[:, k] for k in range(K))) + conv_b
            xBC = jax.nn.silu(xBC)
            x = xBC[..., :D_INNER]
            Bm = xBC[..., D_INNER:D_INNER + NS]
            Cm = xBC[..., D_INNER + NS:]
            x_og = x
            x2 = jnp.concatenate([x, jnp.flip(x, 1)], 0).reshape(2 * Bt, L, H, P)
            B2 = jnp.concatenate([Bm, jnp.flip(Bm, 1)], 0)
            C2 = jnp.concatenate([Cm, jnp.flip(Cm, 1)], 0)
            dA = jnp.exp(dt * -jnp.exp(A_log))
            dBx = jnp.einsum('blh,bln,blhp->blhpn', dt, B2, x2)

            def step(h, inp):
                dA_t, dBx_t, C_t = inp
                h = h * dA_t[:, :, None, None] + dBx_t
                return (h, jnp.einsum('bhpn,bn->bhp', h, C_t))
            h0 = jnp.zeros((2 * Bt, H, P, NS), u.dtype)
            _, ys = jax.lax.scan(step, h0, (dA.transpose(1, 0, 2), dBx.transpose(1, 0, 2, 3, 4), C2.transpose(1, 0, 2)))
            y = ys.transpose(1, 0, 2, 3).reshape(2 * Bt, L, D_INNER)
            y_fw, y_bw = (y[:Bt], jnp.flip(y[Bt:], 1))
            y = jnp.pad(y_fw[:, :-1], ((0, 0), (1, 0), (0, 0))) + jnp.pad(y_bw[:, 1:], ((0, 0), (0, 1), (0, 0)))
            y = y + x_og * jnp.repeat(x_og @ fcD_w.T + Dp, P, axis=-1)
            yg = y * jax.nn.silu(z)
            yg = yg * jax.lax.rsqrt(jnp.mean(jnp.square(yg), -1, keepdims=True) + 1e-05) * norm_w
            return yg @ out_w.T
        B, N, _ = x.shape
        fx = (x @ W_fx.T + b_fx).reshape(B, N, H, P).transpose(0, 2, 1, 3)
        xm = (x @ W_x.T + b_x).reshape(B, N, H, P).transpose(0, 2, 1, 3)
        temp = jnp.maximum(temperature, 1e-06)
        sw = jax.nn.softmax((xm @ W_slice.T + b_slice) / temp, axis=-1)
        snorm = sw.sum(2)
        st = jnp.einsum('bhnc,bhng->bhgc', fx, sw) / (snorm + 1e-05)[..., None]
        st = st.transpose(0, 2, 1, 3).reshape(B, G, D_INNER)
        ot = _hydra(st, hy_in_w, hy_conv_w, hy_conv_b, hy_dt_bias, hy_A_log, hy_D, hy_fcD_w, hy_norm_w, hy_out_w)
        ot = ot.reshape(B, G, H, P).transpose(0, 2, 1, 3)
        out = jnp.einsum('bhgc,bhng->bhnc', ot, sw).transpose(0, 2, 1, 3).reshape(B, N, D_INNER)
        return out @ out_w.T + out_b
    x = x + _L0_gnn_ref(_layernorm(x, axis=-1), adj, L0_gnn_W)
    x = x + _L0_ffn_ref(_layernorm(x, axis=-1)[None], L0_ffn_W_fx, L0_ffn_b_fx, L0_ffn_W_x, L0_ffn_b_x, L0_ffn_W_slice, L0_ffn_b_slice, L0_ffn_temperature, L0_ffn_hy_in_w, L0_ffn_hy_conv_w, L0_ffn_hy_conv_b, L0_ffn_hy_dt_bias, L0_ffn_hy_A_log, L0_ffn_hy_D, L0_ffn_hy_fcD_w, L0_ffn_hy_norm_w, L0_ffn_hy_out_w, L0_ffn_out_w, L0_ffn_out_b)[0]
    return x

_drawn_inputs = setup_inputs


def setup_inputs(seed=0):
    import zlib

    import numpy as np

    out = dict(_drawn_inputs(seed))
    spreads = {'L0_ffn_b_fx': (0.0, 0.1),
     'L0_ffn_b_x': (0.0, 0.8),
     'L0_ffn_b_slice': (0.0, 0.8),
     'L0_ffn_temperature': (0.5, 0.6),
     'L0_ffn_hy_conv_b': (0.0, 0.1),
     'L0_ffn_hy_dt_bias': (-4.600166320800781, 0.6),
     'L0_ffn_hy_D': (1.0, 0.6),
     'L0_ffn_hy_norm_w': (1.0, 0.6),
     'L0_ffn_out_b': (0.0, 0.1)}
    factors = {'L0_ffn_W_fx': 8.0,
     'L0_ffn_W_x': 8.0,
     'L0_ffn_W_slice': 8.0,
     'L0_ffn_hy_conv_w': 8.0,
     'L0_ffn_hy_A_log': 64.0,
     'L0_ffn_hy_fcD_w': 24.865}
    for name, (base, spread) in spreads.items():
        noise = np.random.default_rng([zlib.crc32(name.encode()), seed]).standard_normal(out[name].shape)
        drawn = base * np.exp(spread * noise) if base else spread * noise
        out[name] = jnp.asarray(drawn.astype(out[name].dtype))
    for name, factor in factors.items():
        out[name] = (out[name] * factor).astype(out[name].dtype)
    return out
```

```python
from collections import namedtuple
from contextlib import ExitStack, contextmanager

import concourse.bass as bass
from concourse import mybir

ALU = mybir.AluOpType
ACT = mybir.ActivationFunctionType
AX = mybir.AxisListType
F32 = mybir.dt.float32
F32R = mybir.dt.float32r

P = 128
D = 128
CH = 512
T4 = CH // P
RING = 4
H = 8
HD = 64
G = 64
HG = H * G
INNER = H * HD
NS = 64
CONV = INNER + 2 * NS
KW = 3
PROJ = 2 * INNER + 2 * NS + 2 * H
LN_EPS = 1e-5
EXP_MAX = 88.0
DECAY_MIN = -1.0e4

Chunk = namedtuple("Chunk", "n m J first")
Seg = namedtuple("Seg", "rounds chunks")


class Steps:

    def __init__(self, sem, names):
        self.sem, self.names = sem, names.split()

    def value(self, name, rnd=0):
        return rnd * len(self.names) + self.names.index(name) + 1


def wait_step(eng, steps, name, rnd=0):
    eng.wait_ge(steps.sem, steps.value(name, rnd))


@contextmanager
def rounds(eng, count):
    if count == 1:
        yield 0
    else:
        with eng.Fori(0, count) as g:
            yield g


def plan_first_reading(blocks):
    plan, n, m = [], 0, 0
    for K in range(blocks):
        a, b = divmod(K, RING)
        sums, both = [], []
        straight = [Chunk(n + i, None, RING * a + b + 1 + i, False) for i in range(RING - 1 - b)]
        n += len(straight)
        if straight:
            sums.append(Seg(1, straight))
        loops = blocks // RING - 1 - a
        if loops:
            sums.append(Seg(loops, [Chunk(n + i, None, RING * (a + 1) + i, False) for i in range(RING)]))
            n += RING * loops
        if a:
            both.append(Seg(a, [Chunk(n + i, m + i, i, False) for i in range(RING)]))
            n += RING * a
            m += RING * a
        both.append(Seg(1, [Chunk(n + i, m + i, RING * a + i, a == 0 and i == 0) for i in range(b + 1)]))
        n += b + 1
        m += b + 1
        plan.append((sums, both))
    return plan, n, m


def plan_second_reading(blocks, n, m):
    plan = []
    for I in reversed(range(blocks - 1)):
        a, b = divmod(I, RING)
        segs = []
        straight = RING - 1 - b
        if straight:
            segs.append(Seg(1, [Chunk(n + i, m + i, I + 1 + i, i == 0) for i in range(straight)]))
            n, m = n + straight, m + straight
        loops = blocks // RING - 1 - a
        parts = [loops] if I or loops < 2 else [loops - 1, 1]
        done = 0
        for k in parts:
            if k:
                segs.append(Seg(k, [Chunk(n + i, m + i, RING * (a + 1 + done) + i, False) for i in range(RING)]))
                n, m, done = n + RING * k, m + RING * k, done + k
        plan.append((I, segs))
    return plan, n, m


def gnn_slice_ffn(nc, x, adj, gnn_W, W_fx, b_fx, W_x, b_x, W_slice, b_slice, temperature, in_w, conv_w,
                  conv_b, dt_bias, A_log, Dp, fcD_w, norm_w, hy_out_w, out_w, out_b, out):
    N = x.shape[0]
    BL = N // CH
    TILES = N // P
    first_plan, n1, m1 = plan_first_reading(BL)
    second_plan, n2, m2 = plan_second_reading(BL, n1, m1)
    assert n1 == BL * BL and n1 % RING == 0 and n2 % RING == 0 and m2 % 2 == 0
    SLICE_LAST = TILES + 4
    M0 = m1
    N0 = n1

    def sliced(m_base):
        i = m_base - M0
        k = i // 2
        return k if i % 2 == 1 and k <= TILES - 7 else None

    with ExitStack() as ctx:
        def sb(name, shape, dt=F32):
            return ctx.enter_context(nc.sbuf_tensor(name, shape, dt))

        def psum(name, shape):
            return ctx.enter_context(nc.psum_tensor(name, shape, F32))

        def sem(name):
            return ctx.enter_context(nc.semaphore(name))

        turned = [psum(f"turned{i}", [P, 2 * CH]) for i in range(2)]
        acc = psum("acc", [P, CH])
        bank_a = psum("bank_a", [P, CH])
        bank_b = psum("bank_b", [P, CH])
        bank_c = psum("bank_c", [P, CH])

        a_ring = sb("a_ring", [P, RING, T4, CH])
        hi = sb("hi", [P, 4, 2 * CH], F32R)
        lo = sb("lo", [P, 4, 2 * CH], F32R)
        sup = sb("sup", [P, TILES, D])
        rows = sb("rows", [P, BL, CH])
        x1 = rows[:, :, :].rearrange("p b (t d) -> p (b t) d", d=D)
        s_hi = sb("s_hi", [P, 2, CH], F32R)
        s_lo = sb("s_lo", [P, 2, CH], F32R)
        m_hi = sb("m_hi", [P, CH], F32R)
        m_lo = sb("m_lo", [P, CH], F32R)
        x_in = sb("x_in", [P, 2, T4, D])
        lnx = sb("lnx", [P, T4, D])
        lnxT = sb("lnxT", [P, CH])
        logit = sb("logit", [P, 2, HG])
        expd = sb("expd", [P, 2, HG])
        sw = sb("sw", [P, 2, HG])
        w_raw = sw
        in_wT = sb("in_wT", [P, INNER // P, PROJ])
        hy_outT = sb("hy_outT", [P, INNER // P, INNER])
        W_fxT = sb("W_fxT", [P, INNER])
        out_wT = sb("out_wT", [P, INNER // P, D])
        fcD_T = sb("fcD_T", [P, INNER // P, H])
        gnn_WT = sb("gnn_WT", [P, D])
        W_logT = sb("W_logT", [P, HG])
        b_log = sb("b_log", [P, HG])
        ident = sb("ident", [P, P])
        ones = sb("ones", [P, 1])
        row_st = lnxT
        nat = lnx
        part = sb("part", [P, T4, BL])
        rsum = sb("rsum", [P, T4])
        rsq = sb("rsq", [P, T4])
        dcol = sb("dcol", [P, TILES])
        bn = sb("bn", [P, T4, 6])
        mv = sb("mv", [P, T4, 2])
        sd = sb("sd", [P, T4])
        rstd4 = sb("rstd4", [P, T4])
        stat = sb("stat", [P, 2, 6])
        both_st = sb("both_st", [P, 2])
        gap = sb("gap", [P, 1])
        within = sb("within", [P, 1])
        vareps = sb("vareps", [P, 2])
        mean = sb("mean", [P, TILES])
        rstd = sb("rstd", [P, TILES])
        half = sb("half", [P, 1])
        xns = sb("xns", [P, 6, D])
        xn_a, xn_b, xnT = xns[:, 0:2, :], xns[:, 2:4, :], xns[:, 4:6, :]
        junk = xns[:, 0:4, :].rearrange("p a d -> p (a d)").bitcast(mybir.dt.bfloat16)
        mx = sb("mx", [P, H])
        den = sb("den", [P, H])
        rden = sb("rden", [P, 2, H])
        sw_sum = sb("sw_sum", [P, HG])
        temp = sb("temp", [P, H])
        rtemp = sb("rtemp", [P, H])
        bsl = sb("bsl", [P, G])
        out_bc = sb("out_bc", [P, 1])

        sw_dram = nc.dram_tensor("sw_dram", [N, HG], F32, kind="Internal").ap()

        a_in = [sem(f"a_in{i}") for i in range(RING)]
        act_sum = sem("act_sum")
        dve_sum = sem("dve_sum")
        t_done = sem("t_done")
        hi_done = sem("hi_done")
        lo_done = sem("lo_done")
        sh_done = sem("sh_done")
        sl_done = sem("sl_done")
        mm_done = sem("mm_done")
        row_done = sem("row_done")
        ident_ok = sem("ident_ok")
        setup_in = sem("setup_in")
        tiny_in = sem("tiny_in")
        x_landed = [sem(f"x_landed{i}") for i in range(2)]
        w_landed = [sem(f"w_landed{i}") for i in range(2)]
        c_filled = sem("c_filled")
        c_copied = sem("c_copied")
        prep_v = Steps(sem("prep_v"), "stats aggr eps rstd norm")
        prep_a = Steps(sem("prep_a"), "sqrt")
        prep_t = Steps(sem("prep_t"), "support")
        deg_v = Steps(sem("deg_v"), "rows one inv scaled")
        deg_a = Steps(sem("deg_a"), "sqrt")
        fin_v = Steps(sem("fin_v"), "add relu x1")
        fin_t = Steps(sem("fin_t"), "turned")
        fin_sums = sem("fin_sums")
        st_done = Steps(sem("st_done"), "stats sum gap mean within half var")
        rstd_done = sem("rstd_done")
        xa_done = sem("xa_done")
        xt_done = sem("xt_done")
        xtc_done = sem("xtc_done")
        lg_done = sem("lg_done")
        sm_done = Steps(sem("sm_done"), "bias max shift")
        exp_done = sem("exp_done")
        rd_done = Steps(sem("rd_done"), "sum inv")
        xb_done = sem("xb_done")
        sw_done = Steps(sem("sw_done"), "weights total")
        sw_out = [sem(f"sw_out{i}") for i in range(2)]
        tt_done = sem("tt_done")

        set_v = Steps(sem("set_v"), "tmax tinv bx_wide wslT wlog blog_sum blog")
        set_t = Steps(sem("set_t"), "wslT wlog blog")

        conv_v = sem("conv_v")
        units = [("in", in_w[r * P:min((r + 1) * P, PROJ), :], min(P, PROJ - r * P),
                  in_wT[:, :, r * P:min((r + 1) * P, PROJ)]) for r in range(-(-PROJ // P))]
        units += [("ho", hy_out_w[r * P:(r + 1) * P, :], P, hy_outT[:, :, r * P:(r + 1) * P])
                  for r in range(INNER // P)]
        units += [("fx", W_fx.rearrange("(t p) d -> p t d", p=P), P, W_fxT[:, :].rearrange("p (t d) -> p t d", t=T4))]
        units += [("ow", out_w[:, :], P, out_wT[:, :, :])]
        units += [("fd", fcD_w[:, :], H, fcD_T[:, :, :])]
        PER = 2
        unit_block = {u: u // PER for u in range(len(units))}
        c_uses = ["g", ("x", 0)]
        for K in range(BL):
            if K + 1 < BL:
                c_uses.append(("x", K + 1))
            c_uses += [("w", u) for u in unit_block if unit_block[u] == K]

        def c_use(u):
            return c_uses.index(u)

        w_sl = lnx[0:G, 0, 0:HD]
        w_slT = lnx[0:HD, 2, 0:G]
        w_x_c = expd[0:HD, :, :].rearrange("c a (h d) -> c (a h) d", d=D)
        b_xT = sb("b_xT", [HD, H])
        b_x_wide = logit[0:HD, :, :].rearrange("c a (h d) -> c (a h) d", d=P)

        supf = sup[:, :, :].rearrange("p t d -> p (t d)")
        regions = [[ap, 0, size] for ap, size in (
            (supf, TILES * D), (logit[:, :, :].rearrange("p a g -> p (a g)"), 2 * HG),
            (expd[:, :, :].rearrange("p a g -> p (a g)"), 2 * HG))]

        def tmp(parts, *shape):
            size = 1
            for k in shape:
                size *= k
            region = next(r for r in regions if r[1] + size <= r[2])
            ap = region[0][0:parts, region[1]:region[1] + size]
            region[1] += size
            if len(shape) == 2:
                ap = ap.rearrange("p (a b) -> p a b", b=shape[1])
            return ap

        L = G
        KC = INNER // P
        TTs = tmp(P, HG)
        snorm = tmp(L, H)
        snorm_e = tmp(L, H)
        rsnorm = tmp(L, H)
        b_fx_w = sb("b_fx_w", [L, INNER])
        norm_ww = sb("norm_ww", [L, INNER])
        st_b = tmp(L, H, HD)
        st_s = st_b
        u_tok = tmp(L, INNER)
        uT = tmp(P, KC, L)
        z_tok = tmp(L, INNER)
        z_e = tmp(L, INNER)
        z_1 = z_r = z_e
        gate = tmp(L, INNER)
        CK = KC + 2
        cpad = tmp(P, CK, L + 2)
        cva = tmp(P, CK, L)
        cvb = tmp(P, CK, L)
        cvc = tmp(P, CK, L)
        cve = tmp(P, CK, L)
        cvr = cve
        xT = tmp(P, CK, L)
        conv_ws = sb("conv_ws", [P, CK, KW])
        conv_bs = sb("conv_bs", [P, CK])
        Cpad = tmp(NS, L + 2)
        x_tok = tmp(L, INNER)
        dtr = tmp(L, 2, H)
        dta = tmp(L, 2, H)
        dtb = tmp(L, 2, H)
        dtc = tmp(L, 2, H)
        dtd = tmp(L, 2, H)
        dtm = tmp(L, 2, H)
        dt = tmp(L, 2, H)
        dec = tmp(L, 2, H)
        decm = tmp(L, 2, H)
        dt_bw = sb("dt_bw", [L, H])
        a_lw = sb("a_lw", [L, H])
        a_cl = tmp(L, H)
        a_ex = tmp(L, H)
        Dw = sb("Dw", [L, H])
        seg_rhs = [tmp(L, H, L) for _ in range(2)]
        dec_e = [tmp(L, H, L) for _ in range(2)]
        cb = [tmp(L, L) for _ in range(2)]
        cbh = [tmp(L, H, L) for _ in range(2)]
        dmix = dec_e
        dsum = dec_e[0]
        fcd = tmp(L, H)
        xf = u_tok.rearrange("p (h c) -> p h c", h=H)
        y_s = z_tok
        yg = ygn = ygw = y_s
        ygs = sb("ygs", [L, 1])
        ygm = sb("ygm", [L, 1])
        ygq = sb("ygq", [L, 1])
        ygr = sb("ygr", [L, 1])
        ygT = tmp(P, KC, L)
        bd = lnxT[:, :].rearrange("p (k d) -> p k d", k=KC)
        less = sb("less", [L, L])
        more = sb("more", [L, L])
        MIX_V = Steps(sem("mix_v"), "snorm snorm_e rsnorm st_b st_s u uTc gpad C0 C1 xpad bpad c0 c1 c2 cb "
                      "ce1 cr xT Cp dt_add dt_abs dt_one dt_max dt dtm decm "
                      "rhs0 rhs1 cb0 cb1 xtok zc ze1 zr gate cbd0 cbd1 mix0 mix1 dsum fcd xf y yg ssq mean rms "
                      "ygn ygw ygTc bd0 bd1 mlo")
        MIX_A = Steps(sem("mix_a"), "TT u_z cexp zexp dexp dln aexp dneg dec0 dec1 sqrt mhi")
        MIX_T = Steps(sem("mix_t"), "snorm st uT z xbc bc dt cb xtok seg0 seg1 fcd y ygT ot M")
        MIX_P = Steps(sem("mix_p"), "bdz")
        ot_done = sem("ot_done")
        nat_done = sem("nat_done")
        y_done = sem("y_done")
        y_out = [sem(f"y_out{i}") for i in range(2)]
        o_col = logit
        y_row = expd

        def lin(base, step, g):
            return base + step * g

        a_rows = adj.rearrange("(b t p) c -> b p t c", p=P, t=T4)
        x_rows = x.rearrange("(b t p) d -> b p t d", p=P, t=T4)
        sw_rows = sw_dram.rearrange("(b t p) c -> b p t c", p=P, t=T4)
        out_rows = out.rearrange("(b t p) d -> b p t d", p=P, t=T4)
        LAST_BLOCKS = [(r, n2 + r, m2 + r) for r in range(BL)]

        fin_m = [m1] + [segs[-1].chunks[-1].m + RING * (segs[-1].rounds - 1) + 1 for _, segs in second_plan]
        fin_xt = [sum(1 for m in range(m1, fm) if sliced(m) is not None) for fm in fin_m]

        def wide(vec, parts):
            return vec.partition_broadcast(parts)

        tiny = [
            (temp[:, :], wide(temperature.rearrange("a h b c -> (a h b c)"), P)),
            (b_xT[:, :], b_x.rearrange("(h c) -> c h", c=HD)),
            (bsl[:, :], wide(b_slice, P)),
            (out_bc[:, :], out_b.rearrange("(p a) -> p a", a=1)),
            (b_fx_w[:, :], wide(b_fx, L)),
            (norm_ww[:, :], wide(norm_w, L)),
            (dt_bw[:, :], wide(dt_bias, L)),
            (a_lw[:, :], wide(A_log, L)),
            (Dw[:, :], wide(Dp, L)),
            (conv_ws[:, 0:KC, :], conv_w[0:INNER, :].rearrange("(k p) w -> p k w", p=P)),
            (conv_ws[0:NS, KC:CK, :], conv_w[INNER:CONV, :].rearrange("(k p) w -> p k w", p=NS)),
            (conv_bs[:, 0:KC], conv_b[0:INNER].rearrange("(k p) -> p k", p=P)),
            (conv_bs[0:NS, KC:CK], conv_b[INNER:CONV].rearrange("(k p) -> p k", p=NS)),
        ]
        TINY = 16 * len(tiny)

        block = ctx.enter_context(nc.Block())

        @block.sync
        def _(sp):
            def load_x(i):
                b = i if i < BL else 2 * BL - 1 - i
                if 2 <= i < BL + 2:
                    wait_step(sp, prep_v, "norm", i - 2)
                if i >= BL + 2:
                    wait_step(sp, fin_v, "x1", i - BL - 2)
                sp.dma_start(x_in[:, i % 2], x_rows[b]).then_inc(x_landed[i % 2], 16)

            def load_w(u):
                kind, src, k, _ = units[u]
                if u >= 2:
                    sp.wait_ge(c_filled, c_use(("w", u - 2)) + 1)
                dst = w_raw[0:k, u % 2, :]
                if kind == "fx":
                    dst = dst.rearrange("p (t d) -> p t d", t=T4)
                sp.dma_start(dst, src).then_inc(w_landed[u % 2], 16)

            sp.dma_start(lnx[:, 1, :], gnn_W).then_inc(setup_in, 16)
            sp.dma_start(w_sl, W_slice).then_inc(setup_in, 16)
            sp.dma_start(w_x_c, W_x.rearrange("(h c) d -> c h d", c=HD)).then_inc(setup_in, 16)
            load_x(0)

            def load(n, slot, K, J):
                sp.dma_start(a_ring[:, slot], a_rows[K][:, :, bass.ds(J * CH, CH)]).then_inc(a_in[slot], 16)

            for K, (sums, both) in enumerate(first_plan):
                if K + 1 < BL:
                    load_x(K + 1)
                for u in unit_block:
                    if unit_block[u] == K:
                        load_w(u)
                for seg in sums + both:
                    with rounds(sp, seg.rounds) as g:
                        for c in seg.chunks:
                            if c.n >= RING - 1:
                                sp.wait_ge(act_sum, lin(c.n - RING + 1, RING, g))
                                sp.wait_ge(dve_sum, lin(c.n - RING + 1, RING, g))
                            load(c.n, c.n % RING, K, lin(c.J, RING, g))

            load_x(BL)
            for I, segs in second_plan:
                load_x(2 * BL - 1 - I)
                for seg in segs:
                    with rounds(sp, seg.rounds) as g:
                        for c in seg.chunks:
                            if c.n < N0 + RING:
                                sp.wait_ge(act_sum, c.n - RING + 1)
                                sp.wait_ge(dve_sum, c.n - RING + 1)
                            else:
                                sp.wait_ge(t_done, lin(2 * (c.m - RING + 1), 2 * RING, g))
                            load(c.n, c.n % RING, I, lin(c.J, RING, g))

            for i in range(2):
                sp.wait_ge(sw_out[i], 16 * (TILES // 2))

            def load_sw(r, n, m, g=0):
                sp.wait_ge(t_done, lin(2 * (m - RING + 1), 2 * RING, g))
                sp.dma_start(a_ring[:, n % RING], sw_rows[r + RING * g]).then_inc(a_in[n % RING], 16)

            def store_y(r, g=0):
                sp.wait_ge(y_done, lin(r + 1, RING, g))
                sp.dma_start(out_rows[g * -RING + (BL - 1 - r)], y_row[:, r % 2, :].rearrange("p (t d) -> p t d", t=T4))\
                    .then_inc(y_out[r % 2], 16)

            for r, n, m in LAST_BLOCKS[:RING]:
                load_sw(r, n, m)
            with rounds(sp, BL // RING - 1) as g:
                for r, n, m in LAST_BLOCKS[RING:2 * RING]:
                    store_y(r - RING, g)
                    load_sw(r, n, m, g)
            for r in range(BL - RING, BL):
                store_y(r)
            for i in range(2):
                sp.wait_ge(y_out[i], 16 * (BL // 2))

        @block.tensor
        def _(pe):
            def turn(n, m, h, g=0):
                if h == 0:
                    pe.wait_ge(a_in[n % RING], lin(16 * (n // RING + 1), 16, g))
                if m >= 1:
                    pe.wait_ge(lo_done, lin(2 * (m - 1) + h + 1, 2 * RING, g))
                for s in range(2):
                    for t in range(T4):
                        at = s * CH + t * P
                        col = (2 * h + s) * P
                        ins = pe.transpose(turned[h][:, at:at + P], a_ring[:, n % RING, t, col:col + P], ident[:, :])
                ins.then_inc(t_done, 1)

            def contract(m, h, first, last, g=0, stat_hi=None, stat_lo=None):
                pe.wait_ge(lo_done, lin(2 * m + h + 1, 2 * RING, g))
                slot = 2 * (m % 2) + h
                sh = s_hi[:, m % 2] if stat_hi is None else stat_hi
                sl = s_lo[:, m % 2] if stat_lo is None else stat_lo
                for s in range(2):
                    col = (2 * h + s) * P
                    mov_hi = hi[:, slot, s * CH:(s + 1) * CH]
                    mov_lo = lo[:, slot, s * CH:(s + 1) * CH]
                    opens = first and h == 0 and s == 0
                    closes = last and h == 1 and s == 1
                    pe.matmul(acc[:, :], sh[:, col:col + P], mov_hi, start=opens, stop=False, skip_group_check=True)
                    pe.matmul(acc[:, :], sh[:, col:col + P], mov_lo, start=False, stop=False, skip_group_check=True)
                    ins = pe.matmul(acc[:, :], sl[:, col:col + P], mov_hi, start=False, stop=closes,
                                    skip_group_check=True)
                ins.then_inc(mm_done, 1)

            def clear_acc():
                pe.matmul(acc[:, :], m_hi[:, 0:P], m_hi[:, :], start=True, stop=False, skip_group_check=True)

            def chunk_sums(c, last, ahead, g=0):
                for h in range(2):
                    if ahead:
                        turn(c.n + 1, c.m + 1, h, g)
                    if h == 0:
                        pe.wait_ge(sl_done, lin(c.m + 1, RING, g))
                    contract(c.m, h, c.first, last, g)

            def weights_turned(use, src, k, cols):
                if use >= 1:
                    pe.wait_ge(c_copied, use)
                for t in range(T4):
                    ins = pe.transpose(bank_c[0:cols, t * P:t * P + k], src(t), ident[0:k, 0:k])
                ins.then_inc(c_filled, 1)

            def prepare(K):
                wait_step(pe, prep_v, "norm", K)
                weights_turned(c_use(("x", K)), lambda t: lnx[:, t, :], P, P)
                pe.wait_ge(c_copied, c_use(("x", K)) + 1)
                if K >= 2:
                    wait_step(pe, deg_v, "scaled", K - 2)
                bank = (bank_a, bank_b)[K % 2]
                for t in range(T4):
                    ins = pe.matmul(bank[:, t * D:(t + 1) * D], lnxT[:, t * P:(t + 1) * P], gnn_WT[:, :],
                                    start=True, stop=True)
                ins.then_inc(prep_t.sem, 1)

            pe.wait_ge(ident_ok, 4)
            pe.wait_ge(setup_in, 48)
            pe.transpose(bank_c[:, 0:P], lnx[:, 1, :], ident[:, :]).then_inc(c_filled, 1)
            pe.transpose(bank_a[0:HD, 0:G], w_sl, ident[0:G, 0:G]).then_inc(set_t.sem, 1)
            wait_step(pe, set_v, "wslT")
            for h in range(H):
                ins = pe.matmul(bank_a[:, h * G:(h + 1) * G], w_x_c[:, h, :], w_slT, start=True, stop=True)
            ins.then_inc(set_t.sem, 1)
            for h in range(H):
                ins = pe.matmul(bank_b[:, h * G:(h + 1) * G], b_x_wide[:, h, :], w_slT, start=True, stop=True)
            ins.then_inc(set_t.sem, 1)
            wait_step(pe, set_v, "blog")
            prepare(0)

            for K, (sums, both) in enumerate(first_plan):
                if K + 1 < BL:
                    prepare(K + 1)
                for u in unit_block:
                    if unit_block[u] == K:
                        kind, _, k, dst = units[u]
                        pe.wait_ge(w_landed[u % 2], 16 * (u // 2 + 1))
                        weights_turned(c_use(("w", u)), lambda t: w_raw[0:k, u % 2, t * P:(t + 1) * P], k, P)
                c0 = both[0].chunks[0]
                for h in range(2):
                    turn(c0.n, c0.m, h)
                if K >= 1:
                    pe.wait_ge(row_done, K)
                if not c0.first:
                    clear_acc()
                for i, seg in enumerate(both):
                    with rounds(pe, seg.rounds) as g:
                        for j, c in enumerate(seg.chunks):
                            last = i == len(both) - 1 and j == len(seg.chunks) - 1
                            chunk_sums(c, last, not last, g)

            def finish(f):
                pe.wait_ge(fin_sums, f + 1)
                if f == 0:
                    wait_step(pe, deg_v, "scaled", BL - 1)
                else:
                    wait_step(pe, fin_v, "add", f - 1)
                    if fin_xt[f]:
                        pe.wait_ge(xtc_done, fin_xt[f])
                for t in range(T4):
                    ins = pe.transpose(bank_a[:, t * D:(t + 1) * D], row_st[:, t * P:(t + 1) * P], ident[:, :])
                ins.then_inc(fin_t.sem, 1)

            def slice_step(k, fins, g=0):
                R2 = RING // 2
                if 0 <= k < TILES:
                    pe.wait_ge(xa_done, lin(k + 1, R2, g))
                    wait_step(pe, fin_v, "add", fins - 1)
                    if k >= 1:
                        pe.wait_ge(xtc_done, lin(k, R2, g))
                    pe.transpose(bank_a[:, 0:P], xn_a[:, k % 2, :], ident[:, :]).then_inc(xt_done, 1)
                q = k - 1
                if 0 <= q < TILES:
                    if q >= 1:
                        pe.wait_ge(sm_done.sem, lin(sm_done.value("bias", q - 1), 3 * R2, g))
                    pe.wait_ge(xtc_done, lin(q + 1, R2, g))
                    pe.matmul(bank_c[:, :], xnT[:, q % 2, :], W_logT[:, :], start=True, stop=True).then_inc(lg_done, 1)
                q = k - 5
                if 0 <= q < TILES:
                    pe.wait_ge(sw_done.sem, lin(sw_done.value("weights", q), 2 * R2, g))
                    pe.wait_ge(xb_done, lin(q + 1, R2, g))
                    pe.matmul(bank_b[:, :], xn_b[:, q % 2, :], sw[:, q % 2, :], start=(q == 0), stop=(q == TILES - 1),
                              skip_group_check=True).then_inc(tt_done, 1)

            for h in range(2):
                turn(N0, M0, h)
            finish(0)
            fins = 1
            for k in (-2, -1):
                slice_step(k, fins)
            for I, segs in second_plan:
                c0 = segs[0].chunks[0]
                pe.wait_ge(row_done if fins == 1 else fin_sums, BL if fins == 1 else fins)
                if not c0.first:
                    clear_acc()
                for i, seg in enumerate(segs):
                    with rounds(pe, seg.rounds) as g:
                        for j, c in enumerate(seg.chunks):
                            last = i == len(segs) - 1 and j == len(seg.chunks) - 1
                            chunk_sums(c, last, not (last and I == 0), g)
                            k = sliced(c.m)
                            if k is not None:
                                slice_step(k, fins, g)
                finish(fins)
                fins += 1
            for k in range(TILES - 6, SLICE_LAST + 1):
                slice_step(k, fins)

            def T_(name, rnd=0):
                return wait_step(pe, MIX_T, name)

            def inc(ins):
                ins.then_inc(MIX_T.sem, 1)

            pe.wait_ge(tt_done, TILES)
            wait_step(pe, sw_done, "total", TILES - 1)
            for h in range(H):
                ins = pe.matmul(bank_a[0:G, h:h + 1], sw_sum[:, h * G:(h + 1) * G], ones[:, 0:1], start=True, stop=True)
            inc(ins)
            wait_step(pe, MIX_A, "TT")
            for h in range(H):
                ins = pe.matmul(bank_c[0:G, h * HD:(h + 1) * HD], TTs[:, h * G:(h + 1) * G],
                                W_fxT[:, h * HD:(h + 1) * HD], start=True, stop=True)
            inc(ins)
            wait_step(pe, MIX_V, "u")
            for c in range(KC):
                ins = pe.transpose(bank_b[:, c * L:(c + 1) * L], u_tok[:, c * P:(c + 1) * P], ident[0:L, 0:L])
            inc(ins)
            wait_step(pe, MIX_V, "uTc")
            for c in range(KC):
                ins = pe.matmul(bank_c[0:L, :], uT[:, c, :], in_wT[:, c, 0:INNER], start=(c == 0), stop=(c == KC - 1))
            inc(ins)
            for k in range(KC):
                for c in range(KC):
                    ins = pe.matmul(bank_b[:, k * L:(k + 1) * L], in_wT[:, c, INNER + k * P:INNER + (k + 1) * P],
                                    uT[:, c, :], start=(c == 0), stop=(c == KC - 1))
            inc(ins)
            for k in range(2):
                for c in range(KC):
                    w0 = 2 * INNER + k * NS
                    ins = pe.matmul(acc[0:NS, k * L:(k + 1) * L], in_wT[:, c, w0:w0 + NS],
                                    uT[:, c, :], start=(c == 0), stop=(c == KC - 1))
            inc(ins)
            for c in range(KC):
                ins = pe.matmul(bank_a[0:L, 0:2 * H], uT[:, c, :], in_wT[:, c, PROJ - 2 * H:PROJ],
                                start=(c == 0), stop=(c == KC - 1))
            inc(ins)
            wait_step(pe, MIX_V, "Cp")
            for i, at in ((0, 0), (1, 2)):
                ins = pe.matmul(acc[0:L, i * L:(i + 1) * L], xT[0:NS, KC, :], Cpad[:, at:at + L], start=True, stop=True)
            inc(ins)
            for c in range(KC):
                ins = pe.transpose(bank_b[0:L, c * P:(c + 1) * P], xT[:, c, :], ident[:, :])
            inc(ins)
            for i, (w, name) in enumerate(((more, "rhs0"), (less, "rhs1"))):
                wait_step(pe, MIX_V, name)
                inc(pe.matmul(turned[i][0:L, 0:H * L], w[:, :], seg_rhs[i].rearrange("p a b -> p (a b)"),
                              start=True, stop=True))
            wait_step(pe, MIX_V, "dt_add")
            for c in range(KC):
                ins = pe.matmul(bank_a[0:L, 0:H], xT[:, c, :], fcD_T[:, c, :], start=(c == 0), stop=(c == KC - 1))
            inc(ins)
            wait_step(pe, MIX_V, "dsum")
            for h in range(H):
                ins = pe.matmul(bank_c[0:L, h * HD:(h + 1) * HD], dsum[:, h, :], x_tok[:, h * HD:(h + 1) * HD],
                                start=True, stop=True)
            inc(ins)
            wait_step(pe, MIX_V, "ygw")
            for c in range(KC):
                ins = pe.transpose(bank_b[:, c * L:(c + 1) * L], ygw[:, c * P:(c + 1) * P], ident[0:L, 0:L])
            inc(ins)
            wait_step(pe, MIX_V, "ygTc")
            for k in range(KC):
                for c in range(KC):
                    ins = pe.matmul(bank_a[:, k * L:(k + 1) * L], hy_outT[:, c, k * P:(k + 1) * P], ygT[:, c, :],
                                    start=(c == 0), stop=(c == KC - 1))
            inc(ins)
            wait_step(pe, MIX_V, "bd1")
            for k in range(KC):
                ins = pe.matmul(bank_c[:, k * D:(k + 1) * D], bd[:, k, :], out_wT[:, k, :], start=True, stop=True)
            inc(ins)

            def back(r, g=0):
                pe.wait_ge(ot_done, lin(r + 1, RING, g))
                if r >= 1:
                    pe.wait_ge(y_done, lin(r, RING, g))
                for t in range(T4):
                    ins = pe.transpose(bank_a[:, t * D:(t + 1) * D], o_col[:, r % 2, t * P:(t + 1) * P], ident[:, :])
                ins.then_inc(nat_done, 1)

            def last_block(r, n, m, g=0, final=False, start=False):
                for h in range(2):
                    if not final:
                        turn(n + 1, m + 1, h, g)
                    if h == 0 and not start:
                        pe.wait_ge(ot_done, lin(r, RING, g))
                    contract(m, h, True, True, g, m_hi, m_lo)
                if not start:
                    back(r - 1, g)

            turn(n2, m2, 0)
            turn(n2, m2, 1)
            wait_step(pe, MIX_V, "mlo")
            for r, n, m in LAST_BLOCKS[:RING]:
                last_block(r, n, m, start=(r == 0))
            with rounds(pe, BL // RING - 2) as g:
                for r, n, m in LAST_BLOCKS[RING:2 * RING]:
                    last_block(r, n, m, g)
            for r, n, m in LAST_BLOCKS[BL - RING:]:
                last_block(r, n, m, final=(r == BL - 1))
            back(BL - 1)

        @block.scalar
        def _(act):
            def high(m, h, g=0):
                act.wait_ge(t_done, lin(2 * m + h + 1, 2 * RING, g))
                if m >= 2:
                    act.wait_ge(mm_done, lin(2 * (m - 2) + h + 1, 2 * RING, g))
                act.activation(hi[:, 2 * (m % 2) + h, :], turned[h][:, :], ACT.Copy).then_inc(hi_done, 1)

            def support_high(c, g=0):
                if c.m >= 2:
                    act.wait_ge(mm_done, lin(2 * (c.m - 1), 2 * RING, g))
                act.activation(s_hi[:, c.m % 2, :], supf[:, bass.ds(lin(c.J, RING, g) * CH, CH)], ACT.Copy)\
                    .then_inc(sh_done, 1)

            def row_sums(c, g=0):
                act.wait_ge(a_in[c.n % RING], lin(16 * (c.n // RING + 1), 16, g))
                if c.n >= 1:
                    act.wait_ge(act_sum, lin(c.n, RING, g))
                for t in range(2):
                    ins = act.activation(junk[:, t * CH:(t + 1) * CH], a_ring[:, c.n % RING, t, :], ACT.Copy,
                                         accum_out=part[:, t, bass.ds(lin(c.J, RING, g), 1)])
                ins.then_inc(act_sum, 1)

            def copy_c(use, dst, src):
                act.wait_ge(c_filled, use + 1)
                act.activation(dst, src, ACT.Copy).then_inc(c_copied, 1)

            def prepare(K):
                wait_step(act, prep_v, "eps", K)
                act.activation(sd[:, :], mv[:, :, 1], ACT.Sqrt).then_inc(prep_a.sem, 1)
                if K >= 1:
                    wait_step(act, prep_t, "support", K - 1)
                copy_c(c_use(("x", K)), lnxT[:, :], bank_c[:, :])

            copy_c(0, gnn_WT[:, :], bank_c[:, 0:P])
            prepare(0)
            for K, (sums, both) in enumerate(first_plan):
                if K + 1 < BL:
                    prepare(K + 1)
                for u in unit_block:
                    if unit_block[u] == K:
                        k, dst = units[u][2], units[u][3]
                        copy_c(c_use(("w", u)), dst,
                               bank_c[:, :].rearrange("p (t k) -> p t k", t=T4)[:, :, 0:k])
                for seg in sums:
                    with rounds(act, seg.rounds) as g:
                        for c in seg.chunks:
                            row_sums(c, g)
                for i, seg in enumerate(both):
                    with rounds(act, seg.rounds) as g:
                        for j, c in enumerate(seg.chunks):
                            last = i == len(both) - 1 and j == len(seg.chunks) - 1
                            row_sums(c, g)
                            high(c.m, 0, g)
                            high(c.m, 1, g)
                            if last:
                                wait_step(act, deg_v, "one", K)
                                act.activation(rsq[:, :], rsum[:, :], ACT.Sqrt).then_inc(deg_a.sem, 1)
                                wait_step(act, deg_v, "scaled", K)
                            support_high(c, g)
                act.wait_ge(mm_done, 2 * (both[-1].chunks[-1].m + 1))
                act.activation(rows[:, BL - 1 - K, :], acc[:, :], ACT.Copy).then_inc(row_done, 1)

            def slice_step(k, g=0):
                R2 = RING // 2
                if 0 <= k < TILES:
                    act.wait_ge(xt_done, lin(k + 1, R2, g))
                    if k >= 2:
                        act.wait_ge(lg_done, lin(k - 1, R2, g))
                    act.activation(xnT[:, k % 2, :], bank_a[:, 0:P], ACT.Copy).then_inc(xtc_done, 1)
                q = k - 3
                if 0 <= q < TILES:
                    act.wait_ge(sm_done.sem, lin(sm_done.value("shift", q), 3 * R2, g))
                    if q >= 2:
                        act.wait_ge(sw_done.sem, lin(sw_done.value("weights", q - 2), 2 * R2, g))
                    act.activation(expd[:, q % 2, :], logit[:, q % 2, :], ACT.Exp).then_inc(exp_done, 1)

            for k in (-2, -1):
                slice_step(k)
            for I, segs in second_plan:
                for seg in segs:
                    with rounds(act, seg.rounds) as g:
                        for c in seg.chunks:
                            high(c.m, 0, g)
                            high(c.m, 1, g)
                            support_high(c, g)
                            k = sliced(c.m)
                            if k is not None:
                                slice_step(k, g)
            for k in range(TILES - 6, SLICE_LAST + 1):
                slice_step(k)

            def inc(ins):
                ins.then_inc(MIX_A.sem, 1)

            act.wait_ge(tt_done, TILES)
            inc(act.activation(TTs, bank_b[:, :], ACT.Copy))
            wait_step(act, MIX_T, "z")
            inc(act.activation(z_tok, bank_c[0:L, :], ACT.Copy))
            wait_step(act, MIX_V, "cb")
            inc(act.activation(cve, cvb, ACT.Exp, scale=-1.0))
            wait_step(act, MIX_A, "u_z")
            inc(act.activation(z_e, z_tok, ACT.Exp, scale=-1.0))
            wait_step(act, MIX_V, "dt_abs")
            inc(act.activation(dtc, dtb, ACT.Exp))
            wait_step(act, MIX_V, "dt_one")
            inc(act.activation(dtd, dtm, ACT.Ln))
            wait_step(act, MIX_V, "snorm")
            inc(act.activation(a_ex, a_cl, ACT.Exp))
            wait_step(act, MIX_V, "dtm")
            inc(act.activation(dec, decm, ACT.Copy, scale=-1.0))
            for i in range(2):
                wait_step(act, MIX_T, f"seg{i}")
                inc(act.activation(dec_e[i], turned[i][0:L, 0:H * L].rearrange("p (h l) -> p h l", h=H), ACT.Exp))
            wait_step(act, MIX_V, "mean")
            inc(act.activation(ygq[:, :], ygm[:, :], ACT.Sqrt))
            wait_step(act, MIX_T, "M")
            inc(act.activation(m_hi[:, :], bank_c[:, :], ACT.Copy))

            def last_block(r, n, m, g=0):
                high(m, 0, g)
                high(m, 1, g)
                act.wait_ge(mm_done, lin(2 * (m + 1), 2 * RING, g))
                if r >= 2:
                    act.wait_ge(nat_done, lin(r - 1, RING, g))
                act.activation(o_col[:, r % 2, :], acc[:, :], ACT.Identity, bias=out_bc[:, 0:1]).then_inc(ot_done, 1)

            for r, n, m in LAST_BLOCKS[:RING]:
                last_block(r, n, m)
            with rounds(act, BL // RING - 1) as g:
                for r, n, m in LAST_BLOCKS[RING:2 * RING]:
                    last_block(r, n, m, g)

        @block.vector
        def _(dve):
            def rest(m, h, g=0):
                dve.wait_ge(hi_done, lin(2 * m + h + 1, 2 * RING, g))
                slot = 2 * (m % 2) + h
                dve.tensor_tensor(lo[:, slot, :], turned[h][:, :], hi[:, slot, :], ALU.subtract).then_inc(lo_done, 1)

            def support_rest(c, g=0):
                dve.wait_ge(sh_done, lin(c.m + 1, RING, g))
                dve.tensor_tensor(s_lo[:, c.m % 2, :], supf[:, bass.ds(lin(c.J, RING, g) * CH, CH)],
                                  s_hi[:, c.m % 2, :], ALU.subtract).then_inc(sl_done, 1)

            def row_sums(c, g=0):
                dve.wait_ge(a_in[c.n % RING], lin(16 * (c.n // RING + 1), 16, g))
                dve.tensor_reduce(part[:, 2:T4, bass.ds(lin(c.J, RING, g), 1)],
                                  a_ring[:, c.n % RING, 2:T4, :], AX.X, ALU.add).then_inc(dve_sum, 1)

            def prepare(K):
                dve.wait_ge(x_landed[K % 2], 16 * (K // 2 + 1))
                for t in range(T4):
                    ins = dve.bn_stats(bn[:, t, :], x_in[:, K % 2, t, :])
                ins.then_inc(prep_v.sem, 1)
                wait_step(dve, prep_v, "stats", K)
                for t in range(T4):
                    ins = dve.bn_aggr(mv[:, t, :], bn[:, t, :])
                ins.then_inc(prep_v.sem, 1)
                wait_step(dve, prep_v, "aggr", K)
                dve.tensor_scalar(mv[:, :, 1], mv[:, :, 1], LN_EPS, None, ALU.add).then_inc(prep_v.sem, 1)
                wait_step(dve, prep_a, "sqrt", K)
                dve.reciprocal(rstd4[:, :], sd[:, :]).then_inc(prep_v.sem, 1)
                wait_step(dve, prep_v, "rstd", K)
                if K >= 1:
                    dve.wait_ge(c_filled, c_use(("x", K - 1)) + 1)
                else:
                    dve.wait_ge(c_filled, 1)
                    wait_step(dve, set_t, "wslT")
                for t in range(T4):
                    ins = dve.tensor_scalar(lnx[:, t, :], x_in[:, K % 2, t, :], mv[:, t, 0:1], rstd4[:, t:t + 1],
                                            ALU.subtract, ALU.mult)
                ins.then_inc(prep_v.sem, 1)

            def degrees(K):
                dve.wait_ge(act_sum, BL * (K + 1))
                dve.wait_ge(dve_sum, BL * (K + 1))
                dve.tensor_reduce(rsum[:, :], part[:, :, :], AX.X, ALU.add).then_inc(deg_v.sem, 1)
                wait_step(dve, deg_v, "rows", K)
                dve.tensor_scalar(rsum[:, :], rsum[:, :], 1.0, None, ALU.add).then_inc(deg_v.sem, 1)
                wait_step(dve, deg_a, "sqrt", K)
                dve.reciprocal(dcol[:, K * T4:(K + 1) * T4], rsq[:, :]).then_inc(deg_v.sem, 1)
                wait_step(dve, deg_v, "inv", K)
                wait_step(dve, prep_t, "support", K)
                bank = (bank_a, bank_b)[K % 2]
                dve.tensor_tensor(sup[:, K * T4:(K + 1) * T4, :], bank[:, :].rearrange("p (t d) -> p t d", t=T4),
                                  dcol[:, K * T4:(K + 1) * T4].unsqueeze(2).to_broadcast([P, T4, D]),
                                  ALU.mult).then_inc(deg_v.sem, 1)

            dve.wait_ge(tiny_in, TINY)
            dve.tensor_scalar(temp[:, :], temp[:, :], 1e-6, None, ALU.max).then_inc(set_v.sem, 1)
            wait_step(dve, set_v, "tmax")
            dve.reciprocal(rtemp[:, :], temp[:, :]).then_inc(set_v.sem, 1)
            dve.tensor_copy(b_x_wide, b_xT[:, :].unsqueeze(2).to_broadcast([HD, H, P])).then_inc(set_v.sem, 1)
            wait_step(dve, set_t, "wslT")
            dve.tensor_copy(w_slT, bank_a[0:HD, 0:G]).then_inc(set_v.sem, 1)
            rt = rtemp[:, :].unsqueeze(2).to_broadcast([P, H, G])
            wait_step(dve, set_t, "wlog")
            wait_step(dve, set_v, "tinv")
            dve.tensor_tensor(W_logT[:, :].rearrange("p (h g) -> p h g", h=H),
                              bank_a[:, :].rearrange("p (h g) -> p h g", h=H), rt, ALU.mult).then_inc(set_v.sem, 1)
            wait_step(dve, set_t, "blog")
            bl = b_log[:, :].rearrange("p (h g) -> p h g", h=H)
            dve.tensor_tensor(bl, bank_b[:, :].rearrange("p (h g) -> p h g", h=H),
                              bsl[:, :].unsqueeze(1).to_broadcast([P, H, G]), ALU.add).then_inc(set_v.sem, 1)
            wait_step(dve, set_v, "blog_sum")
            dve.tensor_tensor(bl, bl, rt, ALU.mult).then_inc(set_v.sem, 1)

            prepare(0)
            for K, (sums, both) in enumerate(first_plan):
                if K + 1 < BL:
                    prepare(K + 1)
                for seg in sums:
                    with rounds(dve, seg.rounds) as g:
                        for c in seg.chunks:
                            row_sums(c, g)
                for i, seg in enumerate(both):
                    with rounds(dve, seg.rounds) as g:
                        for j, c in enumerate(seg.chunks):
                            rest(c.m, 0, g)
                            rest(c.m, 1, g)
                            row_sums(c, g)
                            if i == len(both) - 1 and j == len(seg.chunks) - 1:
                                degrees(K)
                            support_rest(c, g)

            def finish(f):
                I = BL - 1 - f
                if f == 0:
                    dve.wait_ge(row_done, BL)
                    dve.tensor_copy(row_st[:, :], rows[:, f, :]).then_inc(fin_sums, 1)
                else:
                    dve.wait_ge(mm_done, 2 * fin_m[f])
                    dve.tensor_tensor(row_st[:, :], acc[:, :], rows[:, f, :], ALU.add).then_inc(fin_sums, 1)
                wait_step(dve, fin_t, "turned", f)
                dve.tensor_tensor(nat[:, :, :], bank_a[:, :].rearrange("p (t d) -> p t d", t=T4),
                                  sup[:, I * T4:(I + 1) * T4, :], ALU.add).then_inc(fin_v.sem, 1)
                wait_step(dve, fin_v, "add", f)
                dve.scalar_tensor_tensor(out=nat[:, :, :], in0=nat[:, :, :], scalar=0.0,
                                         in1=dcol[:, I * T4:(I + 1) * T4].unsqueeze(2).to_broadcast([P, T4, D]),
                                         op0=ALU.max, op1=ALU.mult).then_inc(fin_v.sem, 1)
                wait_step(dve, fin_v, "relu", f)
                i = BL + f
                dve.wait_ge(x_landed[i % 2], 16 * (i // 2 + 1))
                dve.tensor_tensor(x1[:, f * T4:(f + 1) * T4, :], nat[:, :, :], x_in[:, i % 2], ALU.add)\
                    .then_inc(fin_v.sem, 1)

            def slice_step(k, fins, g=0):
                R2 = RING // 2
                q = k - 2
                if 0 <= q < TILES:
                    lt = logit[:, q % 2, :].rearrange("p (h g) -> p h g", h=H)
                    dve.wait_ge(lg_done, lin(q + 1, R2, g))
                    if q >= 2:
                        dve.wait_ge(exp_done, lin(q - 1, R2, g))
                    dve.tensor_tensor(logit[:, q % 2, :], bank_c[:, :], b_log[:, :], ALU.add).then_inc(sm_done.sem, 1)
                    dve.wait_ge(sm_done.sem, lin(sm_done.value("bias", q), 3 * R2, g))
                    if q >= 1:
                        dve.wait_ge(sm_done.sem, lin(sm_done.value("shift", q - 1), 3 * R2, g))
                    dve.tensor_reduce(mx[:, :], lt, AX.X, ALU.max).then_inc(sm_done.sem, 1)
                    dve.wait_ge(sm_done.sem, lin(sm_done.value("max", q), 3 * R2, g))
                    dve.tensor_tensor(lt, lt, mx[:, :].unsqueeze(2).to_broadcast([P, H, G]), ALU.subtract)\
                        .then_inc(sm_done.sem, 1)
                q = k - 4
                if 0 <= q < TILES:
                    dve.wait_ge(exp_done, lin(q + 1, R2, g))
                    if q >= 1:
                        dve.wait_ge(rd_done.sem, lin(rd_done.value("inv", q - 1), 2 * R2, g))
                    dve.tensor_reduce(den[:, :], expd[:, q % 2, :].rearrange("p (h g) -> p h g", h=H), AX.X, ALU.add)\
                        .then_inc(rd_done.sem, 1)
                    dve.wait_ge(rd_done.sem, lin(rd_done.value("sum", q), 2 * R2, g))
                    if q >= 2:
                        dve.wait_ge(sw_done.sem, lin(sw_done.value("weights", q - 2), 2 * R2, g))
                    dve.reciprocal(rden[:, q % 2, :], den[:, :]).then_inc(rd_done.sem, 1)
                    if q >= 2:
                        dve.wait_ge(tt_done, lin(q - 1, R2, g))
                    ti = lin(q, R2, g)
                    dve.tensor_scalar(xn_b[:, q % 2, :], x1[:, bass.ds(ti, 1), :].rearrange("p a d -> p (a d)"),
                                      mean[:, bass.ds(ti, 1)], rstd[:, bass.ds(ti, 1)],
                                      ALU.subtract, ALU.mult).then_inc(xb_done, 1)
                q = k + 1
                if 0 <= q < TILES:
                    ti = lin(q, R2, g)
                    dve.wait_ge(rstd_done, lin(q + 1, R2, g))
                    if q >= 2:
                        dve.wait_ge(xt_done, lin(q - 1, R2, g))
                    dve.tensor_scalar(xn_a[:, q % 2, :], x1[:, bass.ds(ti, 1), :].rearrange("p a d -> p (a d)"),
                                      mean[:, bass.ds(ti, 1)], rstd[:, bass.ds(ti, 1)],
                                      ALU.subtract, ALU.mult).then_inc(xa_done, 1)
                q = k + 2
                if 0 <= q < TILES:
                    ti = lin(q, R2, g)
                    wait_step(dve, fin_v, "x1", fins - 1)
                    dve.bn_stats(stat[:, q % 2, :], x1[:, bass.ds(ti, 1), :].rearrange("p a d -> p (a d)"))\
                        .then_inc(st_done.sem, 1)
                    even, odd = stat[:, q % 2, 1:3], stat[:, q % 2, 4:6]

                    def after(name):
                        dve.wait_ge(st_done.sem, lin(st_done.value(name, q), 7 * R2, g))

                    after("stats")
                    dve.tensor_tensor(both_st[:, :], even, odd, ALU.add).then_inc(st_done.sem, 1)
                    dve.tensor_tensor(gap[:, :], even[:, 0:1], odd[:, 0:1], ALU.subtract).then_inc(st_done.sem, 1)
                    after("sum")
                    dve.tensor_scalar(mean[:, bass.ds(ti, 1)], both_st[:, 0:1], 0.5, None, ALU.mult)\
                        .then_inc(st_done.sem, 1)
                    dve.tensor_scalar(within[:, :], both_st[:, 1:2], 1.0 / D, LN_EPS, ALU.mult, ALU.add)\
                        .then_inc(st_done.sem, 1)
                    after("gap")
                    dve.tensor_scalar(gap[:, :], gap[:, :], 0.5, None, ALU.mult).then_inc(st_done.sem, 1)
                    if q >= 2:
                        dve.wait_ge(rstd_done, lin(q - 1, R2, g))
                    after("half")
                    dve.tensor_scalar(vareps[:, q % 2:q % 2 + 1], gap[:, :], gap[:, 0:1], within[:, 0:1],
                                      ALU.mult, ALU.add).then_inc(st_done.sem, 1)

            finish(0)
            fins = 1
            for k in (-2, -1):
                slice_step(k, fins)
            for I, segs in second_plan:
                for seg in segs:
                    with rounds(dve, seg.rounds) as g:
                        for c in seg.chunks:
                            rest(c.m, 0, g)
                            rest(c.m, 1, g)
                            support_rest(c, g)
                            k = sliced(c.m)
                            if k is not None:
                                slice_step(k, fins, g)
                finish(fins)
                fins += 1
            for k in range(TILES - 6, SLICE_LAST + 1):
                slice_step(k, fins)

            def V(name):
                wait_step(dve, MIX_V, name)

            def Aw(name):
                wait_step(dve, MIX_A, name)

            def Tw(name):
                wait_step(dve, MIX_T, name)

            order = iter(MIX_V.names)

            def inc(name, ins):
                assert next(order) == name, name
                ins.then_inc(MIX_V.sem, 1)

            def bc(ap, shape):
                return ap.unsqueeze(2).to_broadcast(shape)

            Tw("snorm")
            dve.tensor_scalar(a_cl, a_lw[:, :], EXP_MAX, None, ALU.min)
            inc("snorm", dve.tensor_copy(snorm, bank_a[0:L, 0:H]))
            V("snorm")
            inc("snorm_e", dve.tensor_scalar(snorm_e, snorm, 1e-5, None, ALU.add))
            V("snorm_e")
            inc("rsnorm", dve.reciprocal(rsnorm, snorm_e))
            inc("st_b", dve.tensor_tensor(st_b, b_fx_w[:, :].rearrange("p (h c) -> p h c", h=H),
                                          bc(snorm, [L, H, HD]), ALU.mult))
            V("st_b")
            Tw("st")
            inc("st_s", dve.tensor_tensor(st_s, bank_c[0:L, :].rearrange("p (h c) -> p h c", h=H), st_b, ALU.add))
            V("st_s")
            inc("u", dve.tensor_tensor(u_tok.rearrange("p (h c) -> p h c", h=H), st_s, bc(rsnorm, [L, H, HD]), ALU.mult))
            Tw("uT")
            inc("uTc", dve.tensor_copy(uT, bank_b[:, 0:KC * L].rearrange("p (k l) -> p k l", k=KC)))
            inc("gpad", dve.memset(cpad, 0.0))
            inc("C0", dve.memset(Cpad, 0.0))
            inc("C1", dve.memset(ygs[:, :], 0.0))
            V("gpad")
            Tw("xbc")
            inc("xpad", dve.tensor_copy(cpad[:, 0:KC, 2:], bank_b[:, 0:KC * L].rearrange("p (k l) -> p k l", k=KC)))
            Tw("bc")
            inc("bpad", dve.tensor_copy(cpad[0:NS, KC:, 2:], acc[0:NS, 0:2 * L].rearrange("p (k l) -> p k l", k=2)))
            V("bpad")
            inc("c0", dve.tensor_tensor(cva, cpad[:, :, 0:L], bc(conv_ws[:, :, 0], [P, CK, L]), ALU.mult))
            inc("c1", dve.tensor_tensor(cvb, cpad[:, :, 1:L + 1], bc(conv_ws[:, :, 1], [P, CK, L]), ALU.mult))
            inc("c2", dve.tensor_tensor(cvc, cpad[:, :, 2:L + 2], bc(conv_ws[:, :, 2], [P, CK, L]), ALU.mult))
            V("c2")
            dve.tensor_tensor(cva, cva, cvb, ALU.add).then_inc(conv_v, 1)
            dve.wait_ge(conv_v, 1)
            dve.tensor_tensor(cva, cva, cvc, ALU.add).then_inc(conv_v, 1)
            dve.wait_ge(conv_v, 2)
            inc("cb", dve.tensor_tensor(cvb, cva, bc(conv_bs[:, :], [P, CK, L]), ALU.add))
            Aw("cexp")
            inc("ce1", dve.tensor_scalar(cve, cve, 1.0, None, ALU.add))
            V("ce1")
            inc("cr", dve.reciprocal(cvr, cve))
            V("cr")
            inc("xT", dve.tensor_tensor(xT, cvb, cvr, ALU.mult))
            V("xT")
            inc("Cp", dve.tensor_copy(Cpad[:, 1:L + 1], xT[0:NS, KC + 1, :]))
            Tw("dt")
            inc("dt_add", dve.tensor_tensor(dtr, bank_a[0:L, 0:2 * H].rearrange("p (a h) -> p a h", a=2),
                                            dt_bw[:, :].unsqueeze(1).to_broadcast([L, 2, H]), ALU.add))
            V("dt_add")
            dve.tensor_scalar(dta, dtr, -1.0, None, ALU.mult).then_inc(conv_v, 1)
            dve.wait_ge(conv_v, 3)
            inc("dt_abs", dve.tensor_tensor(dtb, dtr, dta, ALU.min))
            Aw("dexp")
            inc("dt_one", dve.tensor_scalar(dtm, dtc, 1.0, None, ALU.add))
            inc("dt_max", dve.tensor_scalar(dtr, dtr, 0.0, None, ALU.max))
            Aw("dln")
            V("dt_max")
            inc("dt", dve.tensor_tensor(dt, dtr, dtd, ALU.add))
            V("dt")
            Aw("aexp")
            inc("dtm", dve.tensor_tensor(decm, dt, a_ex.unsqueeze(1).to_broadcast([L, 2, H]), ALU.mult))
            Aw("dneg")
            inc("decm", dve.tensor_scalar(decm, dec, DECAY_MIN, None, ALU.max))
            V("decm")
            for i, w in enumerate((less, more)):
                inc(f"rhs{i}", dve.tensor_tensor(seg_rhs[i], w[:, :].unsqueeze(1).to_broadcast([L, H, L]),
                                                 bc(decm[:, i, :], [L, H, L]), ALU.mult))
            Tw("cb")
            inc("cb0", dve.tensor_tensor(cb[0], acc[0:L, 0:L], less[:, :], ALU.mult))
            inc("cb1", dve.tensor_tensor(cb[1], acc[0:L, L:2 * L], more[:, :], ALU.mult))
            Tw("xtok")
            inc("xtok", dve.tensor_copy(x_tok, bank_b[0:L, :]))
            Aw("zexp")
            inc("zc", dve.tensor_scalar(z_1, z_e, 1.0, None, ALU.add))
            V("zc")
            inc("ze1", dve.reciprocal(z_r, z_1))
            V("ze1")
            inc("zr", dve.tensor_tensor(gate, z_tok, z_r, ALU.mult))
            inc("gate", dve.memset(ygm[:, :], 0.0))
            for i in range(2):
                inc(f"cbd{i}", dve.tensor_tensor(cbh[i], cb[i].unsqueeze(1).to_broadcast([L, H, L]),
                                                 bc(dt[:, i, :], [L, H, L]), ALU.mult))
            V("cbd1")
            for i in range(2):
                Aw(f"dec{i}")
                inc(f"mix{i}", dve.tensor_tensor(dmix[i], dec_e[i], cbh[i], ALU.mult))
            V("mix1")
            inc("dsum", dve.tensor_tensor(dsum, dmix[0], dmix[1], ALU.add))
            Tw("fcd")
            inc("fcd", dve.tensor_tensor(fcd, bank_a[0:L, 0:H], Dw[:, :], ALU.add))
            V("fcd")
            inc("xf", dve.tensor_tensor(xf, x_tok.rearrange("p (h c) -> p h c", h=H), bc(fcd, [L, H, HD]), ALU.mult))
            V("xf")
            Tw("y")
            inc("y", dve.tensor_tensor(y_s, bank_c[0:L, :], xf.rearrange("p h c -> p (h c)"), ALU.add))
            V("y")
            inc("yg", dve.tensor_tensor(yg, y_s, gate, ALU.mult))
            V("yg")
            inc("ssq", dve.tensor_tensor_reduce(z_e, yg, yg, 1.0, 0.0, ALU.mult, ALU.add, ygs[:, :]))
            V("ssq")
            inc("mean", dve.tensor_scalar(ygm[:, :], ygs[:, :], 1.0 / INNER, 1e-5, ALU.mult, ALU.add))
            Aw("sqrt")
            inc("rms", dve.reciprocal(ygr[:, :], ygq[:, :]))
            V("rms")
            inc("ygn", dve.tensor_scalar(ygn, yg, ygr[:, 0:1], None, ALU.mult))
            V("ygn")
            inc("ygw", dve.tensor_tensor(ygw, ygn, norm_ww[:, :], ALU.mult))
            Tw("ygT")
            inc("ygTc", dve.tensor_copy(ygT, bank_b[:, 0:KC * L].rearrange("p (k l) -> p k l", k=KC)))
            Tw("ot")
            wait_step(dve, MIX_P, "bdz")
            src = bank_a[:, 0:KC * L].rearrange("p (k l) -> p k l", k=KC)
            inc("bd0", dve.tensor_copy(bd[0:HD, :, 0:G], src[0:HD]))
            inc("bd1", dve.tensor_copy(bd[HD:P, :, G:2 * G], src[HD:P]))
            Aw("mhi")
            inc("mlo", dve.tensor_tensor(m_lo[:, :], bank_c[:, :], m_hi[:, :], ALU.subtract))

            def rows_out(r, g=0):
                dve.wait_ge(nat_done, lin(r + 1, RING, g))
                if r >= 2:
                    dve.wait_ge(y_out[r % 2], lin(16 * (r // 2), 16 * RING // 2, g))
                dve.tensor_tensor(y_row[:, r % 2, :].rearrange("p (t d) -> p t d", t=T4),
                                  bank_a[:, :].rearrange("p (t d) -> p t d", t=T4),
                                  x1[:, bass.ds(lin(r * T4, RING * T4, g), T4), :], ALU.add).then_inc(y_done, 1)

            for r, n, m in LAST_BLOCKS[:RING]:
                rest(m, 0)
                rest(m, 1)
                if r:
                    rows_out(r - 1)
            with rounds(dve, BL // RING - 1) as g:
                for r, n, m in LAST_BLOCKS[RING:2 * RING]:
                    rest(m, 0, g)
                    rest(m, 1, g)
                    rows_out(r - 1, g)
            rows_out(BL - 1)

        @block.gpsimd
        def _(pool):
            pool.memset(ident[:, :], 0.0).then_inc(ident_ok, 1)
            pool.memset(ones[:, :], 1.0)
            pool.memset(m_hi[:, :].bitcast(F32), 0.0)
            pool.memset(half[:, :], -0.5).then_inc(ident_ok, 1)
            pool.memset(sw_sum[:, :], 0.0)
            pool.memset(less[:, :], 1.0)
            pool.memset(more[:, :], 1.0)
            pool.memset(conv_ws[:, :, :], 0.0)
            pool.memset(conv_bs[:, :], 0.0).then_inc(ident_ok, 1)
            pool.wait_ge(ident_ok, 3)
            pool.affine_select(out=less[:, :], in_=less[:, :], compare_op=ALU.is_gt, fill=0.0, base=0,
                               pattern=[[1, L]], channel_multiplier=-1)
            pool.affine_select(out=more[:, :], in_=more[:, :], compare_op=ALU.is_gt, fill=0.0, base=0,
                               pattern=[[-1, L]], channel_multiplier=1)
            pool.affine_select(out=ident[:, :], in_=ident[:, :], compare_op=ALU.not_equal, fill=1.0, base=0,
                               pattern=[[-1, P]], channel_multiplier=1).then_inc(ident_ok, 1)
            with nc.allow_non_contiguous_dma(reason="a few hundred parameters"):
                for dst, src in tiny:
                    pool.dma_start(dst, src).then_inc(tiny_in, 16)

            def slice_step(k, g=0):
                R2 = RING // 2
                q = k - 4
                if 0 <= q < TILES:
                    s3 = sw[:, q % 2, :].rearrange("p (h g) -> p h g", h=H)
                    pool.wait_ge(rd_done.sem, lin(rd_done.value("inv", q), 2 * R2, g))
                    if q >= 2:
                        pool.wait_ge(tt_done, lin(q - 1, R2, g))
                        pool.wait_ge(sw_out[q % 2], lin(16 * (q // 2), 16, g))
                    pool.tensor_tensor(s3, expd[:, q % 2, :].rearrange("p (h g) -> p h g", h=H),
                                       rden[:, q % 2, :].unsqueeze(2).to_broadcast([P, H, G]), ALU.mult)\
                        .then_inc(sw_done.sem, 1)
                    pool.wait_ge(sw_done.sem, lin(sw_done.value("weights", q), 2 * R2, g))
                    pool.dma_start(sw_dram[bass.ds(lin(q * P, R2 * P, g), P), :], sw[:, q % 2, :])\
                        .then_inc(sw_out[q % 2], 16)
                    pool.tensor_tensor(sw_sum[:, :], sw_sum[:, :], sw[:, q % 2, :], ALU.add).then_inc(sw_done.sem, 1)
                q = k + 2
                if 0 <= q < TILES:
                    ti = lin(q, R2, g)
                    pool.wait_ge(st_done.sem, lin(st_done.value("var", q), 7 * R2, g))
                    pool.tensor_tensor(rstd[:, bass.ds(ti, 1)], vareps[:, q % 2:q % 2 + 1], half[:, :], ALU.pow)\
                        .then_inc(rstd_done, 1)

            for k in (-2, -1):
                slice_step(k)
            for I, segs in second_plan:
                for seg in segs:
                    steps = [sliced(c.m) for c in seg.chunks]
                    steps = [k for k in steps if k is not None]
                    if steps:
                        with rounds(pool, seg.rounds) as g:
                            for k in steps:
                                slice_step(k, g)
            for k in range(TILES - 6, SLICE_LAST + 1):
                slice_step(k)
            pool.wait_ge(fin_v.sem, fin_v.value("x1", BL - 1))
            pool.memset(bd, 0.0).then_inc(MIX_P.sem, 1)


INPUTS = ["x", "adj", "L0_gnn_W", "L0_ffn_W_fx", "L0_ffn_b_fx", "L0_ffn_W_x", "L0_ffn_b_x", "L0_ffn_W_slice",
          "L0_ffn_b_slice", "L0_ffn_temperature", "L0_ffn_hy_in_w", "L0_ffn_hy_conv_w", "L0_ffn_hy_conv_b",
          "L0_ffn_hy_dt_bias", "L0_ffn_hy_A_log", "L0_ffn_hy_D", "L0_ffn_hy_fcD_w", "L0_ffn_hy_norm_w",
          "L0_ffn_hy_out_w", "L0_ffn_out_w", "L0_ffn_out_b"]


def kernel(**inputs):
    import numpy as np
    import concourse.bacc as bacc
    from concourse.bass_utils import run_bass_kernel_spmd

    nc = bacc.Bacc("TRN2", target_bir_lowering=False, num_devices=1)
    arrays, args = {}, []
    for name in INPUTS:
        a = np.ascontiguousarray(inputs[name])
        arrays[f"in_{name}"] = a
        args.append(nc.dram_tensor(f"in_{name}", a.shape, mybir.dt.from_np(a.dtype), kind="ExternalInput").ap())
    shape = tuple(inputs["x"].shape)
    out = nc.dram_tensor("out_x", shape, F32, kind="ExternalOutput").ap()
    gnn_slice_ffn(nc, *args, out)
    result = run_bass_kernel_spmd(nc, [arrays], core_ids=[0])
    return result.results[0]["out_x"]
```

```python
from collections import namedtuple
from contextlib import ExitStack, contextmanager

import concourse.bass as bass
from concourse import mybir

ALU = mybir.AluOpType
ACT = mybir.ActivationFunctionType
AX = mybir.AxisListType
F32 = mybir.dt.float32
F32R = mybir.dt.float32r

P = 128
D = 128
CH = 512
T4 = CH // P
RING = 4
H = 8
HD = 64
G = 64
HG = H * G
INNER = H * HD
NS = 64
CONV = INNER + 2 * NS
KW = 3
PROJ = 2 * INNER + 2 * NS + 2 * H
LN_EPS = 1e-5
EXP_MAX = 88.0
DECAY_MIN = -1.0e4

Chunk = namedtuple("Chunk", "n m J k last")
Seg = namedtuple("Seg", "rounds chunks")


class Steps:

    def __init__(self, sem, names):
        self.sem, self.names = sem, names.split()

    def value(self, name, rnd=0):
        return rnd * len(self.names) + self.names.index(name) + 1


def wait_step(eng, steps, name, rnd=0):
    eng.wait_ge(steps.sem, steps.value(name, rnd))


@contextmanager
def rounds(eng, count):
    if count == 1:
        yield 0
    else:
        with eng.Fori(0, count) as g:
            yield g


def spread(a, b):
    marks = [((i + 0.5) / len(a), 0, v) for i, v in enumerate(a)] + [((i + 0.5) / len(b), 1, v) for i, v in enumerate(b)]
    return [v for _, _, v in sorted(marks)]


def plan_first_reading(blocks):
    plan, n, m = [], 0, 0
    groups = blocks // RING
    for K in range(blocks):
        below, above = list(range(K)), list(range(K + 1, blocks))
        if K < RING:
            loop = above[RING:RING * (groups - 1)]
            parts = [spread(above[:RING], below), loop, above[RING * (groups - 1):] + [K]]
        elif K < RING * (groups - 1):
            parts = [spread(above, below) + [K]]
        else:
            loop = below[RING:RING * (groups - 1)]
            parts = [spread(above, below[:RING]), loop, below[RING * (groups - 1):] + [K]]
        segs, k = [], 0
        for part in parts:
            looped = len(parts) > 1 and part is parts[1]
            chunks = []
            for J in part[:RING] if looped else part:
                contracted = J <= K
                chunks.append(Chunk(n, m if contracted else None, J, k if contracted and not looped else None, J == K))
                n += 1
                m += contracted
                k += contracted
            count = len(part) // RING if looped else 1
            n += RING * (count - 1)
            m += RING * (count - 1) * (chunks[0].m is not None)
            segs.append(Seg(count, chunks))
        plan.append(segs)
    return plan, n, m


def plan_second_reading(blocks, n, m):
    plan = []
    for I in reversed(range(blocks - 1)):
        a, b = divmod(I, RING)
        segs = []
        straight = RING - 1 - b
        if straight:
            segs.append(Seg(1, [Chunk(n + i, m + i, I + 1 + i, i, False) for i in range(straight)]))
            n, m = n + straight, m + straight
        loops = blocks // RING - 1 - a
        parts = [loops] if straight else [1, loops - 1]
        if not I:
            parts = [loops - 1, 1]
        done = 0
        for k in parts:
            if k:
                segs.append(Seg(k, [Chunk(n + i, m + i, RING * (a + 1 + done) + i, i if not segs else None, False)
                                    for i in range(RING)]))
                n, m, done = n + RING * k, m + RING * k, done + k
        plan.append((I, segs))
    return plan, n, m


def gnn_slice_ffn(nc, x, adj, gnn_W, W_fx, b_fx, W_x, b_x, W_slice, b_slice, temperature, in_w, conv_w,
                  conv_b, dt_bias, A_log, Dp, fcD_w, norm_w, hy_out_w, out_w, out_b, out):
    N = x.shape[0]
    BL = N // CH
    TILES = N // P
    first_plan, n1, m1 = plan_first_reading(BL)
    second_plan, n2, m2 = plan_second_reading(BL, n1, m1)
    contracted_at = {}
    for segs in first_plan:
        for seg in segs:
            for r in range(seg.rounds):
                contracted_at.update((c.n + RING * r, c.m + RING * r) for c in seg.chunks if c.m is not None)
    n_at = {m: n for n, m in contracted_at.items()}
    n_at[m1] = n1
    assert n1 == BL * BL and n1 % RING == 0 and n2 % RING == 0 and m2 % 2 == 0
    SLICE_LAST = TILES + 4
    M0 = m1
    N0 = n1

    def sliced(m_base):
        i = m_base - M0
        k = i // 2
        return k if i > 0 and i % 2 == 1 and k <= TILES - 7 else None

    with ExitStack() as ctx:
        def sb(name, shape, dt=F32):
            return ctx.enter_context(nc.sbuf_tensor(name, shape, dt))

        def psum(name, shape):
            return ctx.enter_context(nc.psum_tensor(name, shape, F32))

        def sem(name):
            return ctx.enter_context(nc.semaphore(name))

        turned = [psum(f"turned{i}", [P, 2 * CH]) for i in range(2)]
        acc = psum("acc", [P, CH])
        bank_a = psum("bank_a", [P, CH])
        bank_b = psum("bank_b", [P, CH])
        bank_c = psum("bank_c", [P, CH])

        a_ring = sb("a_ring", [P, RING, T4, CH])
        hi = sb("hi", [P, 4, 2 * CH], F32R)
        lo = sb("lo", [P, 4, 2 * CH], F32R)
        sup = sb("sup", [P, TILES, D])
        rows = sb("rows", [P, BL, CH])
        x1 = rows[:, :, :].rearrange("p b (t d) -> p (b t) d", d=D)
        s_hi = sb("s_hi", [P, 2, CH], F32R)
        s_lo = sb("s_lo", [P, 2, CH], F32R)
        m_hi = sb("m_hi", [P, CH], F32R)
        m_lo = sb("m_lo", [P, CH], F32R)
        x_in = sb("x_in", [P, 2, T4, D])
        lnx = sb("lnx", [P, T4, D])
        lnxT = sb("lnxT", [P, CH])
        logit = sb("logit", [P, 2, HG])
        expd = sb("expd", [P, 2, HG])
        sw = sb("sw", [P, 2, HG])
        w_raw = sw
        in_wT = sb("in_wT", [P, INNER // P, PROJ])
        hy_outT = sb("hy_outT", [P, INNER // P, INNER])
        W_fxT = sb("W_fxT", [P, INNER])
        out_wT = sb("out_wT", [P, INNER // P, D])
        fcD_T = sb("fcD_T", [P, INNER // P, H])
        gnn_WT = sb("gnn_WT", [P, D])
        W_logT = sb("W_logT", [P, HG])
        b_log = sb("b_log", [P, HG])
        ident = sb("ident", [P, P])
        ones = sb("ones", [P, 1])
        row_st = lnxT
        nat = lnx
        part = sb("part", [P, T4, BL])
        rsum = sb("rsum", [P, T4])
        rsq = sb("rsq", [P, T4])
        dcol = sb("dcol", [P, TILES])
        bn = sb("bn", [P, T4, 6])
        mv = sb("mv", [P, T4, 2])
        sd = sb("sd", [P, T4])
        rstd4 = sb("rstd4", [P, T4])
        stat = sb("stat", [P, 2, 6])
        both_st = sb("both_st", [P, 2])
        gap = sb("gap", [P, 1])
        within = sb("within", [P, 1])
        vareps = sb("vareps", [P, 2])
        mean = sb("mean", [P, TILES])
        rstd = sb("rstd", [P, TILES])
        half = sb("half", [P, 1])
        xns = sb("xns", [P, 6, D])
        xn_a, xn_b, xnT = xns[:, 0:2, :], xns[:, 2:4, :], xns[:, 4:6, :]
        junk = xns[:, 0:4, :].rearrange("p a d -> p (a d)").bitcast(mybir.dt.bfloat16)
        mx = sb("mx", [P, H])
        den = sb("den", [P, H])
        rden = sb("rden", [P, 2, H])
        sw_sum = sb("sw_sum", [P, HG])
        temp = sb("temp", [P, H])
        rtemp = sb("rtemp", [P, H])
        bsl = sb("bsl", [P, G])
        out_bc = sb("out_bc", [P, 1])

        sw_dram = nc.dram_tensor("sw_dram", [N, HG], F32, kind="Internal").ap()

        a_in = [sem(f"a_in{i}") for i in range(RING)]
        act_sum = sem("act_sum")
        dve_sum = sem("dve_sum")
        t_done = sem("t_done")
        hi_done = sem("hi_done")
        lo_done = sem("lo_done")
        sh_done = sem("sh_done")
        sl_done = sem("sl_done")
        mm_done = sem("mm_done")
        row_done = sem("row_done")
        ident_ok = sem("ident_ok")
        setup_in = sem("setup_in")
        tiny_in = sem("tiny_in")
        logits_in = sem("logits_in")
        x_landed = [sem(f"x_landed{i}") for i in range(2)]
        w_landed = [sem(f"w_landed{i}") for i in range(2)]
        c_filled = sem("c_filled")
        c_copied = sem("c_copied")
        prep_v = Steps(sem("prep_v"), "stats aggr eps rstd norm")
        prep_a = Steps(sem("prep_a"), "sqrt")
        prep_t = Steps(sem("prep_t"), "support")
        deg_v = Steps(sem("deg_v"), "rows one inv scaled")
        deg_a = Steps(sem("deg_a"), "sqrt")
        fin_v = Steps(sem("fin_v"), "add relu x1")
        fin_t = Steps(sem("fin_t"), "turned")
        fin_sums = sem("fin_sums")
        st_done = Steps(sem("st_done"), "stats sum gap mean within half var")
        rstd_done = sem("rstd_done")
        xa_done = sem("xa_done")
        xt_done = sem("xt_done")
        xtc_done = sem("xtc_done")
        lg_done = sem("lg_done")
        sm_done = Steps(sem("sm_done"), "bias max shift")
        exp_done = sem("exp_done")
        rd_done = Steps(sem("rd_done"), "sum inv")
        xb_done = sem("xb_done")
        sw_done = Steps(sem("sw_done"), "weights total")
        sw_out = [sem(f"sw_out{i}") for i in range(2)]
        tt_done = sem("tt_done")

        set_v = Steps(sem("set_v"), "tmax tinv bx_wide wslT wlog blog_sum blog")
        set_t = Steps(sem("set_t"), "wslT wlog blog")

        conv_v = sem("conv_v")
        units = [("in", in_w[r * P:min((r + 1) * P, PROJ), :], min(P, PROJ - r * P),
                  in_wT[:, :, r * P:min((r + 1) * P, PROJ)]) for r in range(-(-PROJ // P))]
        units += [("ho", hy_out_w[r * P:(r + 1) * P, :], P, hy_outT[:, :, r * P:(r + 1) * P])
                  for r in range(INNER // P)]
        units += [("fx", W_fx.rearrange("(t p) d -> p t d", p=P), P, W_fxT[:, :].rearrange("p (t d) -> p t d", t=T4))]
        units += [("ow", out_w[:, :], P, out_wT[:, :, :])]
        units += [("fd", fcD_w[:, :], H, fcD_T[:, :, :])]
        PER = 2
        FIRST_UNITS = RING
        unit_block = {u: FIRST_UNITS + u // PER for u in range(len(units))}
        c_uses = ["g", ("x", 0)]
        for K in range(BL):
            if K + 1 < BL:
                c_uses.append(("x", K + 1))
            c_uses += [("w", u) for u in unit_block if unit_block[u] == K]

        def c_use(u):
            return c_uses.index(u)

        w_sl = lnx[0:G, 0, 0:HD]
        w_slT = lnx[0:HD, 2, 0:G]
        w_x_c = expd[0:HD, :, :].rearrange("c a (h d) -> c (a h) d", d=D)
        b_xT = sb("b_xT", [HD, H])
        b_x_wide = logit[0:HD, :, :].rearrange("c a (h d) -> c (a h) d", d=P)

        supf = sup[:, :, :].rearrange("p t d -> p (t d)")
        regions = [[ap, 0, size] for ap, size in (
            (supf, TILES * D), (logit[:, :, :].rearrange("p a g -> p (a g)"), 2 * HG),
            (expd[:, :, :].rearrange("p a g -> p (a g)"), 2 * HG))]

        def tmp(parts, *shape):
            size = 1
            for k in shape:
                size *= k
            region = next(r for r in regions if r[1] + size <= r[2])
            ap = region[0][0:parts, region[1]:region[1] + size]
            region[1] += size
            if len(shape) == 2:
                ap = ap.rearrange("p (a b) -> p a b", b=shape[1])
            return ap

        L = G
        KC = INNER // P
        TTs = tmp(P, HG)
        snorm = tmp(L, H)
        snorm_e = tmp(L, H)
        rsnorm = tmp(L, H)
        b_fx_w = sb("b_fx_w", [L, INNER])
        norm_ww = sb("norm_ww", [L, INNER])
        st_b = tmp(L, H, HD)
        st_s = st_b
        u_tok = tmp(L, INNER)
        uT = tmp(P, KC, L)
        z_tok = tmp(L, INNER)
        z_e = tmp(L, INNER)
        z_1 = z_r = z_e
        gate = tmp(L, INNER)
        CK = KC + 2
        cpad = tmp(P, CK, L + 2)
        cva = tmp(P, CK, L)
        cvb = tmp(P, CK, L)
        cvc = tmp(P, CK, L)
        cve = tmp(P, CK, L)
        cvr = cve
        xT = tmp(P, CK, L)
        conv_ws = sb("conv_ws", [P, CK, KW])
        conv_bs = sb("conv_bs", [P, CK])
        Cpad = tmp(NS, L + 2)
        x_tok = tmp(L, INNER)
        dtr = tmp(L, 2, H)
        dta = tmp(L, 2, H)
        dtb = tmp(L, 2, H)
        dtc = tmp(L, 2, H)
        dtd = tmp(L, 2, H)
        dtm = tmp(L, 2, H)
        dt = tmp(L, 2, H)
        dec = tmp(L, 2, H)
        decm = tmp(L, 2, H)
        dt_bw = sb("dt_bw", [L, H])
        a_lw = sb("a_lw", [L, H])
        a_cl = tmp(L, H)
        a_ex = tmp(L, H)
        Dw = sb("Dw", [L, H])
        seg_rhs = [tmp(L, H, L) for _ in range(2)]
        dec_e = [tmp(L, H, L) for _ in range(2)]
        cb = [tmp(L, L) for _ in range(2)]
        cbh = [tmp(L, H, L) for _ in range(2)]
        dmix = dec_e
        dsum = dec_e[0]
        fcd = tmp(L, H)
        xf = u_tok.rearrange("p (h c) -> p h c", h=H)
        y_s = z_tok
        yg = ygn = ygw = y_s
        ygs = sb("ygs", [L, 1])
        ygm = sb("ygm", [L, 1])
        ygq = sb("ygq", [L, 1])
        ygr = sb("ygr", [L, 1])
        ygT = tmp(P, KC, L)
        bd = lnxT[:, :].rearrange("p (k d) -> p k d", k=KC)
        less = sb("less", [L, L])
        more = sb("more", [L, L])
        MIX_V = Steps(sem("mix_v"), "snorm snorm_e rsnorm st_b st_s u uTc gpad C0 C1 xpad bpad c0 c1 c2 cb "
                      "ce1 cr xT Cp dt_add dt_abs dt_one dt_max dt dtm decm "
                      "rhs0 rhs1 cb0 cb1 xtok zc ze1 zr gate cbd0 cbd1 mix0 mix1 dsum fcd xf y yg ssq mean rms "
                      "ygn ygw ygTc bd0 bd1 mlo")
        MIX_A = Steps(sem("mix_a"), "TT u_z cexp zexp dexp dln aexp dneg dec0 dec1 sqrt mhi")
        MIX_T = Steps(sem("mix_t"), "snorm st uT z xbc bc dt cb xtok seg0 seg1 fcd y ygT ot M")
        MIX_P = Steps(sem("mix_p"), "bdz")
        ot_done = sem("ot_done")
        nat_done = sem("nat_done")
        y_done = sem("y_done")
        y_out = [sem(f"y_out{i}") for i in range(2)]
        o_col = logit
        y_row = expd

        def lin(base, step, g):
            return base + step * g

        a_rows = adj.rearrange("(b t p) c -> b p t c", p=P, t=T4)
        x_rows = x.rearrange("(b t p) d -> b p t d", p=P, t=T4)
        sw_rows = sw_dram.rearrange("(b t p) c -> b p t c", p=P, t=T4)
        out_rows = out.rearrange("(b t p) d -> b p t d", p=P, t=T4)
        LAST_BLOCKS = [(r, n2 + r, m2 + r) for r in range(BL)]

        fin_m = [m1] + [segs[-1].chunks[-1].m + RING * (segs[-1].rounds - 1) + 1 for _, segs in second_plan]
        fin_xt = [sum(1 for m in range(m1, fm) if sliced(m) is not None) for fm in fin_m]

        def wide(vec, parts):
            return vec.partition_broadcast(parts)

        tiny = [
            (temp[:, :], wide(temperature.rearrange("a h b c -> (a h b c)"), P)),
            (b_xT[:, :], b_x.rearrange("(h c) -> c h", c=HD)),
            (bsl[:, :], wide(b_slice, P)),
            (out_bc[:, :], out_b.rearrange("(p a) -> p a", a=1)),
            (b_fx_w[:, :], wide(b_fx, L)),
            (norm_ww[:, :], wide(norm_w, L)),
            (dt_bw[:, :], wide(dt_bias, L)),
            (a_lw[:, :], wide(A_log, L)),
            (Dw[:, :], wide(Dp, L)),
            (conv_ws[:, 0:KC, :], conv_w[0:INNER, :].rearrange("(k p) w -> p k w", p=P)),
            (conv_ws[0:NS, KC:CK, :], conv_w[INNER:CONV, :].rearrange("(k p) w -> p k w", p=NS)),
            (conv_bs[:, 0:KC], conv_b[0:INNER].rearrange("(k p) -> p k", p=P)),
            (conv_bs[0:NS, KC:CK], conv_b[INNER:CONV].rearrange("(k p) -> p k", p=NS)),
        ]
        TINY_FIRST = 3
        TINY = 16 * (len(tiny) - TINY_FIRST)

        block = ctx.enter_context(nc.Block())

        @block.sync
        def _(sp):
            def load_x(i):
                b = i if i < BL else 2 * BL - 1 - i
                if 2 <= i < BL + 2:
                    wait_step(sp, prep_v, "norm", i - 2)
                if i >= BL + 2:
                    wait_step(sp, fin_v, "x1", i - BL - 2)
                sp.dma_start(x_in[:, i % 2], x_rows[b]).then_inc(x_landed[i % 2], 16)

            def load_w(u):
                kind, src, k, _ = units[u]
                if u >= 2:
                    sp.wait_ge(c_filled, c_use(("w", u - 2)) + 1)
                dst = w_raw[0:k, u % 2, :]
                if kind == "fx":
                    dst = dst.rearrange("p (t d) -> p t d", t=T4)
                sp.dma_start(dst, src).then_inc(w_landed[u % 2], 16)

            sp.dma_start(lnx[:, 1, :], gnn_W).then_inc(setup_in, 16)
            sp.dma_start(w_sl, W_slice).then_inc(setup_in, 16)
            sp.dma_start(w_x_c, W_x.rearrange("(h c) d -> c h d", c=HD)).then_inc(setup_in, 16)
            load_x(0)
            with nc.allow_non_contiguous_dma(reason="512 biases, turned"):
                for dst, src in tiny[:TINY_FIRST]:
                    sp.dma_start(dst, src).then_inc(logits_in, 16)

            def load(n, slot, K, J):
                sp.dma_start(a_ring[:, slot], a_rows[K][:, :, bass.ds(J * CH, CH)]).then_inc(a_in[slot], 16)

            for K, segs in enumerate(first_plan):
                if K + 1 < BL:
                    load_x(K + 1)
                for u in unit_block:
                    if unit_block[u] == K:
                        load_w(u)
                for seg in segs:
                    with rounds(sp, seg.rounds) as g:
                        for c in seg.chunks:
                            old = c.n - RING
                            if old in contracted_at:
                                sp.wait_ge(lo_done, 2 * (contracted_at[old] + 1))
                            elif old >= 0:
                                sp.wait_ge(act_sum, old + 1)
                                sp.wait_ge(dve_sum, old + 1)
                            if seg.rounds > 1:
                                if c.m is not None:
                                    sp.wait_ge(lo_done, lin(2 * (c.m - RING + 1), 2 * RING, g))
                                else:
                                    sp.wait_ge(act_sum, lin(old + 1, RING, g))
                                    sp.wait_ge(dve_sum, lin(old + 1, RING, g))
                            load(c.n, c.n % RING, K, lin(c.J, RING, g))

            load_x(BL)
            for I, segs in second_plan:
                load_x(2 * BL - 1 - I)
                for seg in segs:
                    with rounds(sp, seg.rounds) as g:
                        for c in seg.chunks:
                            if c.n < N0 + RING:
                                sp.wait_ge(act_sum, c.n - RING + 1)
                                sp.wait_ge(dve_sum, c.n - RING + 1)
                            sp.wait_ge(t_done, lin(2 * (c.m - RING + 1), 2 * RING, g))
                            load(c.n, c.n % RING, I, lin(c.J, RING, g))

            for i in range(2):
                sp.wait_ge(sw_out[i], 16 * (TILES // 2))

            def load_sw(r, n, m, g=0):
                sp.wait_ge(t_done, lin(2 * (m - RING + 1), 2 * RING, g))
                sp.dma_start(a_ring[:, n % RING], sw_rows[r + RING * g]).then_inc(a_in[n % RING], 16)

            def store_y(r, g=0):
                sp.wait_ge(y_done, lin(r + 1, RING, g))
                sp.dma_start(out_rows[g * -RING + (BL - 1 - r)], y_row[:, r % 2, :].rearrange("p (t d) -> p t d", t=T4))\
                    .then_inc(y_out[r % 2], 16)

            for r, n, m in LAST_BLOCKS[:RING]:
                load_sw(r, n, m)
            with rounds(sp, BL // RING - 1) as g:
                for r, n, m in LAST_BLOCKS[RING:2 * RING]:
                    store_y(r - RING, g)
                    load_sw(r, n, m, g)
            for r in range(BL - RING, BL):
                store_y(r)
            for i in range(2):
                sp.wait_ge(y_out[i], 16 * (BL // 2))

        @block.tensor
        def _(pe):
            def turn(n, m, h, g=0):
                if h == 0:
                    pe.wait_ge(a_in[n % RING], lin(16 * (n // RING + 1), 16, g))
                if m >= 1:
                    pe.wait_ge(lo_done, lin(2 * (m - 1) + h + 1, 2 * RING, g))
                for s in range(2):
                    for t in range(T4):
                        at = s * CH + t * P
                        col = (2 * h + s) * P
                        ins = pe.transpose(turned[h][:, at:at + P], a_ring[:, n % RING, t, col:col + P], ident[:, :])
                ins.then_inc(t_done, 1)

            def contract(m, h, first, last, g=0, stat_hi=None, stat_lo=None, into=acc):
                pe.wait_ge(lo_done, lin(2 * m + h + 1, 2 * RING, g))
                slot = 2 * (m % 2) + h
                sh = s_hi[:, m % 2] if stat_hi is None else stat_hi
                sl = s_lo[:, m % 2] if stat_lo is None else stat_lo
                for s in range(2):
                    col = (2 * h + s) * P
                    mov_hi = hi[:, slot, s * CH:(s + 1) * CH]
                    mov_lo = lo[:, slot, s * CH:(s + 1) * CH]
                    opens = first and h == 0 and s == 0
                    closes = last and h == 1 and s == 1
                    pe.matmul(into[:, :], sh[:, col:col + P], mov_hi, start=opens, stop=False, skip_group_check=True)
                    pe.matmul(into[:, :], sh[:, col:col + P], mov_lo, start=False, stop=False, skip_group_check=True)
                    ins = pe.matmul(into[:, :], sl[:, col:col + P], mov_hi, start=False, stop=closes,
                                    skip_group_check=True)
                ins.then_inc(mm_done, 1)

            def chunk_sums(c, last, n_next, g=0):
                for h in range(2):
                    if n_next is not None:
                        turn(n_next, c.m + 1, h, g)
                    if h == 0:
                        pe.wait_ge(sl_done, lin(c.m + 1, RING, g))
                    contract(c.m, h, c.k == 0, last, g)

            def weights_turned(use, src, k, cols):
                if use >= 1:
                    pe.wait_ge(c_copied, use)
                for t in range(T4):
                    ins = pe.transpose(bank_c[0:cols, t * P:t * P + k], src(t), ident[0:k, 0:k])
                ins.then_inc(c_filled, 1)

            def turn_x(K):
                wait_step(pe, prep_v, "norm", K)
                weights_turned(c_use(("x", K)), lambda t: lnx[:, t, :], P, P)

            def support(K):
                pe.wait_ge(c_copied, c_use(("x", K)) + 1)
                if K >= 2:
                    wait_step(pe, deg_v, "scaled", K - 2)
                bank = (bank_a, bank_b)[K % 2]
                for t in range(T4):
                    ins = pe.matmul(bank[:, t * D:(t + 1) * D], lnxT[:, t * P:(t + 1) * P], gnn_WT[:, :],
                                    start=True, stop=True)
                ins.then_inc(prep_t.sem, 1)

            pe.wait_ge(ident_ok, 4)
            pe.wait_ge(setup_in, 48)
            pe.transpose(bank_c[:, 0:P], lnx[:, 1, :], ident[:, :]).then_inc(c_filled, 1)
            pe.transpose(bank_a[0:HD, 0:G], w_sl, ident[0:G, 0:G]).then_inc(set_t.sem, 1)
            wait_step(pe, set_v, "wslT")
            for h in range(H):
                ins = pe.matmul(bank_a[:, h * G:(h + 1) * G], w_x_c[:, h, :], w_slT, start=True, stop=True)
            ins.then_inc(set_t.sem, 1)
            for h in range(H):
                ins = pe.matmul(bank_b[:, h * G:(h + 1) * G], b_x_wide[:, h, :], w_slT, start=True, stop=True)
            ins.then_inc(set_t.sem, 1)
            wait_step(pe, set_v, "blog")
            def turn_weights(K, i):
                u = PER * (K - FIRST_UNITS) + i
                if 0 <= u and u in unit_block and unit_block[u] == K:
                    k = units[u][2]
                    pe.wait_ge(w_landed[u % 2], 16 * (u // 2 + 1))
                    weights_turned(c_use(("w", u)), lambda t: w_raw[0:k, u % 2, t * P:(t + 1) * P], k, P)

            turn_x(0)
            support(0)
            turn_x(1)
            support(1)
            for h in range(2):
                turn(n_at[0], 0, h)
            for K, segs in enumerate(first_plan):
                for seg in segs:
                    with rounds(pe, seg.rounds) as g:
                        for c in seg.chunks:
                            if c.m is None:
                                continue
                            if c.k == 0 and K >= 1:
                                pe.wait_ge(row_done, K)
                            chunk_sums(c, c.last, n_at[c.m + 1], g)
                            if c.k == 0 and 1 <= K < BL - 1:
                                turn_x(K + 1)
                            if c.k == 1 and K < BL - 1:
                                support(K + 1)
                            if c.k in (1, 2):
                                turn_weights(K, c.k - 1)

            def finish(f):
                pe.wait_ge(fin_sums, f + 1)
                if f == 0:
                    wait_step(pe, deg_v, "scaled", BL - 1)
                else:
                    wait_step(pe, fin_v, "add", f - 1)
                    if fin_xt[f]:
                        pe.wait_ge(xtc_done, fin_xt[f])
                for t in range(T4):
                    ins = pe.transpose(bank_a[:, t * D:(t + 1) * D], row_st[:, t * P:(t + 1) * P], ident[:, :])
                ins.then_inc(fin_t.sem, 1)

            def slice_step(k, fins, g=0):
                R2 = RING // 2
                if 0 <= k < TILES:
                    pe.wait_ge(xa_done, lin(k + 1, R2, g))
                    wait_step(pe, fin_v, "add", fins - 1)
                    if k >= 1:
                        pe.wait_ge(xtc_done, lin(k, R2, g))
                    pe.transpose(bank_a[:, 0:P], xn_a[:, k % 2, :], ident[:, :]).then_inc(xt_done, 1)
                q = k - 1
                if 0 <= q < TILES:
                    if q >= 1:
                        pe.wait_ge(sm_done.sem, lin(sm_done.value("bias", q - 1), 3 * R2, g))
                    pe.wait_ge(xtc_done, lin(q + 1, R2, g))
                    pe.matmul(bank_c[:, :], xnT[:, q % 2, :], W_logT[:, :], start=True, stop=True).then_inc(lg_done, 1)
                q = k - 5
                if 0 <= q < TILES:
                    pe.wait_ge(sw_done.sem, lin(sw_done.value("weights", q), 2 * R2, g))
                    pe.wait_ge(xb_done, lin(q + 1, R2, g))
                    pe.matmul(bank_b[:, :], xn_b[:, q % 2, :], sw[:, q % 2, :], start=(q == 0), stop=(q == TILES - 1),
                              skip_group_check=True).then_inc(tt_done, 1)

            fins = 0
            for I, segs in second_plan:
                if fins == 0:
                    pe.wait_ge(row_done, BL)
                finish(fins)
                fins += 1
                if fins == 1:
                    for k in (-2, -1):
                        slice_step(k, fins)
                for i, seg in enumerate(segs):
                    with rounds(pe, seg.rounds) as g:
                        for j, c in enumerate(seg.chunks):
                            last = i == len(segs) - 1 and j == len(seg.chunks) - 1
                            chunk_sums(c, last, None if last and I == 0 else c.n + 1, g)
                            k = sliced(c.m)
                            if k is not None:
                                slice_step(k, fins, g)
            finish(fins)
            fins += 1
            for k in range(TILES - 6, SLICE_LAST + 1):
                slice_step(k, fins)

            def T_(name, rnd=0):
                return wait_step(pe, MIX_T, name)

            def inc(ins):
                ins.then_inc(MIX_T.sem, 1)

            pe.wait_ge(tt_done, TILES)
            wait_step(pe, sw_done, "total", TILES - 1)
            for h in range(H):
                ins = pe.matmul(bank_a[0:G, h:h + 1], sw_sum[:, h * G:(h + 1) * G], ones[:, 0:1], start=True, stop=True)
            inc(ins)
            wait_step(pe, MIX_A, "TT")
            for h in range(H):
                ins = pe.matmul(bank_c[0:G, h * HD:(h + 1) * HD], TTs[:, h * G:(h + 1) * G],
                                W_fxT[:, h * HD:(h + 1) * HD], start=True, stop=True)
            inc(ins)
            wait_step(pe, MIX_V, "u")
            for c in range(KC):
                ins = pe.transpose(bank_b[:, c * L:(c + 1) * L], u_tok[:, c * P:(c + 1) * P], ident[0:L, 0:L])
            inc(ins)
            wait_step(pe, MIX_V, "uTc")
            for c in range(KC):
                ins = pe.matmul(bank_c[0:L, :], uT[:, c, :], in_wT[:, c, 0:INNER], start=(c == 0), stop=(c == KC - 1))
            inc(ins)
            for k in range(KC):
                for c in range(KC):
                    ins = pe.matmul(bank_b[:, k * L:(k + 1) * L], in_wT[:, c, INNER + k * P:INNER + (k + 1) * P],
                                    uT[:, c, :], start=(c == 0), stop=(c == KC - 1))
            inc(ins)
            for k in range(2):
                for c in range(KC):
                    w0 = 2 * INNER + k * NS
                    ins = pe.matmul(acc[0:NS, k * L:(k + 1) * L], in_wT[:, c, w0:w0 + NS],
                                    uT[:, c, :], start=(c == 0), stop=(c == KC - 1))
            inc(ins)
            for c in range(KC):
                ins = pe.matmul(bank_a[0:L, 0:2 * H], uT[:, c, :], in_wT[:, c, PROJ - 2 * H:PROJ],
                                start=(c == 0), stop=(c == KC - 1))
            inc(ins)
            wait_step(pe, MIX_V, "Cp")
            for i, at in ((0, 0), (1, 2)):
                ins = pe.matmul(acc[0:L, i * L:(i + 1) * L], xT[0:NS, KC, :], Cpad[:, at:at + L], start=True, stop=True)
            inc(ins)
            for c in range(KC):
                ins = pe.transpose(bank_b[0:L, c * P:(c + 1) * P], xT[:, c, :], ident[:, :])
            inc(ins)
            for i, (w, name) in enumerate(((more, "rhs0"), (less, "rhs1"))):
                wait_step(pe, MIX_V, name)
                inc(pe.matmul(turned[i][0:L, 0:H * L], w[:, :], seg_rhs[i].rearrange("p a b -> p (a b)"),
                              start=True, stop=True))
            wait_step(pe, MIX_V, "dt_add")
            for c in range(KC):
                ins = pe.matmul(bank_a[0:L, 0:H], xT[:, c, :], fcD_T[:, c, :], start=(c == 0), stop=(c == KC - 1))
            inc(ins)
            wait_step(pe, MIX_V, "dsum")
            for h in range(H):
                ins = pe.matmul(bank_c[0:L, h * HD:(h + 1) * HD], dsum[:, h, :], x_tok[:, h * HD:(h + 1) * HD],
                                start=True, stop=True)
            inc(ins)
            wait_step(pe, MIX_V, "ygw")
            for c in range(KC):
                ins = pe.transpose(bank_b[:, c * L:(c + 1) * L], ygw[:, c * P:(c + 1) * P], ident[0:L, 0:L])
            inc(ins)
            wait_step(pe, MIX_V, "ygTc")
            for k in range(KC):
                for c in range(KC):
                    ins = pe.matmul(bank_a[:, k * L:(k + 1) * L], hy_outT[:, c, k * P:(k + 1) * P], ygT[:, c, :],
                                    start=(c == 0), stop=(c == KC - 1))
            inc(ins)
            wait_step(pe, MIX_V, "bd1")
            for k in range(KC):
                ins = pe.matmul(bank_c[:, k * D:(k + 1) * D], bd[:, k, :], out_wT[:, k, :], start=True, stop=True)
            inc(ins)

            def back(r, g=0):
                pe.wait_ge(ot_done, lin(r + 1, RING, g))
                if r >= 1:
                    pe.wait_ge(y_done, lin(r, RING, g))
                for t in range(T4):
                    ins = pe.transpose(bank_a[:, t * D:(t + 1) * D], o_col[:, r % 2, t * P:(t + 1) * P], ident[:, :])
                ins.then_inc(nat_done, 1)

            def last_block(r, n, m, g=0, final=False, start=False):
                for h in range(2):
                    if not final:
                        turn(n + 1, m + 1, h, g)
                    if h == 0 and r >= 2:
                        pe.wait_ge(ot_done, lin(r - 1, RING, g))
                    contract(m, h, True, True, g, m_hi, m_lo, into=(acc, bank_c)[r % 2])
                if not start:
                    back(r - 1, g)

            turn(n2, m2, 0)
            turn(n2, m2, 1)
            wait_step(pe, MIX_V, "mlo")
            for r, n, m in LAST_BLOCKS[:RING]:
                last_block(r, n, m, start=(r == 0))
            with rounds(pe, BL // RING - 2) as g:
                for r, n, m in LAST_BLOCKS[RING:2 * RING]:
                    last_block(r, n, m, g)
            for r, n, m in LAST_BLOCKS[BL - RING:]:
                last_block(r, n, m, final=(r == BL - 1))
            back(BL - 1)

        @block.scalar
        def _(act):
            def high(m, h, g=0):
                act.wait_ge(t_done, lin(2 * m + h + 1, 2 * RING, g))
                if m >= 2:
                    act.wait_ge(mm_done, lin(2 * (m - 2) + h + 1, 2 * RING, g))
                act.activation(hi[:, 2 * (m % 2) + h, :], turned[h][:, :], ACT.Copy).then_inc(hi_done, 1)

            def support_high(c, g=0):
                if c.m >= 2:
                    act.wait_ge(mm_done, lin(2 * (c.m - 1), 2 * RING, g))
                act.activation(s_hi[:, c.m % 2, :], supf[:, bass.ds(lin(c.J, RING, g) * CH, CH)], ACT.Copy)\
                    .then_inc(sh_done, 1)

            def row_sums(c, g=0):
                act.wait_ge(a_in[c.n % RING], lin(16 * (c.n // RING + 1), 16, g))
                if c.n >= 1:
                    act.wait_ge(act_sum, lin(c.n, RING, g))
                for t in range(2):
                    ins = act.activation(junk[:, t * CH:(t + 1) * CH], a_ring[:, c.n % RING, t, :], ACT.Copy,
                                         accum_out=part[:, t, bass.ds(lin(c.J, RING, g), 1)])
                ins.then_inc(act_sum, 1)

            def copy_c(use, dst, src):
                act.wait_ge(c_filled, use + 1)
                act.activation(dst, src, ACT.Copy).then_inc(c_copied, 1)

            def norm_root(K):
                wait_step(act, prep_v, "eps", K)
                act.activation(sd[:, :], mv[:, :, 1], ACT.Sqrt).then_inc(prep_a.sem, 1)

            def copy_x(K):
                if K >= 1:
                    wait_step(act, prep_t, "support", K - 1)
                copy_c(c_use(("x", K)), lnxT[:, :], bank_c[:, :])

            def copy_weights(K, i):
                u = PER * (K - FIRST_UNITS) + i
                if 0 <= u and u in unit_block and unit_block[u] == K:
                    k, dst = units[u][2], units[u][3]
                    copy_c(c_use(("w", u)), dst, bank_c[:, :].rearrange("p (t k) -> p t k", t=T4)[:, :, 0:k])

            def save_sums(K):
                act.wait_ge(mm_done, 2 * (first_plan[K][-1].chunks[-1].m + 1))
                act.activation(rows[:, BL - 1 - K, :], acc[:, :], ACT.Copy).then_inc(row_done, 1)

            copy_c(0, gnn_WT[:, :], bank_c[:, 0:P])
            norm_root(0)
            copy_x(0)
            for K, segs in enumerate(first_plan):
                if K + 1 < BL:
                    norm_root(K + 1)
                    if K == 0:
                        copy_x(1)
                for seg in segs:
                    with rounds(act, seg.rounds) as g:
                        for c in seg.chunks:
                            row_sums(c, g)
                            if c.m is None:
                                continue
                            if c.last:
                                wait_step(act, deg_v, "one", K)
                                act.activation(rsq[:, :], rsum[:, :], ACT.Sqrt).then_inc(deg_a.sem, 1)
                                high(c.m, 0, g)
                                wait_step(act, deg_v, "scaled", K)
                                support_high(c, g)
                                high(c.m, 1, g)
                            else:
                                support_high(c, g)
                                high(c.m, 0, g)
                                high(c.m, 1, g)
                            if c.k == 0 and K >= 1:
                                save_sums(K - 1)
                            if c.k == 1 and K < BL - 1:
                                copy_x(K + 1)
                            if c.k in (2, 3):
                                copy_weights(K, c.k - 2)

            def slice_step(k, g=0):
                R2 = RING // 2
                if 0 <= k < TILES:
                    act.wait_ge(xt_done, lin(k + 1, R2, g))
                    if k >= 2:
                        act.wait_ge(lg_done, lin(k - 1, R2, g))
                    act.activation(xnT[:, k % 2, :], bank_a[:, 0:P], ACT.Copy).then_inc(xtc_done, 1)
                q = k - 2
                if 0 <= q < TILES:
                    act.wait_ge(sm_done.sem, lin(sm_done.value("shift", q), 3 * R2, g))
                    if q >= 2:
                        act.wait_ge(sw_done.sem, lin(sw_done.value("weights", q - 2), 2 * R2, g))
                    act.activation(expd[:, q % 2, :], logit[:, q % 2, :], ACT.Exp).then_inc(exp_done, 1)

            for k in (-2, -1):
                slice_step(k)
            for I, segs in second_plan:
                for seg in segs:
                    with rounds(act, seg.rounds) as g:
                        for c in seg.chunks:
                            support_high(c, g)
                            high(c.m, 0, g)
                            high(c.m, 1, g)
                            if c.m == M0:
                                save_sums(BL - 1)
                            k = sliced(c.m - 1)
                            if k is not None:
                                slice_step(k, g)
            for k in range(TILES - 6, SLICE_LAST + 1):
                slice_step(k)

            def inc(ins):
                ins.then_inc(MIX_A.sem, 1)

            act.wait_ge(tt_done, TILES)
            inc(act.activation(TTs, bank_b[:, :], ACT.Copy))
            wait_step(act, MIX_T, "z")
            inc(act.activation(z_tok, bank_c[0:L, :], ACT.Copy))
            wait_step(act, MIX_V, "cb")
            inc(act.activation(cve, cvb, ACT.Exp, scale=-1.0))
            wait_step(act, MIX_A, "u_z")
            inc(act.activation(z_e, z_tok, ACT.Exp, scale=-1.0))
            wait_step(act, MIX_V, "dt_abs")
            inc(act.activation(dtc, dtb, ACT.Exp))
            wait_step(act, MIX_V, "dt_one")
            inc(act.activation(dtd, dtm, ACT.Ln))
            wait_step(act, MIX_V, "snorm")
            inc(act.activation(a_ex, a_cl, ACT.Exp))
            wait_step(act, MIX_V, "dtm")
            inc(act.activation(dec, decm, ACT.Copy, scale=-1.0))
            for i in range(2):
                wait_step(act, MIX_T, f"seg{i}")
                inc(act.activation(dec_e[i], turned[i][0:L, 0:H * L].rearrange("p (h l) -> p h l", h=H), ACT.Exp))
            wait_step(act, MIX_V, "mean")
            inc(act.activation(ygq[:, :], ygm[:, :], ACT.Sqrt))
            wait_step(act, MIX_T, "M")
            inc(act.activation(m_hi[:, :], bank_c[:, :], ACT.Copy))

            def finish_columns(r, g=0):
                act.wait_ge(mm_done, lin(2 * (m2 + r + 1), 2 * RING, g))
                if r >= 2:
                    act.wait_ge(nat_done, lin(r - 1, RING, g))
                act.activation(o_col[:, r % 2, :], (acc, bank_c)[r % 2][:, :], ACT.Identity, bias=out_bc[:, 0:1])\
                    .then_inc(ot_done, 1)

            def last_block(r, n, m, g=0):
                high(m, 0, g)
                high(m, 1, g)
                if r >= 1:
                    finish_columns(r - 1, g)

            for r, n, m in LAST_BLOCKS[:RING]:
                last_block(r, n, m)
            with rounds(act, BL // RING - 1) as g:
                for r, n, m in LAST_BLOCKS[RING:2 * RING]:
                    last_block(r, n, m, g)
            finish_columns(BL - 1)

        @block.vector
        def _(dve):
            def rest(m, h, g=0):
                dve.wait_ge(hi_done, lin(2 * m + h + 1, 2 * RING, g))
                slot = 2 * (m % 2) + h
                dve.tensor_tensor(lo[:, slot, :], turned[h][:, :], hi[:, slot, :], ALU.subtract).then_inc(lo_done, 1)

            def row_sums(c, g=0):
                dve.wait_ge(a_in[c.n % RING], lin(16 * (c.n // RING + 1), 16, g))
                dve.tensor_reduce(part[:, 2:T4, bass.ds(lin(c.J, RING, g), 1)],
                                  a_ring[:, c.n % RING, 2:T4, :], AX.X, ALU.add).then_inc(dve_sum, 1)

            def prepare(K):
                dve.wait_ge(x_landed[K % 2], 16 * (K // 2 + 1))
                for t in range(T4):
                    ins = dve.bn_stats(bn[:, t, :], x_in[:, K % 2, t, :])
                ins.then_inc(prep_v.sem, 1)
                wait_step(dve, prep_v, "stats", K)
                for t in range(T4):
                    ins = dve.bn_aggr(mv[:, t, :], bn[:, t, :])
                ins.then_inc(prep_v.sem, 1)
                wait_step(dve, prep_v, "aggr", K)
                dve.tensor_scalar(mv[:, :, 1], mv[:, :, 1], LN_EPS, None, ALU.add).then_inc(prep_v.sem, 1)
                wait_step(dve, prep_a, "sqrt", K)
                dve.reciprocal(rstd4[:, :], sd[:, :]).then_inc(prep_v.sem, 1)
                wait_step(dve, prep_v, "rstd", K)
                if K >= 1:
                    dve.wait_ge(c_filled, c_use(("x", K - 1)) + 1)
                else:
                    dve.wait_ge(c_filled, 1)
                    wait_step(dve, set_t, "wslT")
                for t in range(T4):
                    ins = dve.tensor_scalar(lnx[:, t, :], x_in[:, K % 2, t, :], mv[:, t, 0:1], rstd4[:, t:t + 1],
                                            ALU.subtract, ALU.mult)
                ins.then_inc(prep_v.sem, 1)

            def degrees(K):
                dve.wait_ge(act_sum, BL * (K + 1))
                dve.wait_ge(dve_sum, BL * (K + 1))
                dve.tensor_reduce(rsum[:, :], part[:, :, :], AX.X, ALU.add).then_inc(deg_v.sem, 1)
                wait_step(dve, deg_v, "rows", K)
                dve.tensor_scalar(rsum[:, :], rsum[:, :], 1.0, None, ALU.add).then_inc(deg_v.sem, 1)
                wait_step(dve, deg_a, "sqrt", K)
                dve.reciprocal(dcol[:, K * T4:(K + 1) * T4], rsq[:, :]).then_inc(deg_v.sem, 1)
                wait_step(dve, deg_v, "inv", K)
                wait_step(dve, prep_t, "support", K)
                bank = (bank_a, bank_b)[K % 2]
                dve.tensor_tensor(sup[:, K * T4:(K + 1) * T4, :], bank[:, :].rearrange("p (t d) -> p t d", t=T4),
                                  dcol[:, K * T4:(K + 1) * T4].unsqueeze(2).to_broadcast([P, T4, D]),
                                  ALU.mult).then_inc(deg_v.sem, 1)

            dve.wait_ge(logits_in, 16 * TINY_FIRST)
            dve.tensor_scalar(temp[:, :], temp[:, :], 1e-6, None, ALU.max).then_inc(set_v.sem, 1)
            wait_step(dve, set_v, "tmax")
            dve.reciprocal(rtemp[:, :], temp[:, :]).then_inc(set_v.sem, 1)
            dve.tensor_copy(b_x_wide, b_xT[:, :].unsqueeze(2).to_broadcast([HD, H, P])).then_inc(set_v.sem, 1)
            wait_step(dve, set_t, "wslT")
            dve.tensor_copy(w_slT, bank_a[0:HD, 0:G]).then_inc(set_v.sem, 1)
            rt = rtemp[:, :].unsqueeze(2).to_broadcast([P, H, G])
            wait_step(dve, set_t, "wlog")
            wait_step(dve, set_v, "tinv")
            dve.tensor_tensor(W_logT[:, :].rearrange("p (h g) -> p h g", h=H),
                              bank_a[:, :].rearrange("p (h g) -> p h g", h=H), rt, ALU.mult).then_inc(set_v.sem, 1)
            wait_step(dve, set_t, "blog")
            bl = b_log[:, :].rearrange("p (h g) -> p h g", h=H)
            dve.tensor_tensor(bl, bank_b[:, :].rearrange("p (h g) -> p h g", h=H),
                              bsl[:, :].unsqueeze(1).to_broadcast([P, H, G]), ALU.add).then_inc(set_v.sem, 1)
            wait_step(dve, set_v, "blog_sum")
            dve.tensor_tensor(bl, bl, rt, ALU.mult).then_inc(set_v.sem, 1)

            prepare(0)
            for K, segs in enumerate(first_plan):
                if K + 1 < BL:
                    prepare(K + 1)
                for seg in segs:
                    with rounds(dve, seg.rounds) as g:
                        for c in seg.chunks:
                            row_sums(c, g)
                            if c.last:
                                degrees(K)
                            if c.m is not None:
                                rest(c.m, 0, g)
                                rest(c.m, 1, g)

            def finish(f):
                I = BL - 1 - f
                if f == 0:
                    dve.wait_ge(row_done, BL)
                    dve.tensor_copy(row_st[:, :], rows[:, f, :]).then_inc(fin_sums, 1)
                else:
                    dve.wait_ge(mm_done, 2 * fin_m[f])
                    dve.tensor_tensor(row_st[:, :], acc[:, :], rows[:, f, :], ALU.add).then_inc(fin_sums, 1)
                wait_step(dve, fin_t, "turned", f)
                dve.tensor_tensor(nat[:, :, :], bank_a[:, :].rearrange("p (t d) -> p t d", t=T4),
                                  sup[:, I * T4:(I + 1) * T4, :], ALU.add).then_inc(fin_v.sem, 1)
                wait_step(dve, fin_v, "add", f)
                dve.scalar_tensor_tensor(out=nat[:, :, :], in0=nat[:, :, :], scalar=0.0,
                                         in1=dcol[:, I * T4:(I + 1) * T4].unsqueeze(2).to_broadcast([P, T4, D]),
                                         op0=ALU.max, op1=ALU.mult).then_inc(fin_v.sem, 1)
                wait_step(dve, fin_v, "relu", f)
                i = BL + f
                dve.wait_ge(x_landed[i % 2], 16 * (i // 2 + 1))
                dve.tensor_tensor(x1[:, f * T4:(f + 1) * T4, :], nat[:, :, :], x_in[:, i % 2], ALU.add)\
                    .then_inc(fin_v.sem, 1)

            def slice_logits(k, g=0):
                R2 = RING // 2
                q = k - 1
                if 0 <= q < TILES:
                    lt = logit[:, q % 2, :].rearrange("p (h g) -> p h g", h=H)
                    dve.wait_ge(lg_done, lin(q + 1, R2, g))
                    if q >= 2:
                        dve.wait_ge(exp_done, lin(q - 1, R2, g))
                    dve.tensor_tensor(logit[:, q % 2, :], bank_c[:, :], b_log[:, :], ALU.add).then_inc(sm_done.sem, 1)
                    dve.wait_ge(sm_done.sem, lin(sm_done.value("bias", q), 3 * R2, g))
                    if q >= 1:
                        dve.wait_ge(sm_done.sem, lin(sm_done.value("shift", q - 1), 3 * R2, g))
                    dve.tensor_reduce(mx[:, :], lt, AX.X, ALU.max).then_inc(sm_done.sem, 1)
                    dve.wait_ge(sm_done.sem, lin(sm_done.value("max", q), 3 * R2, g))
                    dve.tensor_tensor(lt, lt, mx[:, :].unsqueeze(2).to_broadcast([P, H, G]), ALU.subtract)\
                        .then_inc(sm_done.sem, 1)

            def slice_rows(k, fins, g=0):
                R2 = RING // 2
                q = k + 1
                if 0 <= q < TILES:
                    ti = lin(q, R2, g)
                    dve.wait_ge(rstd_done, lin(q + 1, R2, g))
                    if q >= 2:
                        dve.wait_ge(xt_done, lin(q - 1, R2, g))
                    dve.tensor_scalar(xn_a[:, q % 2, :], x1[:, bass.ds(ti, 1), :].rearrange("p a d -> p (a d)"),
                                      mean[:, bass.ds(ti, 1)], rstd[:, bass.ds(ti, 1)],
                                      ALU.subtract, ALU.mult).then_inc(xa_done, 1)
                q = k - 3
                if 0 <= q < TILES:
                    dve.wait_ge(exp_done, lin(q + 1, R2, g))
                    if q >= 1:
                        dve.wait_ge(rd_done.sem, lin(rd_done.value("inv", q - 1), 2 * R2, g))
                    dve.tensor_reduce(den[:, :], expd[:, q % 2, :].rearrange("p (h g) -> p h g", h=H), AX.X, ALU.add)\
                        .then_inc(rd_done.sem, 1)
                    dve.wait_ge(rd_done.sem, lin(rd_done.value("sum", q), 2 * R2, g))
                    if q >= 2:
                        dve.wait_ge(sw_done.sem, lin(sw_done.value("weights", q - 2), 2 * R2, g))
                    dve.reciprocal(rden[:, q % 2, :], den[:, :]).then_inc(rd_done.sem, 1)
                    if q >= 2:
                        dve.wait_ge(tt_done, lin(q - 1, R2, g))
                    ti = lin(q, R2, g)
                    dve.tensor_scalar(xn_b[:, q % 2, :], x1[:, bass.ds(ti, 1), :].rearrange("p a d -> p (a d)"),
                                      mean[:, bass.ds(ti, 1)], rstd[:, bass.ds(ti, 1)],
                                      ALU.subtract, ALU.mult).then_inc(xb_done, 1)
                q = k + 2
                if 0 <= q < TILES:
                    ti = lin(q, R2, g)
                    wait_step(dve, fin_v, "x1", fins - 1)
                    dve.bn_stats(stat[:, q % 2, :], x1[:, bass.ds(ti, 1), :].rearrange("p a d -> p (a d)"))\
                        .then_inc(st_done.sem, 1)
                    even, odd = stat[:, q % 2, 1:3], stat[:, q % 2, 4:6]

                    def after(name):
                        dve.wait_ge(st_done.sem, lin(st_done.value(name, q), 7 * R2, g))

                    after("stats")
                    dve.tensor_tensor(both_st[:, :], even, odd, ALU.add).then_inc(st_done.sem, 1)
                    dve.tensor_tensor(gap[:, :], even[:, 0:1], odd[:, 0:1], ALU.subtract).then_inc(st_done.sem, 1)
                    after("sum")
                    dve.tensor_scalar(mean[:, bass.ds(ti, 1)], both_st[:, 0:1], 0.5, None, ALU.mult)\
                        .then_inc(st_done.sem, 1)
                    dve.tensor_scalar(within[:, :], both_st[:, 1:2], 1.0 / D, LN_EPS, ALU.mult, ALU.add)\
                        .then_inc(st_done.sem, 1)
                    after("gap")
                    dve.tensor_scalar(gap[:, :], gap[:, :], 0.5, None, ALU.mult).then_inc(st_done.sem, 1)
                    if q >= 2:
                        dve.wait_ge(rstd_done, lin(q - 1, R2, g))
                    after("half")
                    dve.tensor_scalar(vareps[:, q % 2:q % 2 + 1], gap[:, :], gap[:, 0:1], within[:, 0:1],
                                      ALU.mult, ALU.add).then_inc(st_done.sem, 1)

            fins = 0
            for I, segs in second_plan:
                for i, seg in enumerate(segs):
                    with rounds(dve, seg.rounds) as g:
                        for j, c in enumerate(seg.chunks):
                            rest(c.m, 0, g)
                            rest(c.m, 1, g)
                            k = sliced(c.m - 1)
                            if k is not None:
                                slice_logits(k, g)
                            if i == 0 and j == 0:
                                finish(fins)
                                fins += 1
                                if fins == 1:
                                    for k in (-2, -1):
                                        slice_rows(k, fins)
                            k = sliced(c.m - 2)
                            if k is not None:
                                slice_rows(k, fins, g)
            finish(fins)
            fins += 1
            for k in range(TILES - 6, SLICE_LAST + 1):
                slice_logits(k)
                slice_rows(k, fins)

            def V(name):
                wait_step(dve, MIX_V, name)

            def Aw(name):
                wait_step(dve, MIX_A, name)

            def Tw(name):
                wait_step(dve, MIX_T, name)

            order = iter(MIX_V.names)

            def inc(name, ins):
                assert next(order) == name, name
                ins.then_inc(MIX_V.sem, 1)

            def bc(ap, shape):
                return ap.unsqueeze(2).to_broadcast(shape)

            Tw("snorm")
            dve.wait_ge(tiny_in, TINY)
            dve.tensor_scalar(a_cl, a_lw[:, :], EXP_MAX, None, ALU.min)
            inc("snorm", dve.tensor_copy(snorm, bank_a[0:L, 0:H]))
            V("snorm")
            inc("snorm_e", dve.tensor_scalar(snorm_e, snorm, 1e-5, None, ALU.add))
            V("snorm_e")
            inc("rsnorm", dve.reciprocal(rsnorm, snorm_e))
            inc("st_b", dve.tensor_tensor(st_b, b_fx_w[:, :].rearrange("p (h c) -> p h c", h=H),
                                          bc(snorm, [L, H, HD]), ALU.mult))
            V("st_b")
            Tw("st")
            inc("st_s", dve.tensor_tensor(st_s, bank_c[0:L, :].rearrange("p (h c) -> p h c", h=H), st_b, ALU.add))
            V("st_s")
            inc("u", dve.tensor_tensor(u_tok.rearrange("p (h c) -> p h c", h=H), st_s, bc(rsnorm, [L, H, HD]), ALU.mult))
            Tw("uT")
            inc("uTc", dve.tensor_copy(uT, bank_b[:, 0:KC * L].rearrange("p (k l) -> p k l", k=KC)))
            inc("gpad", dve.memset(cpad, 0.0))
            inc("C0", dve.memset(Cpad, 0.0))
            inc("C1", dve.memset(ygs[:, :], 0.0))
            V("gpad")
            Tw("xbc")
            inc("xpad", dve.tensor_copy(cpad[:, 0:KC, 2:], bank_b[:, 0:KC * L].rearrange("p (k l) -> p k l", k=KC)))
            Tw("bc")
            inc("bpad", dve.tensor_copy(cpad[0:NS, KC:, 2:], acc[0:NS, 0:2 * L].rearrange("p (k l) -> p k l", k=2)))
            V("bpad")
            inc("c0", dve.tensor_tensor(cva, cpad[:, :, 0:L], bc(conv_ws[:, :, 0], [P, CK, L]), ALU.mult))
            inc("c1", dve.tensor_tensor(cvb, cpad[:, :, 1:L + 1], bc(conv_ws[:, :, 1], [P, CK, L]), ALU.mult))
            inc("c2", dve.tensor_tensor(cvc, cpad[:, :, 2:L + 2], bc(conv_ws[:, :, 2], [P, CK, L]), ALU.mult))
            V("c2")
            dve.tensor_tensor(cva, cva, cvb, ALU.add).then_inc(conv_v, 1)
            dve.wait_ge(conv_v, 1)
            dve.tensor_tensor(cva, cva, cvc, ALU.add).then_inc(conv_v, 1)
            dve.wait_ge(conv_v, 2)
            inc("cb", dve.tensor_tensor(cvb, cva, bc(conv_bs[:, :], [P, CK, L]), ALU.add))
            Aw("cexp")
            inc("ce1", dve.tensor_scalar(cve, cve, 1.0, None, ALU.add))
            V("ce1")
            inc("cr", dve.reciprocal(cvr, cve))
            V("cr")
            inc("xT", dve.tensor_tensor(xT, cvb, cvr, ALU.mult))
            V("xT")
            inc("Cp", dve.tensor_copy(Cpad[:, 1:L + 1], xT[0:NS, KC + 1, :]))
            Tw("dt")
            inc("dt_add", dve.tensor_tensor(dtr, bank_a[0:L, 0:2 * H].rearrange("p (a h) -> p a h", a=2),
                                            dt_bw[:, :].unsqueeze(1).to_broadcast([L, 2, H]), ALU.add))
            V("dt_add")
            dve.tensor_scalar(dta, dtr, -1.0, None, ALU.mult).then_inc(conv_v, 1)
            dve.wait_ge(conv_v, 3)
            inc("dt_abs", dve.tensor_tensor(dtb, dtr, dta, ALU.min))
            Aw("dexp")
            inc("dt_one", dve.tensor_scalar(dtm, dtc, 1.0, None, ALU.add))
            inc("dt_max", dve.tensor_scalar(dtr, dtr, 0.0, None, ALU.max))
            Aw("dln")
            V("dt_max")
            inc("dt", dve.tensor_tensor(dt, dtr, dtd, ALU.add))
            V("dt")
            Aw("aexp")
            inc("dtm", dve.tensor_tensor(decm, dt, a_ex.unsqueeze(1).to_broadcast([L, 2, H]), ALU.mult))
            Aw("dneg")
            inc("decm", dve.tensor_scalar(decm, dec, DECAY_MIN, None, ALU.max))
            V("decm")
            for i, w in enumerate((less, more)):
                inc(f"rhs{i}", dve.tensor_tensor(seg_rhs[i], w[:, :].unsqueeze(1).to_broadcast([L, H, L]),
                                                 bc(decm[:, i, :], [L, H, L]), ALU.mult))
            Tw("cb")
            inc("cb0", dve.tensor_tensor(cb[0], acc[0:L, 0:L], less[:, :], ALU.mult))
            inc("cb1", dve.tensor_tensor(cb[1], acc[0:L, L:2 * L], more[:, :], ALU.mult))
            Tw("xtok")
            inc("xtok", dve.tensor_copy(x_tok, bank_b[0:L, :]))
            Aw("zexp")
            inc("zc", dve.tensor_scalar(z_1, z_e, 1.0, None, ALU.add))
            V("zc")
            inc("ze1", dve.reciprocal(z_r, z_1))
            V("ze1")
            inc("zr", dve.tensor_tensor(gate, z_tok, z_r, ALU.mult))
            inc("gate", dve.memset(ygm[:, :], 0.0))
            for i in range(2):
                inc(f"cbd{i}", dve.tensor_tensor(cbh[i], cb[i].unsqueeze(1).to_broadcast([L, H, L]),
                                                 bc(dt[:, i, :], [L, H, L]), ALU.mult))
            V("cbd1")
            for i in range(2):
                Aw(f"dec{i}")
                inc(f"mix{i}", dve.tensor_tensor(dmix[i], dec_e[i], cbh[i], ALU.mult))
            V("mix1")
            inc("dsum", dve.tensor_tensor(dsum, dmix[0], dmix[1], ALU.add))
            Tw("fcd")
            inc("fcd", dve.tensor_tensor(fcd, bank_a[0:L, 0:H], Dw[:, :], ALU.add))
            V("fcd")
            inc("xf", dve.tensor_tensor(xf, x_tok.rearrange("p (h c) -> p h c", h=H), bc(fcd, [L, H, HD]), ALU.mult))
            V("xf")
            Tw("y")
            inc("y", dve.tensor_tensor(y_s, bank_c[0:L, :], xf.rearrange("p h c -> p (h c)"), ALU.add))
            V("y")
            inc("yg", dve.tensor_tensor(yg, y_s, gate, ALU.mult))
            V("yg")
            inc("ssq", dve.tensor_tensor_reduce(z_e, yg, yg, 1.0, 0.0, ALU.mult, ALU.add, ygs[:, :]))
            V("ssq")
            inc("mean", dve.tensor_scalar(ygm[:, :], ygs[:, :], 1.0 / INNER, 1e-5, ALU.mult, ALU.add))
            Aw("sqrt")
            inc("rms", dve.reciprocal(ygr[:, :], ygq[:, :]))
            V("rms")
            inc("ygn", dve.tensor_scalar(ygn, yg, ygr[:, 0:1], None, ALU.mult))
            V("ygn")
            inc("ygw", dve.tensor_tensor(ygw, ygn, norm_ww[:, :], ALU.mult))
            Tw("ygT")
            inc("ygTc", dve.tensor_copy(ygT, bank_b[:, 0:KC * L].rearrange("p (k l) -> p k l", k=KC)))
            Tw("ot")
            wait_step(dve, MIX_P, "bdz")
            src = bank_a[:, 0:KC * L].rearrange("p (k l) -> p k l", k=KC)
            inc("bd0", dve.tensor_copy(bd[0:HD, :, 0:G], src[0:HD]))
            inc("bd1", dve.tensor_copy(bd[HD:P, :, G:2 * G], src[HD:P]))
            Aw("mhi")
            inc("mlo", dve.tensor_tensor(m_lo[:, :], bank_c[:, :], m_hi[:, :], ALU.subtract))

            def rows_out(r, g=0):
                dve.wait_ge(nat_done, lin(r + 1, RING, g))
                if r >= 2:
                    dve.wait_ge(y_out[r % 2], lin(16 * (r // 2), 16 * RING // 2, g))
                dve.tensor_tensor(y_row[:, r % 2, :].rearrange("p (t d) -> p t d", t=T4),
                                  bank_a[:, :].rearrange("p (t d) -> p t d", t=T4),
                                  x1[:, bass.ds(lin(r * T4, RING * T4, g), T4), :], ALU.add).then_inc(y_done, 1)

            for r, n, m in LAST_BLOCKS[:RING]:
                rest(m, 0)
                rest(m, 1)
                if r >= 2:
                    rows_out(r - 2)
            with rounds(dve, BL // RING - 1) as g:
                for r, n, m in LAST_BLOCKS[RING:2 * RING]:
                    rest(m, 0, g)
                    rest(m, 1, g)
                    rows_out(r - 2, g)
            rows_out(BL - 2)
            rows_out(BL - 1)

        @block.gpsimd
        def _(pool):
            pool.memset(ident[:, :], 0.0).then_inc(ident_ok, 1)
            pool.memset(ones[:, :], 1.0)
            pool.memset(half[:, :], -0.5).then_inc(ident_ok, 1)
            pool.memset(sw_sum[:, :], 0.0)
            pool.memset(less[:, :], 1.0)
            pool.memset(more[:, :], 1.0)
            pool.memset(conv_ws[:, :, :], 0.0)
            pool.memset(conv_bs[:, :], 0.0).then_inc(ident_ok, 1)
            pool.wait_ge(ident_ok, 3)
            pool.affine_select(out=less[:, :], in_=less[:, :], compare_op=ALU.is_gt, fill=0.0, base=0,
                               pattern=[[1, L]], channel_multiplier=-1)
            pool.affine_select(out=more[:, :], in_=more[:, :], compare_op=ALU.is_gt, fill=0.0, base=0,
                               pattern=[[-1, L]], channel_multiplier=1)
            pool.affine_select(out=ident[:, :], in_=ident[:, :], compare_op=ALU.not_equal, fill=1.0, base=0,
                               pattern=[[-1, P]], channel_multiplier=1).then_inc(ident_ok, 1)
            with nc.allow_non_contiguous_dma(reason="a few hundred parameters"):
                for dst, src in tiny[TINY_FIRST:]:
                    pool.dma_start(dst, src).then_inc(tiny_in, 16)

            def support_rest(c, g=0):
                pool.wait_ge(sh_done, lin(c.m + 1, RING, g))
                pool.tensor_tensor(s_lo[:, c.m % 2, :], supf[:, bass.ds(lin(c.J, RING, g) * CH, CH)],
                                   s_hi[:, c.m % 2, :], ALU.subtract).then_inc(sl_done, 1)

            def slice_step(k, g=0):
                R2 = RING // 2
                q = k - 3
                if 0 <= q < TILES:
                    s3 = sw[:, q % 2, :].rearrange("p (h g) -> p h g", h=H)
                    pool.wait_ge(rd_done.sem, lin(rd_done.value("inv", q), 2 * R2, g))
                    if q >= 2:
                        pool.wait_ge(tt_done, lin(q - 1, R2, g))
                        pool.wait_ge(sw_out[q % 2], lin(16 * (q // 2), 16, g))
                    pool.tensor_tensor(s3, expd[:, q % 2, :].rearrange("p (h g) -> p h g", h=H),
                                       rden[:, q % 2, :].unsqueeze(2).to_broadcast([P, H, G]), ALU.mult)\
                        .then_inc(sw_done.sem, 1)
                    pool.wait_ge(sw_done.sem, lin(sw_done.value("weights", q), 2 * R2, g))
                    pool.dma_start(sw_dram[bass.ds(lin(q * P, R2 * P, g), P), :], sw[:, q % 2, :])\
                        .then_inc(sw_out[q % 2], 16)
                    pool.tensor_tensor(sw_sum[:, :], sw_sum[:, :], sw[:, q % 2, :], ALU.add).then_inc(sw_done.sem, 1)
                q = k + 2
                if 0 <= q < TILES:
                    ti = lin(q, R2, g)
                    pool.wait_ge(st_done.sem, lin(st_done.value("var", q), 7 * R2, g))
                    pool.tensor_tensor(rstd[:, bass.ds(ti, 1)], vareps[:, q % 2:q % 2 + 1], half[:, :], ALU.pow)\
                        .then_inc(rstd_done, 1)

            for segs in first_plan:
                for seg in segs:
                    if any(c.m is not None for c in seg.chunks):
                        with rounds(pool, seg.rounds) as g:
                            for c in seg.chunks:
                                if c.m is not None:
                                    support_rest(c, g)
            for I, segs in second_plan:
                for seg in segs:
                    with rounds(pool, seg.rounds) as g:
                        for c in seg.chunks:
                            support_rest(c, g)
                            if c.m == M0:
                                for k in (-2, -1):
                                    slice_step(k)
                            k = sliced(c.m - 3)
                            if k is not None:
                                slice_step(k, g)
            for k in range(TILES - 6, SLICE_LAST + 1):
                slice_step(k)
            pool.wait_ge(fin_v.sem, fin_v.value("x1", BL - 1))
            pool.memset(bd, 0.0).then_inc(MIX_P.sem, 1)


INPUTS = ["x", "adj", "L0_gnn_W", "L0_ffn_W_fx", "L0_ffn_b_fx", "L0_ffn_W_x", "L0_ffn_b_x", "L0_ffn_W_slice",
          "L0_ffn_b_slice", "L0_ffn_temperature", "L0_ffn_hy_in_w", "L0_ffn_hy_conv_w", "L0_ffn_hy_conv_b",
          "L0_ffn_hy_dt_bias", "L0_ffn_hy_A_log", "L0_ffn_hy_D", "L0_ffn_hy_fcD_w", "L0_ffn_hy_norm_w",
          "L0_ffn_hy_out_w", "L0_ffn_out_w", "L0_ffn_out_b"]


def kernel(**inputs):
    import numpy as np
    import concourse.bacc as bacc
    from concourse.bass_utils import run_bass_kernel_spmd

    nc = bacc.Bacc("TRN2", target_bir_lowering=False, num_devices=1)
    arrays, args = {}, []
    for name in INPUTS:
        a = np.ascontiguousarray(inputs[name])
        arrays[f"in_{name}"] = a
        args.append(nc.dram_tensor(f"in_{name}", a.shape, mybir.dt.from_np(a.dtype), kind="ExternalInput").ap())
    shape = tuple(inputs["x"].shape)
    out = nc.dram_tensor("out_x", shape, F32, kind="ExternalOutput").ap()
    gnn_slice_ffn(nc, *args, out)
    result = run_bass_kernel_spmd(nc, [arrays], core_ids=[0])
    return result.results[0]["out_x"]
```

```python
from collections import namedtuple
from contextlib import ExitStack, contextmanager

import concourse.bass as bass
from concourse import mybir

ALU = mybir.AluOpType
ACT = mybir.ActivationFunctionType
AX = mybir.AxisListType
F32 = mybir.dt.float32
F32R = mybir.dt.float32r

P = 128
D = 128
CH = 512
T4 = CH // P
RING = 4
H = 8
HD = 64
G = 64
HG = H * G
INNER = H * HD
NS = 64
CONV = INNER + 2 * NS
KW = 3
PROJ = 2 * INNER + 2 * NS + 2 * H
LN_EPS = 1e-5
EXP_MAX = 88.0
DECAY_MIN = -1.0e4

Chunk = namedtuple("Chunk", "n m J k last")
Seg = namedtuple("Seg", "rounds chunks")


class Steps:

    def __init__(self, sem, names):
        self.sem, self.names = sem, names.split()

    def value(self, name, rnd=0):
        return rnd * len(self.names) + self.names.index(name) + 1


def wait_step(eng, steps, name, rnd=0):
    eng.wait_ge(steps.sem, steps.value(name, rnd))


@contextmanager
def rounds(eng, count):
    if count == 1:
        yield 0
    else:
        with eng.Fori(0, count) as g:
            yield g


def spread(a, b):
    marks = [((i + 0.5) / len(a), 0, v) for i, v in enumerate(a)] + [((i + 0.5) / len(b), 1, v) for i, v in enumerate(b)]
    return [v for _, _, v in sorted(marks)]


def plan_first_reading(blocks):
    plan, n, m = [], 0, 0
    groups = blocks // RING
    for K in range(blocks):
        below, above = list(range(K)), list(range(K + 1, blocks))
        if K < RING:
            loop = above[RING:RING * (groups - 1)]
            parts = [spread(above[:RING], below), loop, above[RING * (groups - 1):] + [K]]
        elif K < RING * (groups - 1):
            parts = [spread(above, below) + [K]]
        else:
            loop = below[RING:RING * (groups - 1)]
            parts = [spread(above, below[:RING]), loop, below[RING * (groups - 1):] + [K]]
        segs, k = [], 0
        for part in parts:
            looped = len(parts) > 1 and part is parts[1]
            chunks = []
            for J in part[:RING] if looped else part:
                contracted = J <= K
                chunks.append(Chunk(n, m if contracted else None, J, k if contracted and not looped else None, J == K))
                n += 1
                m += contracted
                k += contracted
            count = len(part) // RING if looped else 1
            n += RING * (count - 1)
            m += RING * (count - 1) * (chunks[0].m is not None)
            segs.append(Seg(count, chunks))
        plan.append(segs)
    return plan, n, m


def plan_second_reading(blocks, n, m):
    plan = []
    for I in reversed(range(blocks - 1)):
        a, b = divmod(I, RING)
        segs = []
        straight = RING - 1 - b
        if straight:
            segs.append(Seg(1, [Chunk(n + i, m + i, I + 1 + i, i, False) for i in range(straight)]))
            n, m = n + straight, m + straight
        loops = blocks // RING - 1 - a
        parts = [loops] if straight == RING - 1 or not loops else [1, loops - 1]
        if not I:
            parts = [loops - 1, 1]
        done = 0
        for k in parts:
            if k:
                segs.append(Seg(k, [Chunk(n + i, m + i, RING * (a + 1 + done) + i, straight + RING * done + i if k == 1 else None, False)
                                    for i in range(RING)]))
                n, m, done = n + RING * k, m + RING * k, done + k
        plan.append((I, segs))
    return plan, n, m


def gnn_slice_ffn(nc, x, adj, gnn_W, W_fx, b_fx, W_x, b_x, W_slice, b_slice, temperature, in_w, conv_w,
                  conv_b, dt_bias, A_log, Dp, fcD_w, norm_w, hy_out_w, out_w, out_b, out):
    N = x.shape[0]
    BL = N // CH
    TILES = N // P
    first_plan, n1, m1 = plan_first_reading(BL)
    second_plan, n2, m2 = plan_second_reading(BL, n1, m1)
    contracted_at = {}
    for segs in first_plan:
        for seg in segs:
            for r in range(seg.rounds):
                contracted_at.update((c.n + RING * r, c.m + RING * r) for c in seg.chunks if c.m is not None)
    n_at = {m: n for n, m in contracted_at.items()}
    n_at[m1] = n1
    first_blocks = [next(c.m for seg in segs for c in seg.chunks if c.k == 0) for segs in first_plan]
    second_blocks = [segs[0].chunks[0].m for _, segs in second_plan]
    assert n1 == BL * BL and n1 % RING == 0 and n2 % RING == 0 and m2 % 2 == 0
    SLICE_LAST = TILES + 4
    SLICE_ALONE = TILES - 6
    LATE = SLICE_ALONE - 3
    M0 = m1
    N0 = n1

    def sliced(m_base):
        i = m_base - M0
        k = i // 2
        return k if i > 0 and i % 2 == 1 and k < SLICE_ALONE else None

    with ExitStack() as ctx:
        def sb(name, shape, dt=F32):
            return ctx.enter_context(nc.sbuf_tensor(name, shape, dt))

        def psum(name, shape):
            return ctx.enter_context(nc.psum_tensor(name, shape, F32))

        def sem(name):
            return ctx.enter_context(nc.semaphore(name))

        turned = [psum(f"turned{i}", [P, 2 * CH]) for i in range(2)]
        acc = psum("acc", [P, CH])
        bank_a = psum("bank_a", [P, CH])
        bank_b = psum("bank_b", [P, CH])
        bank_c = psum("bank_c", [P, CH])

        a_ring = sb("a_ring", [P, RING, T4, CH])
        hi = sb("hi", [P, 4, 2 * CH], F32R)
        lo = sb("lo", [P, 4, 2 * CH], F32R)
        sup = sb("sup", [P, TILES, D])
        rows = sb("rows", [P, BL, CH])
        x1 = rows[:, :, :].rearrange("p b (t d) -> p (b t) d", d=D)
        s_hi = sb("s_hi", [P, 2, CH], F32R)
        s_lo = sb("s_lo", [P, 2, CH], F32R)
        m_hi = sb("m_hi", [P, CH], F32R)
        m_lo = sb("m_lo", [P, CH], F32R)
        x_in = sb("x_in", [P, 2, T4, D])
        lnx = sb("lnx", [P, T4, D])
        lnxT = sb("lnxT", [P, CH])
        logit = sb("logit", [P, 2, HG])
        expd = sb("expd", [P, 2, HG])
        sw = sb("sw", [P, 2, HG])
        w_raw = sw
        W_logT = sw[:, 0, :]
        in_wT = sb("in_wT", [P, INNER // P, PROJ])
        hy_outT = sb("hy_outT", [P, INNER // P, INNER])
        W_fxT = sb("W_fxT", [P, INNER])
        out_wT = sb("out_wT", [P, INNER // P, D])
        fcD_T = sb("fcD_T", [P, INNER // P, H])
        gnn_WT = sb("gnn_WT", [P, D])
        W_log_hi, W_log_lo = m_hi, m_lo
        b_log = sb("b_log", [P, HG])
        ident = sb("ident", [P, P])
        ones = sb("ones", [P, 1])
        row_st = lnxT
        nat = lnx
        part = sb("part", [P, T4, BL])
        rsum = sb("rsum", [P, T4])
        rsq = sb("rsq", [P, T4])
        dcol = sb("dcol", [P, TILES])
        bn = sb("bn", [P, T4, 6])
        mv = sb("mv", [P, T4, 2])
        sd = sb("sd", [P, T4])
        rstd4 = sb("rstd4", [P, T4])
        mvx = sb("mvx", [P, TILES, 2])
        rstd = sb("rstd", [P, TILES])
        half = sb("half", [P, 1])
        xns = sb("xns", [P, 4, D])
        xnT = sb("xnT", [P, 2, D], F32R)
        xn_a, xn_b = xns[:, 0:2, :], xns[:, 2:4, :]
        xnT_hi, xnT_lo = xnT[:, 0, :], xnT[:, 1, :]
        junk = xns[:, 0:4, :].rearrange("p a d -> p (a d)").bitcast(mybir.dt.bfloat16)
        mx = sb("mx", [P, H])
        neg_mx = sb("neg_mx", [P, 2, H])
        den = sb("den", [P, 2, H])
        rden = sb("rden", [P, 2, H])
        sw_sum = sb("sw_sum", [P, HG])
        temp = sb("temp", [P, H])
        rtemp = sb("rtemp", [P, H])
        bsl = sb("bsl", [P, G])
        out_bc = sb("out_bc", [P, 1])

        sw_dram = nc.dram_tensor("sw_dram", [N, HG], F32, kind="Internal").ap()

        a_in = [sem(f"a_in{i}") for i in range(RING)]
        act_sum = sem("act_sum")
        dve_sum = sem("dve_sum")
        t_done = sem("t_done")
        hi_done = sem("hi_done")
        lo_done = sem("lo_done")
        sh_done = sem("sh_done")
        sl_done = sem("sl_done")
        mm_done = sem("mm_done")
        row_done = sem("row_done")
        ident_ok = sem("ident_ok")
        setup_in = sem("setup_in")
        tiny_in = sem("tiny_in")
        logits_in = sem("logits_in")
        x_landed = [sem(f"x_landed{i}") for i in range(2)]
        w_landed = [sem(f"w_landed{i}") for i in range(2)]
        c_filled = sem("c_filled")
        c_copied = sem("c_copied")
        prep_v = Steps(sem("prep_v"), "stats aggr eps rstd norm")
        prep_a = Steps(sem("prep_a"), "sqrt")
        prep_t = Steps(sem("prep_t"), "support")
        deg_v = Steps(sem("deg_v"), "rows one inv scaled")
        deg_a = Steps(sem("deg_a"), "sqrt")
        fin_v = Steps(sem("fin_v"), "add relu x1 stats aggr eps")
        fin_t = Steps(sem("fin_t"), "turned")
        fin_sums = sem("fin_sums")
        rstd_done = sem("rstd_done")
        xa_done = sem("xa_done")
        xt_done = sem("xt_done")
        xtc_done = sem("xtc_done")
        xtl_done = sem("xtl_done")
        lg_done = sem("lg_done")
        sm_done = Steps(sem("sm_done"), "bias max neg")
        exp_done = sem("exp_done")
        rd_done = sem("rd_done")
        xb_done = sem("xb_done")
        sw_done = Steps(sem("sw_done"), "weights total")
        sw_out = [sem(f"sw_out{i}") for i in range(2)]
        sw_late = [sem(f"sw_late{i}") for i in range(2)]
        tt_done = sem("tt_done")

        set_v = Steps(sem("set_v"), "tmax tinv bx_wide wslT wlog blog_sum blog whi wlo")
        set_t = Steps(sem("set_t"), "wslT wlog blog")

        units = [("in", in_w[r * P:min((r + 1) * P, PROJ), :], min(P, PROJ - r * P),
                  in_wT[:, :, r * P:min((r + 1) * P, PROJ)]) for r in range(-(-PROJ // P))]
        units += [("ho", hy_out_w[r * P:(r + 1) * P, :], P, hy_outT[:, :, r * P:(r + 1) * P])
                  for r in range(INNER // P)]
        units += [("fx", W_fx.rearrange("(t p) d -> p t d", p=P), P, W_fxT[:, :].rearrange("p (t d) -> p t d", t=T4))]
        units += [("ow", out_w[:, :], P, out_wT[:, :, :])]
        units += [("fd", fcD_w[:, :], H, fcD_T[:, :, :])]
        PER = 2
        FIRST_UNITS = RING
        unit_block = {u: FIRST_UNITS + u // PER for u in range(len(units))}
        c_uses = ["g", ("x", 0)]
        for K in range(BL):
            if K + 1 < BL:
                c_uses.append(("x", K + 1))
            c_uses += [("w", u) for u in unit_block if unit_block[u] == K]

        def c_use(u):
            return c_uses.index(u)

        w_sl = rows[0:G, 0, 0:HD]
        w_slT = rows[0:HD, 1, 0:G]
        w_x_c = expd[0:HD, :, :].rearrange("c a (h d) -> c (a h) d", d=D)
        b_xT = sb("b_xT", [HD, H])
        b_x_wide = logit[0:HD, :, :].rearrange("c a (h d) -> c (a h) d", d=P)

        supf = sup[:, :, :].rearrange("p t d -> p (t d)")
        regions = [[ap, 0, size] for ap, size in (
            (supf, TILES * D), (logit[:, :, :].rearrange("p a g -> p (a g)"), 2 * HG),
            (expd[:, :, :].rearrange("p a g -> p (a g)"), 2 * HG))]

        def tmp(parts, *shape):
            size = 1
            for k in shape:
                size *= k
            region = next(r for r in regions if r[1] + size <= r[2])
            ap = region[0][0:parts, region[1]:region[1] + size]
            region[1] += size
            if len(shape) == 2:
                ap = ap.rearrange("p (a b) -> p a b", b=shape[1])
            return ap

        L = G
        KC = INNER // P
        TTs = tmp(P, HG)
        snorm = tmp(L, H)
        snorm_e = tmp(L, H)
        rsnorm = tmp(L, H)
        b_fx_w = sb("b_fx_w", [L, INNER])
        norm_ww = sb("norm_ww", [L, INNER])
        st_b = tmp(L, H, HD)
        st_s = st_b
        u_tok = tmp(L, INNER)
        uT = tmp(P, KC, L)
        z_tok = tmp(L, INNER)
        z_e = tmp(L, INNER)
        z_1 = z_e
        gate = tmp(L, INNER)
        CK = KC + 2
        cpad = tmp(P, CK, L + 2)
        cva = tmp(P, CK, L)
        cvb = tmp(P, CK, L)
        cvc = tmp(P, CK, L)
        cve = tmp(P, CK, L)
        xT = tmp(P, CK, L)
        conv_ws = sb("conv_ws", [P, CK, KW])
        conv_bs = sb("conv_bs", [P, CK])
        Cpad = tmp(NS, L + 2)
        x_tok = tmp(L, INNER)
        dtr = tmp(L, 2, H)
        dta = tmp(L, 2, H)
        dtb = tmp(L, 2, H)
        dtc = tmp(L, 2, H)
        dtd = tmp(L, 2, H)
        dtm = tmp(L, 2, H)
        dt = tmp(L, 2, H)
        dec = tmp(L, 2, H)
        decm = tmp(L, 2, H)
        dt_bw = sb("dt_bw", [L, H])
        a_lw = sb("a_lw", [L, H])
        a_cl = tmp(L, H)
        a_ex = tmp(L, H)
        Dw = sb("Dw", [L, H])
        seg_rhs = [tmp(L, H, L) for _ in range(2)]
        dec_e = [tmp(L, H, L) for _ in range(2)]
        cb = [tmp(L, L) for _ in range(2)]
        cbh = [tmp(L, H, L) for _ in range(2)]
        dmix = dec_e
        dsum = dec_e[0]
        fcd = tmp(L, H)
        xf = u_tok.rearrange("p (h c) -> p h c", h=H)
        y_s = z_tok
        yg = ygn = ygw = y_s
        ygs = sb("ygs", [L, 1])
        ygm = sb("ygm", [L, 1])
        ygq = sb("ygq", [L, 1])
        ygr = sb("ygr", [L, 1])
        ygT = tmp(P, KC, L)
        bd = lnxT[:, :].rearrange("p (k d) -> p k d", k=KC)
        less = sb("less", [L, L])
        more = sb("more", [L, L])
        MIX_V = Steps(sem("mix_v"), "gpad C0 C1 snorm snorm_e rsnorm st_b st_s u uTc dt_add dt_neg dt_abs dt_one dt_max dt dtm decm "
                      "rhs0 rhs1 xpad bpad c0 c1 c2 c01 c012 cb ce1 cr xT Cp "
                      "cb0 cb1 xtok cbd0 cbd1 mix0 mix1 dsum zr fcd xf y yg ssq mean rms "
                      "ygn ygw ygTc bd0 bd1 mlo")
        MIX_A = Steps(sem("mix_a"), "TT aexp dexp dln dec0 dec1 cexp u_z zexp sqrt mhi")
        MIX_T = Steps(sem("mix_t"), "snorm st uT dt xbc bc seg0 seg1 z cb xtok fcd y ygT ot M")
        MIX_P = Steps(sem("mix_p"), "bdz plus gate")
        ot_done = sem("ot_done")
        nat_done = sem("nat_done")
        y_done = sem("y_done")
        y_out = [sem(f"y_out{i}") for i in range(2)]
        o_col = logit
        y_row = expd

        def lin(base, step, g):
            return base + step * g

        a_rows = adj.rearrange("(b t p) c -> b p t c", p=P, t=T4)
        x_rows = x.rearrange("(b t p) d -> b p t d", p=P, t=T4)
        sw_rows = sw_dram.rearrange("(b t p) c -> b p t c", p=P, t=T4)
        out_rows = out.rearrange("(b t p) d -> b p t d", p=P, t=T4)
        LAST_BLOCKS = [(r, n2 + r, m2 + r) for r in range(BL)]

        fin_m = [m1] + [segs[-1].chunks[-1].m + RING * (segs[-1].rounds - 1) + 1 for _, segs in second_plan]
        fin_xt = [sum(1 for m in range(m1, fm + 1) if sliced(m) is not None) for fm in fin_m]
        fin_xt[-1] += 1

        def wide(vec, parts):
            return vec.partition_broadcast(parts)

        tiny = [
            (temp[:, :], wide(temperature.rearrange("a h b c -> (a h b c)"), P)),
            (b_xT[:, :], b_x.rearrange("(h c) -> c h", c=HD)),
            (bsl[:, :], wide(b_slice, P)),
            (out_bc[:, :], out_b.rearrange("(p a) -> p a", a=1)),
            (b_fx_w[:, :], wide(b_fx, L)),
            (norm_ww[:, :], wide(norm_w, L)),
            (dt_bw[:, :], wide(dt_bias, L)),
            (a_lw[:, :], wide(A_log, L)),
            (Dw[:, :], wide(Dp, L)),
            (conv_ws[:, 0:KC, :], conv_w[0:INNER, :].rearrange("(k p) w -> p k w", p=P)),
            (conv_ws[0:NS, KC:CK, :], conv_w[INNER:CONV, :].rearrange("(k p) w -> p k w", p=NS)),
            (conv_bs[:, 0:KC], conv_b[0:INNER].rearrange("(k p) -> p k", p=P)),
            (conv_bs[0:NS, KC:CK], conv_b[INNER:CONV].rearrange("(k p) -> p k", p=NS)),
        ]
        TINY_FIRST = 3
        TINY = 16 * (len(tiny) - TINY_FIRST)

        block = ctx.enter_context(nc.Block())

        @block.sync
        def _(sp):
            def load_x(i):
                b = i if i < BL else 2 * BL - 1 - i
                if 2 <= i < BL + 2:
                    wait_step(sp, prep_v, "norm", i - 2)
                if i >= BL + 2:
                    wait_step(sp, fin_v, "x1", i - BL - 2)
                sp.dma_start(x_in[:, i % 2], x_rows[b]).then_inc(x_landed[i % 2], 16)

            def load_w(u):
                kind, src, k, _ = units[u]
                if u >= 2:
                    sp.wait_ge(c_filled, c_use(("w", u - 2)) + 1)
                dst = w_raw[0:k, u % 2, :]
                if kind == "fx":
                    dst = dst.rearrange("p (t d) -> p t d", t=T4)
                sp.dma_start(dst, src).then_inc(w_landed[u % 2], 16)

            sp.dma_start(lnx[:, 1, :], gnn_W).then_inc(setup_in, 16)
            sp.dma_start(w_sl, W_slice).then_inc(setup_in, 16)
            sp.dma_start(w_x_c, W_x.rearrange("(h c) d -> c h d", c=HD)).then_inc(setup_in, 16)
            load_x(0)
            with nc.allow_non_contiguous_dma(reason="512 biases, turned"):
                for dst, src in tiny[:TINY_FIRST]:
                    sp.dma_start(dst, src).then_inc(logits_in, 16)

            def load(n, slot, K, J):
                sp.dma_start(a_ring[:, slot], a_rows[K][:, :, bass.ds(J * CH, CH)]).then_inc(a_in[slot], 16)

            for K, segs in enumerate(first_plan):
                if K + 1 < BL:
                    load_x(K + 1)
                for u in unit_block:
                    if unit_block[u] == K:
                        load_w(u)
                for seg in segs:
                    with rounds(sp, seg.rounds) as g:
                        for c in seg.chunks:
                            old = c.n - RING
                            if old in contracted_at:
                                sp.wait_ge(t_done, 2 * (contracted_at[old] + 1))
                            if old >= 0:
                                sp.wait_ge(act_sum, old + 1)
                                sp.wait_ge(dve_sum, old + 1)
                            if seg.rounds > 1:
                                if c.m is not None:
                                    sp.wait_ge(lo_done, lin(2 * (c.m - RING + 1), 2 * RING, g))
                                else:
                                    sp.wait_ge(act_sum, lin(old + 1, RING, g))
                                    sp.wait_ge(dve_sum, lin(old + 1, RING, g))
                            load(c.n, c.n % RING, K, lin(c.J, RING, g))

            load_x(BL)
            load_x(BL + 1)
            for I, segs in second_plan:
                for seg in segs:
                    with rounds(sp, seg.rounds) as g:
                        for c in seg.chunks:
                            if c.n < N0 + RING:
                                sp.wait_ge(act_sum, c.n - RING + 1)
                                sp.wait_ge(dve_sum, c.n - RING + 1)
                            sp.wait_ge(t_done, lin(2 * (c.m - RING + 1), 2 * RING, g))
                            load(c.n, c.n % RING, I, lin(c.J, RING, g))
                            if c.k == 2:
                                load_x(2 * BL - 2 - I)
            load_x(2 * BL - 1)

            for q in range(LATE, TILES):
                wait_step(sp, sw_done, "weights", q)
                sp.dma_start(sw_dram[q * P:(q + 1) * P, :], sw[:, q % 2, :]).then_inc(sw_late[q % 2], 16)

            for i in range(2):
                sp.wait_ge(sw_out[i], 16 * len(range(i, LATE, 2)))
                sp.wait_ge(sw_late[i], 16 * (TILES // 2 - len(range(i, LATE, 2))))
            with rounds(sp, BL // RING) as g:
                for r, n, m in LAST_BLOCKS[:RING]:
                    sp.wait_ge(t_done, lin(2 * (m - RING + 1), 2 * RING, g))
                    sp.dma_start(a_ring[:, n % RING], sw_rows[r + RING * g]).then_inc(a_in[n % RING], 16)

        @block.tensor
        def _(pe):
            def turn(n, m, h, g=0):
                if h == 0:
                    pe.wait_ge(a_in[n % RING], lin(16 * (n // RING + 1), 16, g))
                if m >= 1:
                    pe.wait_ge(lo_done, lin(2 * (m - 1) + h + 1, 2 * RING, g))
                for s in range(2):
                    for t in range(T4):
                        at = s * CH + t * P
                        col = (2 * h + s) * P
                        ins = pe.transpose(turned[h][:, at:at + P], a_ring[:, n % RING, t, col:col + P], ident[:, :])
                ins.then_inc(t_done, 1)

            def contract(m, h, first, last, g=0, stat_hi=None, stat_lo=None, into=acc):
                pe.wait_ge(lo_done, lin(2 * m + h + 1, 2 * RING, g))
                slot = 2 * (m % 2) + h
                sh = s_hi[:, m % 2] if stat_hi is None else stat_hi
                sl = s_lo[:, m % 2] if stat_lo is None else stat_lo
                for s in range(2):
                    col = (2 * h + s) * P
                    mov_hi = hi[:, slot, s * CH:(s + 1) * CH]
                    mov_lo = lo[:, slot, s * CH:(s + 1) * CH]
                    opens = first and h == 0 and s == 0
                    closes = last and h == 1 and s == 1
                    pe.matmul(into[:, :], sh[:, col:col + P], mov_hi, start=opens, stop=False, skip_group_check=True)
                    pe.matmul(into[:, :], sh[:, col:col + P], mov_lo, start=False, stop=False, skip_group_check=True)
                    ins = pe.matmul(into[:, :], sl[:, col:col + P], mov_hi, start=False, stop=closes,
                                    skip_group_check=True)
                ins.then_inc(mm_done, 1)

            def chunk_sums(c, last, n_next, g=0):
                for h in range(2):
                    if n_next is not None:
                        turn(n_next, c.m + 1, h, g)
                    if h == 0:
                        pe.wait_ge(sl_done, lin(c.m + 1, RING, g))
                        if c.k == 0 and c.m in first_blocks[1:]:
                            pe.wait_ge(row_done, first_blocks.index(c.m))
                        if c.k == 0 and c.m in second_blocks:
                            pe.wait_ge(fin_sums, second_blocks.index(c.m) + 1)
                        if c.m == M0:
                            pe.wait_ge(row_done, BL)
                    contract(c.m, h, c.k == 0, last, g)

            def weights_turned(use, src, k, cols):
                if use >= 1:
                    pe.wait_ge(c_copied, use)
                for t in range(T4):
                    ins = pe.transpose(bank_c[0:cols, t * P:t * P + k], src(t), ident[0:k, 0:k])
                ins.then_inc(c_filled, 1)

            def turn_x(K):
                wait_step(pe, prep_v, "norm", K)
                weights_turned(c_use(("x", K)), lambda t: lnx[:, t, :], P, P)

            def support(K):
                pe.wait_ge(c_copied, c_use(("x", K)) + 1)
                if K >= 2:
                    wait_step(pe, deg_v, "scaled", K - 2)
                bank = (bank_a, bank_b)[K % 2]
                for t in range(T4):
                    ins = pe.matmul(bank[:, t * D:(t + 1) * D], lnxT[:, t * P:(t + 1) * P], gnn_WT[:, :],
                                    start=True, stop=True)
                ins.then_inc(prep_t.sem, 1)

            pe.wait_ge(ident_ok, 4)
            pe.wait_ge(setup_in, 48)
            pe.transpose(bank_c[:, 0:P], lnx[:, 1, :], ident[:, :]).then_inc(c_filled, 1)
            def turn_weights(K, i):
                u = PER * (K - FIRST_UNITS) + i
                if 0 <= u and u in unit_block and unit_block[u] == K:
                    k = units[u][2]
                    pe.wait_ge(w_landed[u % 2], 16 * (u // 2 + 1))
                    weights_turned(c_use(("w", u)), lambda t: w_raw[0:k, u % 2, t * P:(t + 1) * P], k, P)

            turn_x(0)
            support(0)
            turn_x(1)
            support(1)
            pe.transpose(acc[0:HD, 0:G], w_sl, ident[0:G, 0:G]).then_inc(set_t.sem, 1)
            wait_step(pe, set_v, "wslT")
            for h in range(H):
                ins = pe.matmul(turned[0][:, h * G:(h + 1) * G], w_x_c[:, h, :], w_slT, start=True, stop=True)
            ins.then_inc(set_t.sem, 1)
            for h in range(H):
                ins = pe.matmul(turned[1][:, h * G:(h + 1) * G], b_x_wide[:, h, :], w_slT, start=True, stop=True)
            ins.then_inc(set_t.sem, 1)
            for h, name in enumerate(("wlog", "blog_sum")):
                wait_step(pe, set_v, name)
                turn(n_at[0], 0, h)
            for K, segs in enumerate(first_plan):
                for seg in segs:
                    with rounds(pe, seg.rounds) as g:
                        for c in seg.chunks:
                            if c.m is None:
                                continue
                            chunk_sums(c, c.last, n_at[c.m + 1], g)
                            if c.k == 0 and 1 <= K < BL - 1:
                                turn_x(K + 1)
                            if c.k == 1 and K < BL - 1:
                                support(K + 1)
                            if c.k in (1, 2):
                                turn_weights(K, c.k - 1)

            def finish(f):
                pe.wait_ge(fin_sums, f + 1)
                if f == 0:
                    wait_step(pe, deg_v, "scaled", BL - 1)
                else:
                    wait_step(pe, fin_v, "add", f - 1)
                    if fin_xt[f]:
                        pe.wait_ge(xtl_done, fin_xt[f])
                for t in range(T4):
                    ins = pe.transpose(bank_a[:, t * D:(t + 1) * D], row_st[:, t * P:(t + 1) * P], ident[:, :])
                ins.then_inc(fin_t.sem, 1)

            def slice_step(k, fins, g=0):
                R2 = RING // 2
                if 0 <= k < TILES:
                    pe.wait_ge(xa_done, lin(k + 1, R2, g))
                    wait_step(pe, fin_v, "add", fins - 1)
                    if k >= 1:
                        pe.wait_ge(xtl_done, lin(k, R2, g))
                    pe.transpose(bank_a[:, 0:P], xn_a[:, k % 2, :], ident[:, :]).then_inc(xt_done, 1)
                q = k - 1
                if 0 <= q < TILES:
                    if q >= 1:
                        pe.wait_ge(sm_done.sem, lin(sm_done.value("bias", q - 1), 3 * R2, g))
                    pe.wait_ge(xtl_done, lin(q + 1, R2, g))
                    pe.matmul(bank_c[:, :], xnT_hi, W_log_hi[:, :], start=True, stop=False, skip_group_check=True)
                    pe.matmul(bank_c[:, :], xnT_lo, W_log_hi[:, :], start=False, stop=False, skip_group_check=True)
                    pe.matmul(bank_c[:, :], xnT_hi, W_log_lo[:, :], start=False, stop=True, skip_group_check=True)\
                        .then_inc(lg_done, 1)
                q = k - 5
                if 0 <= q < TILES:
                    pe.wait_ge(sw_done.sem, lin(sw_done.value("weights", q), 2 * R2, g))
                    pe.wait_ge(xb_done, lin(q + 1, R2, g))
                    pe.matmul(bank_b[:, :], xn_b[:, q % 2, :], sw[:, q % 2, :], start=(q == 0), stop=(q == TILES - 1),
                              skip_group_check=True).then_inc(tt_done, 1)

            fins = 0
            for I, segs in second_plan:
                for i, seg in enumerate(segs):
                    with rounds(pe, seg.rounds) as g:
                        for j, c in enumerate(seg.chunks):
                            last = i == len(segs) - 1 and j == len(seg.chunks) - 1
                            chunk_sums(c, last, None if last and I == 0 else c.n + 1, g)
                            k = sliced(c.m)
                            if k is not None:
                                slice_step(k, fins, g)
                            if c.k == 0:
                                finish(fins)
                                fins += 1
            slice_step(SLICE_ALONE, fins)
            finish(fins)
            fins += 1
            for k in range(SLICE_ALONE + 1, SLICE_LAST + 1):
                slice_step(k, fins)


            def inc(ins):
                ins.then_inc(MIX_T.sem, 1)

            pe.wait_ge(tt_done, TILES)
            wait_step(pe, sw_done, "total", TILES - 1)
            for h in range(H):
                ins = pe.matmul(bank_a[0:G, h:h + 1], sw_sum[:, h * G:(h + 1) * G], ones[:, 0:1], start=True, stop=True)
            inc(ins)
            wait_step(pe, MIX_A, "TT")
            for h in range(H):
                ins = pe.matmul(bank_c[0:G, h * HD:(h + 1) * HD], TTs[:, h * G:(h + 1) * G],
                                W_fxT[:, h * HD:(h + 1) * HD], start=True, stop=True)
            inc(ins)
            wait_step(pe, MIX_V, "u")
            for c in range(KC):
                ins = pe.transpose(bank_b[:, c * L:(c + 1) * L], u_tok[:, c * P:(c + 1) * P], ident[0:L, 0:L])
            inc(ins)
            wait_step(pe, MIX_V, "uTc")
            for c in range(KC):
                ins = pe.matmul(bank_a[0:L, 0:2 * H], uT[:, c, :], in_wT[:, c, PROJ - 2 * H:PROJ],
                                start=(c == 0), stop=(c == KC - 1))
            inc(ins)
            for k in range(KC):
                for c in range(KC):
                    ins = pe.matmul(bank_b[:, k * L:(k + 1) * L], in_wT[:, c, INNER + k * P:INNER + (k + 1) * P],
                                    uT[:, c, :], start=(c == 0), stop=(c == KC - 1))
            inc(ins)
            for k in range(2):
                for c in range(KC):
                    w0 = 2 * INNER + k * NS
                    ins = pe.matmul(acc[0:NS, k * L:(k + 1) * L], in_wT[:, c, w0:w0 + NS],
                                    uT[:, c, :], start=(c == 0), stop=(c == KC - 1))
            inc(ins)
            for i, (w, name) in enumerate(((more, "rhs0"), (less, "rhs1"))):
                wait_step(pe, MIX_V, name)
                inc(pe.matmul(turned[i][0:L, 0:H * L], w[:, :], seg_rhs[i].rearrange("p a b -> p (a b)"),
                              start=True, stop=True))
            for c in range(KC):
                ins = pe.matmul(bank_c[0:L, :], uT[:, c, :], in_wT[:, c, 0:INNER], start=(c == 0), stop=(c == KC - 1))
            inc(ins)
            wait_step(pe, MIX_V, "Cp")
            for i, at in ((0, 0), (1, 2)):
                ins = pe.matmul(acc[0:L, i * L:(i + 1) * L], xT[0:NS, KC, :], Cpad[:, at:at + L], start=True, stop=True)
            inc(ins)
            for c in range(KC):
                ins = pe.transpose(bank_b[0:L, c * P:(c + 1) * P], xT[:, c, :], ident[:, :])
            inc(ins)
            wait_step(pe, MIX_V, "dt_add")
            for c in range(KC):
                ins = pe.matmul(bank_a[0:L, 0:H], xT[:, c, :], fcD_T[:, c, :], start=(c == 0), stop=(c == KC - 1))
            inc(ins)
            wait_step(pe, MIX_A, "dec1")
            for h in range(2):
                turn(n2, m2, h)
            wait_step(pe, MIX_A, "u_z")
            wait_step(pe, MIX_V, "dsum")
            for h in range(H):
                ins = pe.matmul(bank_c[0:L, h * HD:(h + 1) * HD], dsum[:, h, :], x_tok[:, h * HD:(h + 1) * HD],
                                start=True, stop=True)
            inc(ins)
            wait_step(pe, MIX_V, "ygw")
            for c in range(KC):
                ins = pe.transpose(bank_b[:, c * L:(c + 1) * L], ygw[:, c * P:(c + 1) * P], ident[0:L, 0:L])
            inc(ins)
            wait_step(pe, MIX_V, "ygTc")
            for k in range(KC):
                for c in range(KC):
                    ins = pe.matmul(bank_a[:, k * L:(k + 1) * L], hy_outT[:, c, k * P:(k + 1) * P], ygT[:, c, :],
                                    start=(c == 0), stop=(c == KC - 1))
            inc(ins)
            wait_step(pe, MIX_V, "bd1")
            for k in range(KC):
                ins = pe.matmul(bank_c[:, k * D:(k + 1) * D], bd[:, k, :], out_wT[:, k, :], start=True, stop=True)
            inc(ins)

            def back(r, g=0):
                pe.wait_ge(ot_done, lin(r + 1, RING, g))
                if r >= 1:
                    pe.wait_ge(y_done, lin(r, RING, g))
                for t in range(T4):
                    ins = pe.transpose(bank_a[:, t * D:(t + 1) * D], o_col[:, r % 2, t * P:(t + 1) * P], ident[:, :])
                ins.then_inc(nat_done, 1)

            def last_block(r, n, m, g=0, final=False, start=False):
                for h in range(2):
                    if not final:
                        turn(n + 1, m + 1, h, g)
                    if h == 0 and r >= 2:
                        pe.wait_ge(ot_done, lin(r - 1, RING, g))
                    contract(m, h, True, True, g, m_hi, m_lo, into=(acc, bank_c)[r % 2])
                if not start:
                    back(r - 1, g)

            wait_step(pe, MIX_V, "mlo")
            for r, n, m in LAST_BLOCKS[:RING]:
                last_block(r, n, m, start=(r == 0))
            with rounds(pe, BL // RING - 2) as g:
                for r, n, m in LAST_BLOCKS[RING:2 * RING]:
                    last_block(r, n, m, g)
            for r, n, m in LAST_BLOCKS[BL - RING:]:
                last_block(r, n, m, final=(r == BL - 1))
            back(BL - 1)

        @block.scalar
        def _(act):
            def high(m, h, g=0):
                act.wait_ge(t_done, lin(2 * m + h + 1, 2 * RING, g))
                if m >= 2:
                    act.wait_ge(mm_done, lin(2 * (m - 2) + h + 1, 2 * RING, g))
                act.activation(hi[:, 2 * (m % 2) + h, :], turned[h][:, :], ACT.Copy).then_inc(hi_done, 1)

            def support_high(c, g=0):
                if c.m >= 2:
                    act.wait_ge(mm_done, lin(2 * (c.m - 1), 2 * RING, g))
                act.activation(s_hi[:, c.m % 2, :], supf[:, bass.ds(lin(c.J, RING, g) * CH, CH)], ACT.Copy)\
                    .then_inc(sh_done, 1)

            def row_sums(c, g=0):
                act.wait_ge(a_in[c.n % RING], lin(16 * (c.n // RING + 1), 16, g))
                if c.n >= 1:
                    act.wait_ge(act_sum, lin(c.n, RING, g))
                for t in range(2):
                    ins = act.activation(junk[:, t * CH:(t + 1) * CH], a_ring[:, c.n % RING, t, :], ACT.Copy,
                                         accum_out=part[:, t, bass.ds(lin(c.J, RING, g), 1)])
                ins.then_inc(act_sum, 1)

            def copy_c(use, dst, src):
                act.wait_ge(c_filled, use + 1)
                act.activation(dst, src, ACT.Copy).then_inc(c_copied, 1)

            def norm_root(K):
                wait_step(act, prep_v, "eps", K)
                act.activation(sd[:, :], mv[:, :, 1], ACT.Sqrt).then_inc(prep_a.sem, 1)

            def copy_x(K):
                if K >= 1:
                    wait_step(act, prep_t, "support", K - 1)
                copy_c(c_use(("x", K)), lnxT[:, :], bank_c[:, :])

            def copy_weights(K, i):
                u = PER * (K - FIRST_UNITS) + i
                if 0 <= u and u in unit_block and unit_block[u] == K:
                    k, dst = units[u][2], units[u][3]
                    copy_c(c_use(("w", u)), dst, bank_c[:, :].rearrange("p (t k) -> p t k", t=T4)[:, :, 0:k])

            def save_sums(K):
                act.wait_ge(mm_done, 2 * (first_plan[K][-1].chunks[-1].m + 1))
                act.activation(rows[:, BL - 1 - K, :], acc[:, :], ACT.Copy).then_inc(row_done, 1)

            copy_c(0, gnn_WT[:, :], bank_c[:, 0:P])
            norm_root(0)
            copy_x(0)
            for K, segs in enumerate(first_plan):
                if K + 1 < BL:
                    norm_root(K + 1)
                    if K == 0:
                        copy_x(1)
                for seg in segs:
                    with rounds(act, seg.rounds) as g:
                        for c in seg.chunks:
                            row_sums(c, g)
                            if c.m is None:
                                continue
                            if c.last:
                                wait_step(act, deg_v, "one", K)
                                act.activation(rsq[:, :], rsum[:, :], ACT.Sqrt).then_inc(deg_a.sem, 1)
                                high(c.m, 0, g)
                                wait_step(act, deg_v, "scaled", K)
                                support_high(c, g)
                                high(c.m, 1, g)
                            else:
                                support_high(c, g)
                                high(c.m, 0, g)
                                high(c.m, 1, g)
                            if c.k == 0 and K >= 1:
                                save_sums(K - 1)
                            if c.k == 1 and K < BL - 1:
                                copy_x(K + 1)
                            if c.k in (2, 3):
                                copy_weights(K, c.k - 2)

            def slice_step(k, g=0):
                R2 = RING // 2
                if 0 <= k < TILES:
                    act.wait_ge(xt_done, lin(k + 1, R2, g))
                    if k >= 1:
                        act.wait_ge(lg_done, lin(k, R2, g))
                    act.activation(xnT_hi, bank_a[:, 0:P], ACT.Copy).then_inc(xtc_done, 1)

            def exponentials(k, i, g=0):
                R2 = RING // 2
                q = k - 2
                if 0 <= q < TILES:
                    act.wait_ge(sm_done.sem, lin(sm_done.value("neg", q), 3 * R2, g))
                    if q >= 2:
                        act.wait_ge(sw_done.sem, lin(sw_done.value("weights", q - 2), 2 * R2, g))
                    for h in range(i * H // 2, (i + 1) * H // 2):
                        ins = act.activation(expd[:, q % 2, h * G:(h + 1) * G], logit[:, q % 2, h * G:(h + 1) * G],
                                             ACT.Exp, bias=neg_mx[:, q % 2, h:h + 1], accum_out=den[:, q % 2, h:h + 1])
                    if i:
                        ins.then_inc(exp_done, 1)

            for I, segs in second_plan:
                for seg in segs:
                    with rounds(act, seg.rounds) as g:
                        for c in seg.chunks:
                            support_high(c, g)
                            high(c.m, 0, g)
                            high(c.m, 1, g)
                            if c.m == M0:
                                save_sums(BL - 1)
                            k = sliced(c.m - 1)
                            if k is not None:
                                slice_step(k, g)
                                exponentials(k, 0, g)
                            k = sliced(c.m - 2)
                            if k is not None:
                                exponentials(k, 1, g)
            for k in range(SLICE_ALONE, SLICE_LAST + 1):
                slice_step(k)
                for i in range(2):
                    exponentials(k, i)

            def inc(ins):
                ins.then_inc(MIX_A.sem, 1)

            act.wait_ge(tt_done, TILES)
            inc(act.activation(TTs, bank_b[:, :], ACT.Copy))
            wait_step(act, MIX_V, "snorm")
            inc(act.activation(a_ex, a_cl, ACT.Exp))
            wait_step(act, MIX_V, "dt_abs")
            inc(act.activation(dtc, dtb, ACT.Exp))
            wait_step(act, MIX_V, "dt_one")
            inc(act.activation(dtd, dtm, ACT.Ln))
            for i in range(2):
                wait_step(act, MIX_T, f"seg{i}")
                inc(act.activation(dec_e[i], turned[i][0:L, 0:H * L].rearrange("p (h l) -> p h l", h=H), ACT.Exp))
            wait_step(act, MIX_V, "cb")
            inc(act.activation(cve, cvb, ACT.Exp, scale=-1.0))
            wait_step(act, MIX_T, "z")
            inc(act.activation(z_tok, bank_c[0:L, :], ACT.Copy))
            wait_step(act, MIX_A, "u_z")
            inc(act.activation(z_e, z_tok, ACT.Exp, scale=-1.0))
            for h in range(2):
                high(m2, h)
            wait_step(act, MIX_V, "mean")
            inc(act.activation(ygq[:, :], ygm[:, :], ACT.Sqrt))
            wait_step(act, MIX_T, "M")
            inc(act.activation(m_hi[:, :], bank_c[:, :], ACT.Copy))

            def finish_columns(r, g=0):
                act.wait_ge(mm_done, lin(2 * (m2 + r + 1), 2 * RING, g))
                if r >= 2:
                    act.wait_ge(nat_done, lin(r - 1, RING, g))
                act.activation(o_col[:, r % 2, :], (acc, bank_c)[r % 2][:, :], ACT.Identity, bias=out_bc[:, 0:1])\
                    .then_inc(ot_done, 1)

            def last_block(r, n, m, g=0):
                if r >= 1:
                    high(m, 0, g)
                    high(m, 1, g)
                if r >= 1:
                    finish_columns(r - 1, g)

            for r, n, m in LAST_BLOCKS[:RING]:
                last_block(r, n, m)
            with rounds(act, BL // RING - 1) as g:
                for r, n, m in LAST_BLOCKS[RING:2 * RING]:
                    last_block(r, n, m, g)
            finish_columns(BL - 1)

        @block.vector
        def _(dve):
            def rest(m, h, g=0):
                dve.wait_ge(hi_done, lin(2 * m + h + 1, 2 * RING, g))
                slot = 2 * (m % 2) + h
                dve.tensor_tensor(lo[:, slot, :], turned[h][:, :], hi[:, slot, :], ALU.subtract).then_inc(lo_done, 1)

            def row_sums(c, g=0):
                dve.wait_ge(a_in[c.n % RING], lin(16 * (c.n // RING + 1), 16, g))
                dve.tensor_reduce(part[:, 2:T4, bass.ds(lin(c.J, RING, g), 1)],
                                  a_ring[:, c.n % RING, 2:T4, :], AX.X, ALU.add).then_inc(dve_sum, 1)

            def prepare(K):
                dve.wait_ge(x_landed[K % 2], 16 * (K // 2 + 1))
                for t in range(T4):
                    ins = dve.bn_stats(bn[:, t, :], x_in[:, K % 2, t, :])
                ins.then_inc(prep_v.sem, 1)
                wait_step(dve, prep_v, "stats", K)
                for t in range(T4):
                    ins = dve.bn_aggr(mv[:, t, :], bn[:, t, :])
                ins.then_inc(prep_v.sem, 1)
                wait_step(dve, prep_v, "aggr", K)
                dve.tensor_scalar(mv[:, :, 1], mv[:, :, 1], LN_EPS, None, ALU.add).then_inc(prep_v.sem, 1)
                wait_step(dve, prep_a, "sqrt", K)
                dve.reciprocal(rstd4[:, :], sd[:, :]).then_inc(prep_v.sem, 1)
                wait_step(dve, prep_v, "rstd", K)
                if K >= 1:
                    dve.wait_ge(c_filled, c_use(("x", K - 1)) + 1)
                else:
                    dve.wait_ge(c_filled, 1)
                for t in range(T4):
                    ins = dve.tensor_scalar(lnx[:, t, :], x_in[:, K % 2, t, :], mv[:, t, 0:1], rstd4[:, t:t + 1],
                                            ALU.subtract, ALU.mult)
                ins.then_inc(prep_v.sem, 1)

            def degrees(K):
                dve.wait_ge(act_sum, BL * (K + 1))
                dve.wait_ge(dve_sum, BL * (K + 1))
                dve.tensor_reduce(rsum[:, :], part[:, :, :], AX.X, ALU.add).then_inc(deg_v.sem, 1)
                wait_step(dve, deg_v, "rows", K)
                dve.tensor_scalar(rsum[:, :], rsum[:, :], 1.0, None, ALU.add).then_inc(deg_v.sem, 1)
                wait_step(dve, deg_a, "sqrt", K)
                dve.reciprocal(dcol[:, K * T4:(K + 1) * T4], rsq[:, :]).then_inc(deg_v.sem, 1)
                wait_step(dve, deg_v, "inv", K)
                wait_step(dve, prep_t, "support", K)
                bank = (bank_a, bank_b)[K % 2]
                dve.tensor_tensor(sup[:, K * T4:(K + 1) * T4, :], bank[:, :].rearrange("p (t d) -> p t d", t=T4),
                                  dcol[:, K * T4:(K + 1) * T4].unsqueeze(2).to_broadcast([P, T4, D]),
                                  ALU.mult).then_inc(deg_v.sem, 1)

            def logits_setup():
                dve.wait_ge(logits_in, 16 * TINY_FIRST)
                dve.tensor_scalar(temp[:, :], temp[:, :], 1e-6, None, ALU.max).then_inc(set_v.sem, 1)
                wait_step(dve, set_v, "tmax")
                dve.reciprocal(rtemp[:, :], temp[:, :]).then_inc(set_v.sem, 1)
                dve.tensor_copy(b_x_wide, b_xT[:, :].unsqueeze(2).to_broadcast([HD, H, P])).then_inc(set_v.sem, 1)
                wait_step(dve, set_t, "wslT")
                dve.tensor_copy(w_slT, acc[0:HD, 0:G]).then_inc(set_v.sem, 1)
                rt = rtemp[:, :].unsqueeze(2).to_broadcast([P, H, G])
                wait_step(dve, set_t, "wlog")
                wait_step(dve, set_v, "tinv")
                dve.tensor_tensor(W_logT.rearrange("p (h g) -> p h g", h=H),
                                  turned[0][:, 0:HG].rearrange("p (h g) -> p h g", h=H), rt, ALU.mult).then_inc(set_v.sem, 1)
                wait_step(dve, set_t, "blog")
                bl = b_log[:, :].rearrange("p (h g) -> p h g", h=H)
                dve.tensor_tensor(bl, turned[1][:, 0:HG].rearrange("p (h g) -> p h g", h=H),
                                  bsl[:, :].unsqueeze(1).to_broadcast([P, H, G]), ALU.add).then_inc(set_v.sem, 1)
                wait_step(dve, set_v, "blog_sum")
                dve.tensor_tensor(bl, bl, rt, ALU.mult).then_inc(set_v.sem, 1)
                dve.tensor_copy(W_log_hi[:, :], W_logT).then_inc(set_v.sem, 1)
                wait_step(dve, set_v, "whi")
                dve.tensor_tensor(W_log_lo[:, :], W_logT, W_log_hi[:, :], ALU.subtract).then_inc(set_v.sem, 1)


            prepare(0)
            for K, segs in enumerate(first_plan):
                if K + 1 < BL:
                    prepare(K + 1)
                for seg in segs:
                    with rounds(dve, seg.rounds) as g:
                        for c in seg.chunks:
                            row_sums(c, g)
                            if c.last:
                                degrees(K)
                            if c.m is not None:
                                rest(c.m, 0, g)
                                rest(c.m, 1, g)
                    if K == 0 and seg is segs[0]:
                        logits_setup()

            def finish_sums(f):
                if f == 0:
                    dve.wait_ge(row_done, BL)
                    dve.tensor_copy(row_st[:, :], rows[:, f, :]).then_inc(fin_sums, 1)
                else:
                    dve.wait_ge(mm_done, 2 * fin_m[f])
                    dve.tensor_tensor(row_st[:, :], acc[:, :], rows[:, f, :], ALU.add).then_inc(fin_sums, 1)

            def finish_rows(f):
                I = BL - 1 - f
                wait_step(dve, fin_t, "turned", f)
                dve.tensor_tensor(nat[:, :, :], bank_a[:, :].rearrange("p (t d) -> p t d", t=T4),
                                  sup[:, I * T4:(I + 1) * T4, :], ALU.add).then_inc(fin_v.sem, 1)
                wait_step(dve, fin_v, "add", f)
                dve.scalar_tensor_tensor(out=nat[:, :, :], in0=nat[:, :, :], scalar=0.0,
                                         in1=dcol[:, I * T4:(I + 1) * T4].unsqueeze(2).to_broadcast([P, T4, D]),
                                         op0=ALU.max, op1=ALU.mult).then_inc(fin_v.sem, 1)
                wait_step(dve, fin_v, "relu", f)
                i = BL + f
                dve.wait_ge(x_landed[i % 2], 16 * (i // 2 + 1))
                dve.tensor_tensor(x1[:, f * T4:(f + 1) * T4, :], nat[:, :, :], x_in[:, i % 2], ALU.add)\
                    .then_inc(fin_v.sem, 1)

            def finish_stats(f):
                wait_step(dve, fin_v, "x1", f)
                for t in range(T4):
                    ins = dve.bn_stats(bn[:, t, :], x1[:, f * T4 + t, :])
                ins.then_inc(fin_v.sem, 1)
                wait_step(dve, fin_v, "stats", f)
                for t in range(T4):
                    ins = dve.bn_aggr(mvx[:, f * T4 + t, :], bn[:, t, :])
                ins.then_inc(fin_v.sem, 1)
                wait_step(dve, fin_v, "aggr", f)
                dve.tensor_scalar(mvx[:, f * T4:(f + 1) * T4, 1], mvx[:, f * T4:(f + 1) * T4, 1], LN_EPS, None, ALU.add)\
                    .then_inc(fin_v.sem, 1)

            def slice_logits(k, g=0):
                R2 = RING // 2
                if 0 <= k < TILES:
                    dve.wait_ge(xtc_done, lin(k + 1, R2, g))
                    dve.tensor_tensor(xnT_lo, bank_a[:, 0:P], xnT_hi, ALU.subtract).then_inc(xtl_done, 1)
                q = k - 1
                if 0 <= q < TILES:
                    lt = logit[:, q % 2, :].rearrange("p (h g) -> p h g", h=H)
                    dve.wait_ge(lg_done, lin(q + 1, R2, g))
                    if q >= 2:
                        dve.wait_ge(exp_done, lin(q - 1, R2, g))
                    dve.tensor_tensor(logit[:, q % 2, :], bank_c[:, :], b_log[:, :], ALU.add).then_inc(sm_done.sem, 1)
                    dve.wait_ge(sm_done.sem, lin(sm_done.value("bias", q), 3 * R2, g))
                    if q >= 1:
                        dve.wait_ge(sm_done.sem, lin(sm_done.value("neg", q - 1), 3 * R2, g))
                    dve.tensor_reduce(mx[:, :], lt, AX.X, ALU.max).then_inc(sm_done.sem, 1)
                    dve.wait_ge(sm_done.sem, lin(sm_done.value("max", q), 3 * R2, g))
                    dve.tensor_scalar(neg_mx[:, q % 2, :], mx[:, :], -1.0, None, ALU.mult).then_inc(sm_done.sem, 1)

            def slice_rows(k, g=0, count=1):
                R2 = RING // 2
                q = k + 1
                if 0 <= q < TILES:
                    ti = lin(q, R2, g)
                    dve.wait_ge(rstd_done, (q + R2 * (count - 1)) // T4 + 1)
                    if q >= 2:
                        dve.wait_ge(xt_done, lin(q - 1, R2, g))
                    dve.tensor_scalar(xn_a[:, q % 2, :], x1[:, bass.ds(ti, 1), :].rearrange("p a d -> p (a d)"),
                                      mvx[:, bass.ds(ti, 1), 0], rstd[:, bass.ds(ti, 1)],
                                      ALU.subtract, ALU.mult).then_inc(xa_done, 1)
                q = k - 3
                if 0 <= q < TILES:
                    ti = lin(q, R2, g)
                    dve.wait_ge(exp_done, lin(q + 1, R2, g))
                    if q >= 2:
                        dve.wait_ge(sw_done.sem, lin(sw_done.value("weights", q - 2), 2 * R2, g))
                    dve.reciprocal(rden[:, q % 2, :], den[:, q % 2, :]).then_inc(rd_done, 1)
                    if q >= 2:
                        dve.wait_ge(tt_done, lin(q - 1, R2, g))
                    dve.tensor_scalar(xn_b[:, q % 2, :], x1[:, bass.ds(ti, 1), :].rearrange("p a d -> p (a d)"),
                                      mvx[:, bass.ds(ti, 1), 0], rstd[:, bass.ds(ti, 1)],
                                      ALU.subtract, ALU.mult).then_inc(xb_done, 1)

            for f, (I, segs) in enumerate(second_plan):
                for seg in segs:
                    with rounds(dve, seg.rounds) as g:
                        for c in seg.chunks:
                            rest(c.m, 0, g)
                            if f == 1 and c.k == 0:
                                finish_rows(0)
                            if c.k == 0:
                                finish_sums(f)
                            rest(c.m, 1, g)
                            k = sliced(c.m - 1)
                            if k is not None:
                                slice_logits(k, g)
                            if c.k == 1:
                                finish_rows(f)
                            if f >= 1 and c.k == min(f, 2):
                                finish_stats(f)
                            if f == 1 and c.k == 0:
                                finish_stats(0)
                                slice_rows(-1)
                            k = sliced(c.m - 2)
                            if k is not None:
                                slice_rows(k, g, seg.rounds)
            slice_logits(SLICE_ALONE)
            slice_rows(SLICE_ALONE)
            finish_sums(BL - 1)
            finish_rows(BL - 1)
            finish_stats(BL - 1)
            for k in range(SLICE_ALONE + 1, SLICE_LAST + 1):
                slice_logits(k)
                slice_rows(k)

            def V(name):
                wait_step(dve, MIX_V, name)

            def Aw(name):
                wait_step(dve, MIX_A, name)

            def Tw(name):
                wait_step(dve, MIX_T, name)

            order = iter(MIX_V.names)

            def inc(name, ins):
                assert next(order) == name, name
                ins.then_inc(MIX_V.sem, 1)

            def bc(ap, shape):
                return ap.unsqueeze(2).to_broadcast(shape)

            inc("gpad", dve.memset(cpad, 0.0))
            inc("C0", dve.memset(Cpad, 0.0))
            inc("C1", dve.memset(ygs[:, :], 0.0))
            dve.wait_ge(tiny_in, TINY)
            Tw("snorm")
            dve.tensor_scalar(a_cl, a_lw[:, :], EXP_MAX, None, ALU.min)
            inc("snorm", dve.tensor_copy(snorm, bank_a[0:L, 0:H]))
            V("snorm")
            inc("snorm_e", dve.tensor_scalar(snorm_e, snorm, 1e-5, None, ALU.add))
            V("snorm_e")
            inc("rsnorm", dve.reciprocal(rsnorm, snorm_e))
            inc("st_b", dve.tensor_tensor(st_b, b_fx_w[:, :].rearrange("p (h c) -> p h c", h=H),
                                          bc(snorm, [L, H, HD]), ALU.mult))
            V("st_b")
            Tw("st")
            inc("st_s", dve.tensor_tensor(st_s, bank_c[0:L, :].rearrange("p (h c) -> p h c", h=H), st_b, ALU.add))
            V("st_s")
            inc("u", dve.tensor_tensor(u_tok.rearrange("p (h c) -> p h c", h=H), st_s, bc(rsnorm, [L, H, HD]), ALU.mult))
            Tw("uT")
            inc("uTc", dve.tensor_copy(uT, bank_b[:, 0:KC * L].rearrange("p (k l) -> p k l", k=KC)))
            Tw("dt")
            inc("dt_add", dve.tensor_tensor(dtr, bank_a[0:L, 0:2 * H].rearrange("p (a h) -> p a h", a=2),
                                            dt_bw[:, :].unsqueeze(1).to_broadcast([L, 2, H]), ALU.add))
            V("dt_add")
            inc("dt_neg", dve.tensor_scalar(dta, dtr, -1.0, None, ALU.mult))
            V("dt_neg")
            inc("dt_abs", dve.tensor_tensor(dtb, dtr, dta, ALU.min))
            Aw("dexp")
            inc("dt_one", dve.tensor_scalar(dtm, dtc, 1.0, None, ALU.add))
            inc("dt_max", dve.tensor_scalar(dtr, dtr, 0.0, None, ALU.max))
            Aw("dln")
            V("dt_max")
            inc("dt", dve.tensor_tensor(dt, dtr, dtd, ALU.add))
            V("dt")
            inc("dtm", dve.tensor_tensor(dec, dt, a_ex.unsqueeze(1).to_broadcast([L, 2, H]), ALU.mult))
            V("dtm")
            inc("decm", dve.tensor_scalar(decm, dec, -1.0, DECAY_MIN, ALU.mult, ALU.max))
            V("decm")
            for i, w in enumerate((less, more)):
                inc(f"rhs{i}", dve.tensor_tensor(seg_rhs[i], w[:, :].unsqueeze(1).to_broadcast([L, H, L]),
                                                 bc(decm[:, i, :], [L, H, L]), ALU.mult))
            Tw("xbc")
            inc("xpad", dve.tensor_copy(cpad[:, 0:KC, 2:], bank_b[:, 0:KC * L].rearrange("p (k l) -> p k l", k=KC)))
            Tw("bc")
            inc("bpad", dve.tensor_copy(cpad[0:NS, KC:, 2:], acc[0:NS, 0:2 * L].rearrange("p (k l) -> p k l", k=2)))
            V("bpad")
            inc("c0", dve.tensor_tensor(cva, cpad[:, :, 0:L], bc(conv_ws[:, :, 0], [P, CK, L]), ALU.mult))
            inc("c1", dve.tensor_tensor(cvb, cpad[:, :, 1:L + 1], bc(conv_ws[:, :, 1], [P, CK, L]), ALU.mult))
            inc("c2", dve.tensor_tensor(cvc, cpad[:, :, 2:L + 2], bc(conv_ws[:, :, 2], [P, CK, L]), ALU.mult))
            V("c2")
            inc("c01", dve.tensor_tensor(cva, cva, cvb, ALU.add))
            V("c01")
            inc("c012", dve.tensor_tensor(cva, cva, cvc, ALU.add))
            V("c012")
            inc("cb", dve.tensor_tensor(cvb, cva, bc(conv_bs[:, :], [P, CK, L]), ALU.add))
            Aw("cexp")
            inc("ce1", dve.tensor_scalar(cve, cve, 1.0, None, ALU.add))
            V("ce1")
            inc("cr", dve.reciprocal(cve, cve))
            V("cr")
            inc("xT", dve.tensor_tensor(xT, cvb, cve, ALU.mult))
            V("xT")
            inc("Cp", dve.tensor_copy(Cpad[:, 1:L + 1], xT[0:NS, KC + 1, :]))
            Tw("cb")
            inc("cb0", dve.tensor_tensor(cb[0], acc[0:L, 0:L], less[:, :], ALU.mult))
            inc("cb1", dve.tensor_tensor(cb[1], acc[0:L, L:2 * L], more[:, :], ALU.mult))
            Tw("xtok")
            inc("xtok", dve.tensor_copy(x_tok, bank_b[0:L, :]))
            V("cb1")
            for i in range(2):
                inc(f"cbd{i}", dve.tensor_tensor(cbh[i], cb[i].unsqueeze(1).to_broadcast([L, H, L]),
                                                 bc(dt[:, i, :], [L, H, L]), ALU.mult))
            V("cbd1")
            for i in range(2):
                Aw(f"dec{i}")
                inc(f"mix{i}", dve.tensor_tensor(dmix[i], dec_e[i], cbh[i], ALU.mult))
            V("mix1")
            inc("dsum", dve.tensor_tensor(dsum, dmix[0], dmix[1], ALU.add))
            wait_step(dve, MIX_P, "plus")
            inc("zr", dve.reciprocal(z_1, z_1))
            Tw("fcd")
            inc("fcd", dve.tensor_tensor(fcd, bank_a[0:L, 0:H], Dw[:, :], ALU.add))
            V("fcd")
            inc("xf", dve.tensor_tensor(xf, x_tok.rearrange("p (h c) -> p h c", h=H), bc(fcd, [L, H, HD]), ALU.mult))
            V("xf")
            wait_step(dve, MIX_P, "gate")
            Tw("y")
            inc("y", dve.tensor_tensor(y_s, bank_c[0:L, :], xf.rearrange("p h c -> p (h c)"), ALU.add))
            V("y")
            inc("yg", dve.tensor_tensor(yg, y_s, gate, ALU.mult))
            V("yg")
            inc("ssq", dve.tensor_tensor_reduce(z_e, yg, yg, 1.0, 0.0, ALU.mult, ALU.add, ygs[:, :]))
            V("ssq")
            inc("mean", dve.tensor_scalar(ygm[:, :], ygs[:, :], 1.0 / INNER, 1e-5, ALU.mult, ALU.add))
            Aw("sqrt")
            inc("rms", dve.reciprocal(ygr[:, :], ygq[:, :]))
            V("rms")
            inc("ygn", dve.tensor_scalar(ygn, yg, ygr[:, 0:1], None, ALU.mult))
            V("ygn")
            inc("ygw", dve.tensor_tensor(ygw, ygn, norm_ww[:, :], ALU.mult))
            Tw("ygT")
            inc("ygTc", dve.tensor_copy(ygT, bank_b[:, 0:KC * L].rearrange("p (k l) -> p k l", k=KC)))
            rest(m2, 0)
            rest(m2, 1)
            Tw("ot")
            wait_step(dve, MIX_P, "bdz")
            src = bank_a[:, 0:KC * L].rearrange("p (k l) -> p k l", k=KC)
            inc("bd0", dve.tensor_copy(bd[0:HD, :, 0:G], src[0:HD]))
            inc("bd1", dve.tensor_copy(bd[HD:P, :, G:2 * G], src[HD:P]))
            Aw("mhi")
            inc("mlo", dve.tensor_tensor(m_lo[:, :], bank_c[:, :], m_hi[:, :], ALU.subtract))

            def rows_out(r, g=0):
                dve.wait_ge(nat_done, lin(r + 1, RING, g))
                if r >= 2:
                    dve.wait_ge(y_out[r % 2], lin(16 * (r // 2), 16 * RING // 2, g))
                dve.tensor_tensor(y_row[:, r % 2, :].rearrange("p (t d) -> p t d", t=T4),
                                  bank_a[:, :].rearrange("p (t d) -> p t d", t=T4),
                                  x1[:, bass.ds(lin(r * T4, RING * T4, g), T4), :], ALU.add).then_inc(y_done, 1)

            for r, n, m in LAST_BLOCKS[:RING]:
                if r >= 1:
                    rest(m, 0)
                    rest(m, 1)
                if r >= 2:
                    rows_out(r - 2)
            with rounds(dve, BL // RING - 1) as g:
                for r, n, m in LAST_BLOCKS[RING:2 * RING]:
                    rest(m, 0, g)
                    rest(m, 1, g)
                    rows_out(r - 2, g)
            rows_out(BL - 2)
            rows_out(BL - 1)

        @block.gpsimd
        def _(pool):
            pool.memset(ident[:, :], 0.0).then_inc(ident_ok, 1)
            pool.memset(ones[:, :], 1.0)
            pool.memset(half[:, :], -0.5).then_inc(ident_ok, 1)
            pool.memset(sw_sum[:, :], 0.0)
            pool.memset(less[:, :], 1.0)
            pool.memset(more[:, :], 1.0)
            pool.memset(conv_ws[:, :, :], 0.0)
            pool.memset(conv_bs[:, :], 0.0).then_inc(ident_ok, 1)
            pool.wait_ge(ident_ok, 3)
            pool.affine_select(out=less[:, :], in_=less[:, :], compare_op=ALU.is_gt, fill=0.0, base=0,
                               pattern=[[1, L]], channel_multiplier=-1)
            pool.affine_select(out=more[:, :], in_=more[:, :], compare_op=ALU.is_gt, fill=0.0, base=0,
                               pattern=[[-1, L]], channel_multiplier=1)
            pool.affine_select(out=ident[:, :], in_=ident[:, :], compare_op=ALU.not_equal, fill=1.0, base=0,
                               pattern=[[-1, P]], channel_multiplier=1).then_inc(ident_ok, 1)
            with nc.allow_non_contiguous_dma(reason="a few hundred parameters"):
                for dst, src in tiny[TINY_FIRST:]:
                    pool.dma_start(dst, src).then_inc(tiny_in, 16)

            def support_rest(c, g=0):
                pool.wait_ge(sh_done, lin(c.m + 1, RING, g))
                pool.tensor_tensor(s_lo[:, c.m % 2, :], supf[:, bass.ds(lin(c.J, RING, g) * CH, CH)],
                                   s_hi[:, c.m % 2, :], ALU.subtract).then_inc(sl_done, 1)

            def slice_step(k, g=0):
                R2 = RING // 2
                q = k - 3
                if 0 <= q < TILES:
                    s3 = sw[:, q % 2, :].rearrange("p (h g) -> p h g", h=H)
                    pool.wait_ge(rd_done, lin(q + 1, R2, g))
                    if q >= 2:
                        pool.wait_ge(tt_done, lin(q - 1, R2, g))
                        if q - 2 < LATE:
                            pool.wait_ge(sw_out[q % 2], lin(16 * (q // 2), 16, g))
                        else:
                            pool.wait_ge(sw_late[q % 2], 16 * len(range(q - 2, LATE - 1, -2)))
                    pool.tensor_tensor(s3, expd[:, q % 2, :].rearrange("p (h g) -> p h g", h=H),
                                       rden[:, q % 2, :].unsqueeze(2).to_broadcast([P, H, G]), ALU.mult)\
                        .then_inc(sw_done.sem, 1)
                    if k < SLICE_ALONE:
                        pool.wait_ge(sw_done.sem, lin(sw_done.value("weights", q), 2 * R2, g))
                        pool.dma_start(sw_dram[bass.ds(lin(q * P, R2 * P, g), P), :], sw[:, q % 2, :])\
                            .then_inc(sw_out[q % 2], 16)
                    else:
                        wait_step(pool, sw_done, "weights", q)
                    pool.tensor_tensor(sw_sum[:, :], sw_sum[:, :], sw[:, q % 2, :], ALU.add).then_inc(sw_done.sem, 1)

            def roots(f):
                wait_step(pool, fin_v, "eps", f)
                pool.tensor_tensor(rstd[:, f * T4:(f + 1) * T4], mvx[:, f * T4:(f + 1) * T4, 1],
                                   half[:, :].to_broadcast([P, T4]), ALU.pow).then_inc(rstd_done, 1)

            for segs in first_plan:
                for seg in segs:
                    if any(c.m is not None for c in seg.chunks):
                        with rounds(pool, seg.rounds) as g:
                            for c in seg.chunks:
                                if c.m is not None:
                                    support_rest(c, g)
            for f, (I, segs) in enumerate(second_plan):
                for seg in segs:
                    with rounds(pool, seg.rounds) as g:
                        for c in seg.chunks:
                            support_rest(c, g)
                            k = sliced(c.m - 3)
                            if k is not None:
                                slice_step(k, g)
                            if f == 1 and c.k == 0:
                                roots(0)
                            if f >= 1 and c.k == min(f, 2):
                                roots(f)
            slice_step(SLICE_ALONE)
            roots(BL - 1)
            for k in range(SLICE_ALONE + 1, SLICE_LAST + 1):
                slice_step(k)
            pool.memset(bd, 0.0).then_inc(MIX_P.sem, 1)
            wait_step(pool, MIX_A, "zexp")
            pool.tensor_tensor(z_1, z_e, ones[0:L, :].to_broadcast([L, INNER]), ALU.add).then_inc(MIX_P.sem, 1)
            wait_step(pool, MIX_V, "zr")
            pool.tensor_tensor(gate, z_tok, z_1, ALU.mult).then_inc(MIX_P.sem, 1)

            def store_y(r, g=0):
                pool.wait_ge(y_done, lin(r + 1, RING, g))
                pool.dma_start(out_rows[g * -RING + (BL - 1 - r)], y_row[:, r % 2, :].rearrange("p (t d) -> p t d", t=T4))\
                    .then_inc(y_out[r % 2], 16)

            with rounds(pool, BL // RING) as g:
                for r in range(RING):
                    store_y(r, g)
            for i in range(2):
                pool.wait_ge(y_out[i], 16 * (BL // 2))


INPUTS = ["x", "adj", "L0_gnn_W", "L0_ffn_W_fx", "L0_ffn_b_fx", "L0_ffn_W_x", "L0_ffn_b_x", "L0_ffn_W_slice",
          "L0_ffn_b_slice", "L0_ffn_temperature", "L0_ffn_hy_in_w", "L0_ffn_hy_conv_w", "L0_ffn_hy_conv_b",
          "L0_ffn_hy_dt_bias", "L0_ffn_hy_A_log", "L0_ffn_hy_D", "L0_ffn_hy_fcD_w", "L0_ffn_hy_norm_w",
          "L0_ffn_hy_out_w", "L0_ffn_out_w", "L0_ffn_out_b"]


def kernel(**inputs):
    import numpy as np
    import concourse.bacc as bacc
    from concourse.bass_utils import run_bass_kernel_spmd

    nc = bacc.Bacc("TRN2", target_bir_lowering=False, num_devices=1)
    arrays, args = {}, []
    for name in INPUTS:
        a = np.ascontiguousarray(inputs[name])
        arrays[f"in_{name}"] = a
        args.append(nc.dram_tensor(f"in_{name}", a.shape, mybir.dt.from_np(a.dtype), kind="ExternalInput").ap())
    shape = tuple(inputs["x"].shape)
    out = nc.dram_tensor("out_x", shape, F32, kind="ExternalOutput").ap()
    gnn_slice_ffn(nc, *args, out)
    result = run_bass_kernel_spmd(nc, [arrays], core_ids=[0])
    return result.results[0]["out_x"]
```
